# Optimizing a Trainium2 kernel written in Bass

```python
import numpy as np
import jax
import jax.numpy as jnp

def _softmax(x, axis=-1):
    return jax.nn.softmax(x, axis=axis)

def _gelu(x):
    return jax.nn.gelu(x, approximate=True)

def _silu(x):
    return jax.nn.silu(x)

def _sigmoid(x):
    return jax.nn.sigmoid(x)

def _layernorm(x, axis=-1, eps=1e-05):
    m = jnp.mean(x, axis=axis, keepdims=True)
    v = jnp.var(x, axis=axis, keepdims=True)
    return (x - m) / jnp.sqrt(v + eps)

def _scatter_add(tgt, idx, src, axis=0):
    return tgt.at[idx].add(src)

def _segment_sum(src, seg, n):
    return jax.ops.segment_sum(src, seg, n)
kernel_name = 'mk_xattn_ffn_d1_seqx_r4_c32697'

def setup_inputs(seed: int=0):
    np.random.seed(seed)
    _w = jnp.asarray

    def _rec_inputs():
        import jax
        import jax.numpy as jnp
        _rk = jax.random.key(seed)
        x = 7.22e-05 + 1 * jax.random.normal(jax.random.fold_in(_rk, 1), (8, 256, 256), jnp.float32)
        _lenS = 256 - jax.random.randint(jax.random.fold_in(_rk, 7), (8,), 0, max(1, 256 // 4) + 1, jnp.int32)
        _lenS2 = 77 - jax.random.randint(jax.random.fold_in(_rk, 8), (8,), 0, max(1, 77 // 4) + 1, jnp.int32)
        _ctx_1024P = jax.random.normal(jax.random.fold_in(_rk, 11), (8, 16, 256), jnp.float32)
        _ctx_1024c = jax.random.dirichlet(jax.random.fold_in(_rk, 511), 0.3 * jnp.ones((16,), jnp.float32), (8, 77))
        _ctx_1024t = jnp.einsum('bsk,bkd->bsd', _ctx_1024c, _ctx_1024P)
        _ctx_1024t = _ctx_1024t * jax.lax.rsqrt(jnp.mean(jnp.square(_ctx_1024t)) + 1e-12) * 0.953939
        ctx_1024 = 0.00171412 + 0.999381 * (_ctx_1024t + 0.3 * jax.random.normal(jax.random.fold_in(_rk, 611), (8, 77, 256), jnp.float32))
        return (x, ctx_1024)
    x, ctx_1024 = _rec_inputs()

    def _L0_xattn_setup():
        import jax, jax.numpy as jnp
        import numpy as np
        B, N, P, DIM, H = (8, 256, 77, 256, 16)
        HD = DIM // H
        LN_EPS = 1e-05
        key = jax.random.key(seed)
        ks = jax.random.split(key, 8)
        s = 0.02
        return {'x': jax.random.normal(ks[0], (B, N, DIM), jnp.float32), 'x_text': jax.random.normal(ks[1], (B, P, DIM), jnp.float32), 'Wq': jax.random.normal(ks[2], (DIM, DIM), jnp.float32) * s, 'Wk': jax.random.normal(ks[3], (DIM, DIM), jnp.float32) * s, 'Wv': jax.random.normal(ks[4], (DIM, DIM), jnp.float32) * s, 'gate': jax.random.normal(ks[5], (1, H, 1, 1), jnp.float32) * 0.5, 'ln_g': jnp.ones((DIM,), jnp.float32), 'ln_b': jnp.zeros((DIM,), jnp.float32), 'Wp': jax.random.normal(ks[6], (DIM, DIM), jnp.float32) * s, 'bp': jnp.zeros((DIM,), jnp.float32)}
    _L0_xattn_all = _L0_xattn_setup()
    _L0_xattn_in = {k: v for k, v in _L0_xattn_all.items() if k in ('Wq', 'Wk', 'Wv', 'gate', 'ln_g', 'ln_b', 'Wp', 'bp')}
    del _L0_xattn_all

    def _L0_ffn_setup():
        import jax, jax.numpy as jnp
        import numpy as np
        S, B, H = (512, 2, 256)
        NUM_HEADS, NUM_KV_HEADS = (16, 4)
        HEAD_DIM = H // NUM_HEADS
        E, TOP_K, FFN = (16, 2, 512)
        CAP_FACTOR = 1.25
        EPS = 1e-05

        def _layernorm(x, w, b):
            mu = jnp.mean(x, axis=-1, keepdims=True)
            var = jnp.mean((x - mu) ** 2, axis=-1, keepdims=True)
            return (x - mu) * jax.lax.rsqrt(var + EPS) * w + b
        key = jax.random.key(seed)
        ks = jax.random.split(key, 6)
        qkv_out = (NUM_HEADS + 2 * NUM_KV_HEADS) * HEAD_DIM
        sdH = 1.0 / np.sqrt(H)
        sdF = 1.0 / np.sqrt(FFN)
        return {'hidden_states': jax.random.normal(ks[0], (S, B, H), jnp.float32), 'ln1_weight': jnp.ones((H,), jnp.float32), 'ln1_bias': jnp.zeros((H,), jnp.float32), 'ln2_weight': jnp.ones((H,), jnp.float32), 'ln2_bias': jnp.zeros((H,), jnp.float32), 'qkv_weight': jax.random.normal(ks[1], (qkv_out, H), jnp.float32) * sdH, 'proj_weight': jax.random.normal(ks[2], (H, H), jnp.float32) * sdH, 'router_weight': jax.random.normal(ks[3], (E, H), jnp.float32) * sdH, 'moe_w1': jax.random.normal(ks[4], (E, FFN, H), jnp.float32) * sdH, 'moe_w2': jax.random.normal(ks[5], (E, H, FFN), jnp.float32) * sdF}
    _L0_ffn_all = _L0_ffn_setup()
    _L0_ffn_in = {k: v for k, v in _L0_ffn_all.items() if k in ('ln1_weight', 'ln1_bias', 'ln2_weight', 'ln2_bias', 'qkv_weight', 'proj_weight', 'router_weight', 'moe_w1', 'moe_w2')}
    del _L0_ffn_all
    return {'x': x, 'ctx_1024': ctx_1024, 'L0_xattn_Wq': _L0_xattn_in['Wq'], 'L0_xattn_Wk': _L0_xattn_in['Wk'], 'L0_xattn_Wv': _L0_xattn_in['Wv'], 'L0_xattn_gate': _L0_xattn_in['gate'], 'L0_xattn_ln_g': _L0_xattn_in['ln_g'], 'L0_xattn_ln_b': _L0_xattn_in['ln_b'], 'L0_xattn_Wp': _L0_xattn_in['Wp'], 'L0_xattn_bp': _L0_xattn_in['bp'], 'L0_ffn_ln1_weight': _L0_ffn_in['ln1_weight'], 'L0_ffn_ln1_bias': _L0_ffn_in['ln1_bias'], 'L0_ffn_ln2_weight': _L0_ffn_in['ln2_weight'], 'L0_ffn_ln2_bias': _L0_ffn_in['ln2_bias'], 'L0_ffn_qkv_weight': _L0_ffn_in['qkv_weight'], 'L0_ffn_proj_weight': _L0_ffn_in['proj_weight'], 'L0_ffn_router_weight': _L0_ffn_in['router_weight'], 'L0_ffn_moe_w1': _L0_ffn_in['moe_w1'], 'L0_ffn_moe_w2': _L0_ffn_in['moe_w2']}

def reference(x, ctx_1024, L0_xattn_Wq, L0_xattn_Wk, L0_xattn_Wv, L0_xattn_gate, L0_xattn_ln_g, L0_xattn_ln_b, L0_xattn_Wp, L0_xattn_bp, L0_ffn_ln1_weight, L0_ffn_ln1_bias, L0_ffn_ln2_weight, L0_ffn_ln2_bias, L0_ffn_qkv_weight, L0_ffn_proj_weight, L0_ffn_router_weight, L0_ffn_moe_w1, L0_ffn_moe_w2):
    import jax
    import jax.numpy as jnp

    def _L0_xattn_ref(x, x_text, Wq, Wk, Wv, gate, ln_g, ln_b, Wp, bp):
        import jax, jax.numpy as jnp
        import numpy as np
        B, N, P, DIM, H = (8, 256, 77, 256, 16)
        HD = DIM // H
        LN_EPS = 1e-05
        b, n, c = x.shape
        h = gate.shape[1]
        q = x @ Wq.T
        k = jnp.concatenate([x_text @ Wk.T, x @ Wk.T], axis=1)
        v = jnp.concatenate([x_text @ Wv.T, x @ Wv.T], axis=1)
        kv = k.shape[1]
        q = q.reshape(b, n, h, -1).transpose(0, 2, 1, 3)
        k = k.reshape(b, kv, h, -1).transpose(0, 2, 1, 3)
        v = v.reshape(b, kv, h, -1).transpose(0, 2, 1, 3)
        d = q.shape[-1]
        scores = jnp.einsum('bhnd,bhkd->bhnk', q, k) / jnp.sqrt(jnp.float32(d))
        first = jnp.tanh(gate) * jnp.ones_like(scores[..., :1])
        rest = jax.nn.softmax(scores[..., 1:], axis=-1)
        attn = jnp.concatenate([first, rest], axis=-1)
        out = jnp.einsum('bhnk,bhkd->bhnd', attn, v)
        out = out.transpose(0, 2, 1, 3).reshape(b, n, -1)
        out = out.astype(jnp.bfloat16).astype(jnp.float32)
        mu = jnp.mean(out, axis=-1, keepdims=True)
        var = jnp.var(out, axis=-1, keepdims=True)
        out = (out - mu) / jnp.sqrt(var + LN_EPS) * ln_g + ln_b
        return out @ Wp.T + bp

    def _L0_ffn_ref(hidden_states, ln1_weight, ln1_bias, ln2_weight, ln2_bias, qkv_weight, proj_weight, router_weight, moe_w1, moe_w2):
        import jax, jax.numpy as jnp
        import numpy as np
        S, B, H = (512, 2, 256)
        NUM_HEADS, NUM_KV_HEADS = (16, 4)
        HEAD_DIM = H // NUM_HEADS
        E, TOP_K, FFN = (16, 2, 512)
        CAP_FACTOR = 1.25
        EPS = 1e-05

        def _layernorm(x, w, b):
            mu = jnp.mean(x, axis=-1, keepdims=True)
            var = jnp.mean((x - mu) ** 2, axis=-1, keepdims=True)
            return (x - mu) * jax.lax.rsqrt(var + EPS) * w + b
        S_, B_, H_ = hidden_states.shape
        dtype = hidden_states.dtype
        ln1 = _layernorm(hidden_states, ln1_weight, ln1_bias)
        qkv = jnp.einsum('sbh,oh->sbo', ln1, qkv_weight)
        q_sz = NUM_HEADS * HEAD_DIM
        kv_sz = NUM_KV_HEADS * HEAD_DIM
        q = qkv[..., :q_sz].reshape(S_, B_, NUM_HEADS, HEAD_DIM)
        k = qkv[..., q_sz:q_sz + kv_sz].reshape(S_, B_, NUM_KV_HEADS, HEAD_DIM)
        v = qkv[..., q_sz + kv_sz:].reshape(S_, B_, NUM_KV_HEADS, HEAD_DIM)
        rep = NUM_HEADS // NUM_KV_HEADS
        k = jnp.repeat(k, rep, axis=2)
        v = jnp.repeat(v, rep, axis=2)
        scale = 1.0 / np.sqrt(HEAD_DIM)
        scores = jnp.einsum('qbhd,kbhd->bhqk', q, k) * scale
        causal = jnp.tril(jnp.ones((S_, S_), bool))
        scores = jnp.where(causal, scores, jnp.asarray(-1e+30, dtype))
        attn = jax.nn.softmax(scores, axis=-1)
        attn_out = jnp.einsum('bhqk,kbhd->qbhd', attn, v).reshape(S_, B_, H_)
        proj_out = jnp.einsum('sbh,oh->sbo', attn_out, proj_weight)
        hidden_after_attn = hidden_states + proj_out
        ln2 = _layernorm(hidden_after_attn, ln2_weight, ln2_bias).reshape(-1, H_)
        T = ln2.shape[0]
        logits = ln2 @ router_weight.T
        probs = jax.nn.softmax(logits, axis=-1)
        top_p, top_i = jax.lax.top_k(probs, TOP_K)
        cap = int(np.ceil(T * TOP_K / E * CAP_FACTOR))
        exp_idx = top_i.reshape(-1)
        gate = top_p.reshape(-1).astype(dtype)
        tok = jnp.repeat(jnp.arange(T), TOP_K)
        onehot = jax.nn.one_hot(exp_idx, E, dtype=jnp.int32)
        pos = (jnp.cumsum(onehot, axis=0) * onehot).sum(-1) - 1
        keep = pos < cap
        pos_c = jnp.where(keep, pos, cap)
        buf = jnp.zeros((E, cap + 1, H_), dtype)
        buf = buf.at[exp_idx, pos_c].add(ln2[tok] * keep[:, None].astype(dtype))
        h1 = jax.nn.gelu(jnp.einsum('ech,efh->ecf', buf, moe_w1))
        h2 = jnp.einsum('ecf,ehf->ech', h1, moe_w2)
        out_ent = h2[exp_idx, pos_c] * (gate * keep.astype(dtype))[:, None]
        moe_out = jnp.zeros((T, H_), dtype).at[tok].add(out_ent)
        return hidden_after_attn + moe_out.reshape(S_, B_, H_)
    x = x + _L0_xattn_ref(_layernorm(x, axis=-1), ctx_1024, L0_xattn_Wq, L0_xattn_Wk, L0_xattn_Wv, L0_xattn_gate, L0_xattn_ln_g, L0_xattn_ln_b, L0_xattn_Wp, L0_xattn_bp)
    x = x + _L0_ffn_ref(_layernorm(x, axis=-1), L0_ffn_ln1_weight, L0_ffn_ln1_bias, L0_ffn_ln2_weight, L0_ffn_ln2_bias, L0_ffn_qkv_weight, L0_ffn_proj_weight, L0_ffn_router_weight, L0_ffn_moe_w1, L0_ffn_moe_w2)
    return x

_drawn_inputs = setup_inputs


def setup_inputs(seed=0):
    import zlib

    import numpy as np

    out = dict(_drawn_inputs(seed))
    spreads = {'L0_xattn_ln_g': (1.0, 0.2),
     'L0_xattn_ln_b': (0.0, 0.1),
     'L0_xattn_bp': (0.0, 0.1),
     'L0_ffn_ln1_weight': (1.0, 0.2),
     'L0_ffn_ln1_bias': (0.0, 0.1),
     'L0_ffn_ln2_weight': (1.0, 0.2),
     'L0_ffn_ln2_bias': (0.0, 0.362)}
    factors = {'L0_xattn_Wq': 6.349, 'L0_xattn_Wk': 6.234}
    for name, (base, spread) in spreads.items():
        noise = np.random.default_rng([zlib.crc32(name.encode()), seed]).standard_normal(out[name].shape)
        drawn = base * np.exp(spread * noise) if base else spread * noise
        out[name] = jnp.asarray(drawn.astype(out[name].dtype))
    for name, factor in factors.items():
        out[name] = (out[name] * factor).astype(out[name].dtype)
    return out
```

```python
from contextlib import ExitStack

import numpy as np

import concourse.bass as bass
import concourse.mybir as mybir

F32 = mybir.dt.float32
F16 = mybir.dt.float16
BF16 = mybir.dt.bfloat16
U32 = mybir.dt.uint32
ALU = mybir.AluOpType
ACT = mybir.ActivationFunctionType
AX = mybir.AxisListType

P = 128
B, N, DIM = 8, 256, 256
HALVES = N // P
CTX = 77
H, HD = 16, 16
KV_H = 4
REP = H // KV_H
SOFT = N + CTX - 1
CTX_SOFT = CTX - 1
KEYS = N + CTX
NT = B * N // P
E, TOP, FFN = 16, 2, 512
CAP = -(-B * N * TOP * 5 // (E * 4))
TRASH = E * CAP
EPS = 1e-5
SCALE = HD ** -0.5
QKV = (H + 2 * KV_H) * HD
PAIRS = H // 2
GROUP = 8
PARTS = 4
STACK = PARTS * HD
ROWS = STACK + 2
VW = HD + 1
UNITS = PAIRS * HALVES
MASKED = -1e30
EXPERT_TILES = [(s, min(P, CAP - s)) for s in range(0, CAP, P)]


class Shared:
    pass


def wait(eng, semaphore, value):
    if not isinstance(value, int) or value > 0:
        eng.wait_ge(semaphore, value)


def hold(eng, held, semaphore, value):
    eng.wait_ge(semaphore, value)
    eng.sem_inc(held, 1)


class Own:

    def __init__(self, eng, semaphore, base):
        self.eng, self.semaphore, self.base, self.n = eng, semaphore, base, 0

    def step(self, instruction):
        instruction.then_inc(self.semaphore, 1)
        self.n += 1

    def settle(self):
        self.eng.wait_ge(self.semaphore, self.base + self.n)


def heads(ap):
    return ap.rearrange("p (h d) -> p h d", d=HD)


def cross_attention(nc, sb, sem, s):
    ps = s.ps
    xn = sb("xn", [P, HALVES, DIM])
    xct = sb("xct", [P, 2, KEYS])
    qh, ql = (sb(n, [P, 2, N], F16) for n in ("qh", "ql"))
    kh, kl = (sb(n, [P, 2, KEYS], F16) for n in ("kh", "kl"))
    qs = [sb(f"qs{i}", [ROWS, H, N], F16) for i in range(2)]
    ks = [sb(f"ks{i}", [ROWS, H, KEYS], F16) for i in range(2)]
    vh = [sb(f"vh{i}", [P, 3, H, VW], F16) for i in range(2)]
    vl = [sb(f"vl{i}", [P, 3, H, VW], F16) for i in range(2)]
    v0f = sb("v0f", [CTX, DIM])
    tv0 = [sb(f"tv0{i}", [P, DIM]) for i in range(2)]
    nmx = sb("nmx", [P, HALVES, H], F16)
    mrow = [sb(f"mrow{i}", [GROUP, N], F16) for i in range(2)]
    pf = [sb(f"pf{i}", [P, 3, 512]) for i in range(2)]
    ph = [sb(f"ph{i}", [P, 3, 512], F16) for i in range(2)]
    pl = [sb(f"pl{i}", [P, 3, 512], F16) for i in range(2)]
    rs = sb("rs", [P, HALVES, H])
    o32 = sb("o32", [P, HALVES, DIM])
    ob = sb("ob", [P, HALVES, DIM], BF16)
    z = sb("z", [P, HALVES, DIM])
    zt = sb("zt", [P, 2, N])
    bn_a, bn_c = (sb(n, [P, HALVES, 6]) for n in ("bn_a", "bn_c"))
    mv_a, mv_c = (sb(n, [P, HALVES, 2]) for n in ("mv_a", "mv_c"))
    ve_a, ve_c = (sb(n, [P, HALVES]) for n in ("ve_a", "ve_c"))
    rstd_a, rstd_c = (sb(n, [P, HALVES]) for n in ("rstd_a", "rstd_c"))

    init_done = sem("init_done")
    var_a, rstd_a_done, xn_done, bias_added = sem("var_a"), sem("rstd_a_done"), sem("xn_done"), sem("bias_added")
    xt_ps, xct_done = sem("xt_ps"), sem("xct_done")
    q_ps, k_ps, v_ps, v0_ps = sem("q_ps"), sem("k_ps"), sem("v_ps"), sem("v0_ps")
    q_hi, k_hi, v_hi, v0_done = sem("q_hi"), sem("k_hi"), sem("v_hi"), sem("v0_done")
    q_lo, k_lo, v_lo, tv0_done = sem("q_lo"), sem("k_lo"), sem("v_lo"), sem("tv0_done")
    stacked = sem("stacked")
    max_ps, max_done = sem("max_ps"), sem("max_done")
    mrow_ps, mrow_done = sem("mrow_ps"), sem("mrow_done")
    mrow_in = [sem("mrow_in0"), sem("mrow_in1")]
    scores, exped, p_hi, p_lo, pv = sem("scores"), sem("exped"), sem("p_hi"), sem("p_lo"), sem("pv")
    pv_read, var_c, rstd_c_done = sem("pv_read"), sem("var_c"), sem("rstd_c_done")
    z_done, zt_ps, zt_done = sem("z_done"), sem("zt_ps"), sem("zt_done")
    wp_ps, wp_read, y_done, yt_ps, yt_done = sem("wp_ps"), sem("wp_read"), sem("y_done"), sem("yt_ps"), sem("yt_done")
    qkv_ps, qkv_done = sem("qkv_ps"), sem("qkv_done")
    own_a, own_c, held_dve, held_pool = sem("own_a"), sem("own_c"), sem("held_dve"), sem("held_pool")
    STACK_DMAS = 2 * PARTS * 2

    with nc.Block() as block:

        @block.sync
        def _(sp):
            s.load_constants(sp)

            def stack_parts(b, par):
                def put(dst, src, rows):
                    for g in range(2):
                        for r in rows:
                            sp.dma_start(dst[r * HD:(r + 1) * HD, g * GROUP:(g + 1) * GROUP, :],
                                         src[:, g, :]).then_inc(stacked, 16)
                sp.wait_ge(q_hi, b + 1)
                put(qs[par], qh, (0, 1))
                sp.wait_ge(q_lo, b + 1)
                put(qs[par], ql, (2, 3))
                sp.wait_ge(k_hi, 2 * b + 2)
                put(ks[par], kh, (0, 2))
                sp.wait_ge(k_lo, 2 * b + 2)
                put(ks[par], kl, (1, 3))

            def put_maxima(b, par, g):
                sp.wait_ge(mrow_done, 2 * b + g + 1)
                sp.dma_start(qs[par][STACK + 1:STACK + 2, g * GROUP:(g + 1) * GROUP, :],
                             mrow[g][:, :]).then_inc(mrow_in[g], 16)

            def stage_a(b, par):
                stack_parts(b, par)
                put_maxima(b, par, 0)
                put_maxima(b, par, 1)

            sp.wait_ge(init_done, 2)
            stage_a(0, 0)
            stage_a(1, 1)
            with sp.Fori(0, (B - 2) // 2) as i:
                stage_a(2 * i + 2, 0)
                stage_a(2 * i + 3, 1)
            s.clear_slots(sp)

        @block.gpsimd
        def _(pool):
            def init():
                for t in (0, 1):
                    pool.memset(vh[t][:], 1.0)
                    pool.memset(vl[t][:], 0.0)
                pool.memset(s.zeros[:], 0.0)
                pool.memset(s.minus_half[:], -0.5).then_inc(init_done, 1)
                pool.wait_ge(init_done, 2)

            def power(b, per, k, ready, ve, rstd, done):
                pool.wait_ge(ready, b * per + k + 1)
                pool.tensor_tensor(rstd[:], ve[:], s.minus_half[:, 0:HALVES], ALU.pow).then_inc(done, 1)

            def add_bias(b):
                pool.wait_ge(xn_done, b + 1)
                for t in range(HALVES):
                    i = pool.tensor_tensor(s.x1[:, HALVES * b + t, :], s.x1[:, HALVES * b + t, :],
                                           s.bp_sb[:], ALU.add)
                i.then_inc(bias_added, 1)

            def hi(b, p):
                t = PAIRS * b + p
                if not (isinstance(b, int) and t < 2):
                    pool.wait_ge(pv, t - 1)
                hold(pool, held_pool, exped, 3 * t + 2)
                pool.tensor_scalar(ph[p % 2][:, 0:2, :], pf[p % 2][:, 0:2, :], 1.0, 0.0, ALU.mult,
                                   ALU.add).then_inc(p_hi, 1)
                hold(pool, held_pool, exped, 3 * t + 3)
                pool.tensor_scalar(ph[p % 2][0:CTX_SOFT, 2, :], pf[p % 2][0:CTX_SOFT, 2, :], 1.0, 0.0,
                                   ALU.mult, ALU.add).then_inc(p_hi, 1)

            def iteration(b, a, c):
                for p in range(PAIRS):
                    if b is not None:
                        hi(b, p)
                    if p == 0 and a is not None:
                        power(a, 1, 0, var_a, ve_a, rstd_a, rstd_a_done)
                    if c is not None and p in (0, 2, 3):
                        power(c, 3, {0: 0, 2: 1, 3: 2}[p], var_c, ve_c, rstd_c, rstd_c_done)
                    if p == 1 and a is not None:
                        add_bias(a)

            init()
            pool.wait_ge(s.const_in, s.N_CONST)
            iteration(None, 0, None)
            iteration(0, 1, None)
            with pool.Fori(0, (B - 2) // 2) as i:
                for odd in (0, 1):
                    n = 2 * i + 1 + odd
                    iteration(n, n + 1, n - 1)
            iteration(B - 1, None, B - 2)
            iteration(None, None, B - 1)

        @block.tensor
        def _(pe):
            def transposes(src, bank):
                for f in range(2):
                    for t in range(HALVES):
                        i = pe.transpose(ps[:, bank, f * N + t * P:f * N + (t + 1) * P],
                                         src[:, t, f * P:(f + 1) * P], s.id32[:])
                return i

            def x_t(a):
                pe.wait_ge(xn_done, a + 1)
                wait(pe, mrow_done, 2 * a)
                transposes(xn, 3).then_inc(xt_ps, 1)

            def project_q(a):
                pe.wait_ge(xct_done, 2 * a + 2)
                wait(pe, max_done, UNITS * a)
                for g in range(2):
                    for f in range(2):
                        i = pe.matmul(ps[:, 4, g * N:(g + 1) * N], s.wq_sb[:, f, g * P:(g + 1) * P],
                                      xct[:, f, 0:N], start=f == 0, stop=f == 1)
                i.then_inc(q_ps, 1)

            def project_k(a, g):
                if g == 1:
                    pe.wait_ge(q_lo, a + 1)
                for f in range(2):
                    i = pe.matmul(ps[:, 3 + g, 0:KEYS], s.wk_sb[:, f, g * P:(g + 1) * P],
                                  xct[:, f, :], start=f == 0, stop=f == 1)
                i.then_inc(k_ps, 1)

            def project_v(a):
                pe.wait_ge(k_lo, 2 * a + 1)
                for c in range(2):
                    for f in range(2):
                        i = pe.matmul(ps[:, 3, c * DIM:(c + 1) * DIM], xct[:, f, c * P:(c + 1) * P],
                                      s.wv_sb[:, f, :], start=f == 0, stop=f == 1)
                i.then_inc(v_ps, 1)
                pe.wait_ge(k_lo, 2 * a + 2)
                for f in range(2):
                    i = pe.matmul(ps[0:CTX, 4, 0:DIM], xct[:, f, N:KEYS], s.wv_sb[:, f, :],
                                  start=f == 0, stop=f == 1)
                i.then_inc(v_ps, 1)

            def spread_v0(a, c):
                pe.wait_ge(v0_done, a + 1)
                if c is not None:
                    pe.wait_ge(wp_read, c + 1)
                else:
                    wait(pe, tv0_done, a)
                pe.matmul(ps[:, 7, 0:DIM], s.ctx0_sb[:], v0f[:], start=True, stop=True).then_inc(v0_ps, 1)

            def max_unit(a, par, u):
                p, t = u // HALVES, u % HALVES
                if u == 0:
                    pe.wait_ge(stacked, 16 * STACK_DMAS * (a + 1))
                    pe.wait_ge(v_lo, 2 * a + 2)
                else:
                    pe.wait_ge(max_done, UNITS * a + u)
                if u == UNITS // 2:
                    pe.wait_ge(mrow_done, 2 * a + 1)
                for e in range(2):
                    i = pe.matmul(ps[:, 3 + e, 0:SOFT], qs[par][0:STACK + 1, 2 * p + e, t * P:(t + 1) * P],
                                  ks[par][0:STACK + 1, 2 * p + e, 0:SOFT], start=True, stop=True)
                i.then_inc(max_ps, 1)

            def max_rows(a, g):
                pe.wait_ge(max_done, UNITS * a + (g + 1) * UNITS // 2)
                rows = ps[0:GROUP, 3, 0:P].bitcast(F16)
                for t in range(HALVES):
                    i = pe.transpose(rows[:, t * P:(t + 1) * P], nmx[:, t, g * GROUP:(g + 1) * GROUP],
                                     s.id16[:])
                i.then_inc(mrow_ps, 1)

            def score(b, par, p, e):
                t = PAIRS * b + p
                if e == 0 and p % 4 == 0:
                    pe.wait_ge(mrow_in[p // 4], 16 * (b + 1))
                h = 2 * p + e
                if not (isinstance(b, int) and t == 0):
                    pe.wait_ge(exped, 3 * t - 2 + e)
                for c in range(2):
                    i = pe.matmul(ps[:, e, c * N:(c + 1) * N], ks[par][:, h, c * P:(c + 1) * P],
                                  qs[par][:, h, :], start=True, stop=True)
                i.then_inc(scores, 1)

            def score_ctx(b, par, p):
                t = PAIRS * b + p
                if not (isinstance(b, int) and t == 0):
                    pe.wait_ge(exped, 3 * t)
                for e in range(2):
                    i = pe.matmul(ps[0:CTX_SOFT, 2, e * N:(e + 1) * N], ks[par][:, 2 * p + e, 2 * P:SOFT],
                                  qs[par][:, 2 * p + e, :], start=True, stop=True)
                i.then_inc(scores, 1)

            def values(b, par, p, e):
                t = PAIRS * b + p
                if e == 0:
                    pe.wait_ge(p_lo, 2 * t + 2)
                    if p == 0:
                        wait(pe, pv_read, b)
                h = 2 * p + e
                for q in range(HALVES):
                    n = 0
                    for left, right in ((ph, vh), (ph, vl), (pl, vh)):
                        for c in range(3):
                            k = P if c < 2 else CTX_SOFT
                            slab, at = (e, c * N) if c < 2 else (2, e * N)
                            i = pe.matmul(ps[:, 5 + q, h * VW:(h + 1) * VW],
                                          left[p % 2][0:k, slab, at + q * P:at + (q + 1) * P],
                                          right[par][0:k, c, h, :], start=n == 0, stop=n == 8)
                            n += 1
                if e == 1:
                    i.then_inc(pv, 1)

            def z_t(c, last):
                pe.wait_ge(z_done, c + 1)
                pe.wait_ge(qkv_done, 2 * c + 1)
                if not last:
                    pe.wait_ge(tv0_done, c + 2)
                transposes(z, 7).then_inc(zt_ps, 1)

            def project_out(c):
                pe.wait_ge(zt_done, 2 * c + 2)
                for t in range(HALVES):
                    for f in range(2):
                        i = pe.matmul(ps[:, 7, t * DIM:(t + 1) * DIM], zt[:, f, t * P:(t + 1) * P],
                                      s.wp_sb[:, f, :], start=f == 0, stop=f == 1)
                i.then_inc(wp_ps, 1)

            def y_t(c, a):
                pe.wait_ge(y_done, c + 1)
                if a is not None:
                    pe.wait_ge(tv0_done, a + 1)
                transposes(z, 7).then_inc(yt_ps, 1)

            def project_qkv(c, t):
                if t == 0:
                    pe.wait_ge(yt_done, 2 * c + 2)
                else:
                    pe.wait_ge(qkv_done, 2 * c + 2)
                for f in range(2):
                    i = pe.matmul(ps[:, 7, 0:QKV], zt[:, f, t * P:(t + 1) * P], s.wqkv_sb[:, f, :],
                                  start=f == 0, stop=f == 1)
                i.then_inc(qkv_ps, 1)

            def iteration(b, a, c, par):
                odd = 1 - par
                for p in range(PAIRS):
                    unit = [4 * (p - 4) + k for k in range(4)] if a is not None and p >= 4 else []
                    if p == 6 and a is not None:
                        max_rows(a, 0)
                    for e in range(2):
                        if unit:
                            max_unit(a, odd, unit[e])
                        if b is not None:
                            score(b, par, p, e)
                    if b is not None:
                        score_ctx(b, par, p)
                    for e in range(2):
                        if unit:
                            max_unit(a, odd, unit[2 + e])
                        if p == 0 and c is not None:
                            values(c, odd, PAIRS - 1, e)
                        elif p > 0 and b is not None:
                            values(b, par, p - 1, e)
                    if p == 1:
                        if a is not None:
                            x_t(a)
                        if c is not None:
                            z_t(c, b is None)
                    if p == 2:
                        if a is not None:
                            project_q(a)
                            project_k(a, 0)
                        if c is not None:
                            project_out(c)
                        if a is not None:
                            project_k(a, 1)
                    if p == 3 and a is not None:
                        project_v(a)
                        spread_v0(a, c)
                    if c is not None and p == 4:
                        y_t(c, a)
                    if c is not None and p in (5, 6):
                        project_qkv(c, p - 5)
                if a is not None:
                    max_rows(a, 1)

            pe.wait_ge(init_done, 2)
            pe.wait_ge(s.const_in, s.N_CONST)
            pe.wait_ge(s.id16_done, 1)
            iteration(None, 0, None, 1)
            iteration(0, 1, None, 0)
            with pe.Fori(0, (B - 2) // 2) as i:
                for odd in (0, 1):
                    n = 2 * i + 1 + odd
                    iteration(n, n + 1, n - 1, 1 - odd)
            iteration(B - 1, None, B - 2, 1)
            iteration(None, None, B - 1, 0)

        @block.scalar
        def _(act):
            def copy(dst, src):
                return act.activation(dst, src, ACT.Copy)

            def x_t(a):
                copy(xct[:, :, N:KEYS], s.ctx_sb[:, a, :, :]).then_inc(xct_done, 1)
                act.wait_ge(xt_ps, a + 1)
                copy(xct[:, :, 0:N], ps[:, 3, :].rearrange("p (f n) -> p f n", f=2)).then_inc(xct_done, 1)

            def split_q(a):
                wait(act, stacked, 16 * STACK_DMAS * a)
                act.wait_ge(q_ps, a + 1)
                copy(qh[:], ps[:, 4, :].rearrange("p (g n) -> p g n", g=2)).then_inc(q_hi, 1)

            def split_k(a, g):
                act.wait_ge(k_ps, 2 * a + g + 1)
                copy(kh[:, g, :], ps[:, 3 + g, 0:KEYS]).then_inc(k_hi, 1)

            def split_v(a, par):
                act.wait_ge(v_ps, 2 * a + 1)
                copy(vh[par][:, 0:2, :, 0:HD],
                     ps[:, 3, :].rearrange("p (c h d) -> p c h d", c=2, h=H)).then_inc(v_hi, 1)
                act.wait_ge(v_ps, 2 * a + 2)
                copy(v0f[:], ps[0:CTX, 4, 0:DIM]).then_inc(v0_done, 1)
                copy(vh[par][0:CTX, 2, :, 0:HD], heads(ps[0:CTX, 4, 0:DIM])).then_inc(v_hi, 1)

            def max_rows(a, g):
                act.wait_ge(mrow_ps, 2 * a + g + 1)
                wait(act, mrow_in[g], 16 * a)
                copy(mrow[g][:], ps[0:GROUP, 3, 0:P].bitcast(F16)).then_inc(mrow_done, 1)

            def exponentials(b, p):
                t = PAIRS * b + p
                if not (isinstance(b, int) and t < 2):
                    act.wait_ge(p_lo, 2 * t - 2)
                for e in range(2):
                    act.wait_ge(scores, 3 * t + e + 1)
                    act.activation(pf[p % 2][:, e, :], ps[:, e, :], ACT.Exp, scale=SCALE).then_inc(exped, 1)
                act.wait_ge(scores, 3 * t + 3)
                act.activation(pf[p % 2][0:CTX_SOFT, 2, :], ps[0:CTX_SOFT, 2, :], ACT.Exp,
                               scale=SCALE).then_inc(exped, 1)

            def affine(dst, gain, bias, done):
                for f in range(2):
                    act.activation(dst[:, f, :], ps[:, 7, f * N:(f + 1) * N], ACT.Identity,
                                   bias=bias[:, f:f + 1], scale=gain[:, f:f + 1]).then_inc(done, 1)

            def z_t(c):
                act.wait_ge(zt_ps, c + 1)
                affine(zt, s.g_sb, s.b_sb, zt_done)

            def y_t(c):
                act.wait_ge(yt_ps, c + 1)
                affine(zt, s.g1_sb, s.b1_sb, yt_done)

            def store_qkv(c, t):
                act.wait_ge(qkv_ps, 2 * c + t + 1)
                copy(s.qkv[:, HALVES * c + t, :], ps[:, 7, 0:QKV]).then_inc(qkv_done, 1)

            def iteration(b, a, c, par):
                odd = 1 - par
                for p in range(PAIRS):
                    if p == 6 and a is not None:
                        max_rows(a, 0)
                    if b is not None:
                        exponentials(b, p)
                    if p == 1:
                        if a is not None:
                            x_t(a)
                        if c is not None:
                            z_t(c)
                    if p == 2 and a is not None:
                        split_q(a)
                        split_k(a, 0)
                        split_k(a, 1)
                    if p == 3 and a is not None:
                        split_v(a, odd)
                    if c is not None and p == 4:
                        y_t(c)
                    if c is not None and p in (5, 6):
                        store_qkv(c, p - 5)
                if a is not None:
                    max_rows(a, 1)

            act.wait_ge(s.const_in, s.N_CONST)
            copy(s.id16[:], s.id32[:]).then_inc(s.id16_done, 1)
            act.activation(s.tgate[:], s.gate_sb[:], ACT.Tanh).then_inc(s.tgate_done, 1)
            act.wait_ge(s.tgate_done, 1)
            copy(s.gate_sb[:], s.tgate[:]).then_inc(qkv_done, 1)
            act.wait_ge(init_done, 2)
            iteration(None, 0, None, 1)
            iteration(0, 1, None, 0)
            with act.Fori(0, (B - 2) // 2) as i:
                for odd in (0, 1):
                    n = 2 * i + 1 + odd
                    iteration(n, n + 1, n - 1, 1 - odd)
            iteration(B - 1, None, B - 2, 1)
            iteration(None, None, B - 1, 0)

        @block.vector
        def _(dve):
            A_STEPS, C_STEPS = 4, 15

            def moments(own, src, bn, mv, ve, ready):
                for t in range(HALVES):
                    own.step(dve.bn_stats(bn[:, t, :], src(t)))
                hold(dve, held_dve, own.semaphore, own.base + own.n)
                for t in range(HALVES):
                    own.step(dve.bn_aggr(mv[:, t, :], bn[:, t, :]))
                own.settle()
                dve.tensor_scalar(ve[:], mv[:, :, 1], EPS, None, ALU.add).then_inc(ready, 1)

            def center(dst, src, mv, rstd):
                for t in range(HALVES):
                    i = dve.tensor_scalar(dst(t), src(t), mv[:, t, 0:1], rstd[:, t:t + 1], ALU.subtract,
                                          ALU.mult)
                return i

            def rows(tensor, b):
                return lambda t: tensor[:, HALVES * b + t, :]

            def part(tensor):
                return lambda t: tensor[:, t, :]

            def norm_x(a):
                moments(Own(dve, own_a, A_STEPS * a), rows(s.x1, a), bn_a, mv_a, ve_a, var_a)

            def center_x(a):
                dve.wait_ge(rstd_a_done, a + 1)
                center(part(xn), rows(s.x1, a), mv_a, rstd_a).then_inc(xn_done, 1)

            def split_q(a):
                dve.wait_ge(q_hi, a + 1)
                dve.tensor_tensor(ql[:], ps[:, 4, :].rearrange("p (g n) -> p g n", g=2), qh[:],
                                  ALU.subtract).then_inc(q_lo, 1)

            def split_k(a, g):
                dve.wait_ge(k_hi, 2 * a + g + 1)
                dve.tensor_tensor(kl[:, g, :], ps[:, 3 + g, 0:KEYS], kh[:, g, :],
                                  ALU.subtract).then_inc(k_lo, 1)

            def split_v(a, par):
                dve.wait_ge(v_hi, 2 * a + 1)
                dve.tensor_tensor(vl[par][:, 0:2, :, 0:HD],
                                  ps[:, 3, :].rearrange("p (c h d) -> p c h d", c=2, h=H),
                                  vh[par][:, 0:2, :, 0:HD], ALU.subtract).then_inc(v_lo, 1)
                dve.wait_ge(v_hi, 2 * a + 2)
                dve.tensor_tensor(vl[par][0:CTX, 2, :, 0:HD], heads(ps[0:CTX, 4, 0:DIM]),
                                  vh[par][0:CTX, 2, :, 0:HD], ALU.subtract).then_inc(v_lo, 1)

            def gate_v0(a, par):
                dve.wait_ge(v0_ps, a + 1)
                dve.tensor_tensor(heads(tv0[par][:]), heads(ps[:, 7, 0:DIM]),
                                  s.tgate[:].unsqueeze(2).to_broadcast([P, H, HD]),
                                  ALU.mult).then_inc(tv0_done, 1)

            def max_unit(a, u):
                p, t = u // HALVES, u % HALVES
                dve.wait_ge(max_ps, UNITS * a + u + 1)
                dve.tensor_reduce(nmx[:, t, 2 * p:2 * p + 2], ps[:, 3:5, 0:SOFT], AX.X, ALU.max,
                                  negate=True).then_inc(max_done, 1)

            def lo(b, p):
                t = PAIRS * b + p
                dve.wait_ge(p_hi, 2 * t + 1)
                dve.tensor_tensor(pl[p % 2][:, 0:2, :], pf[p % 2][:, 0:2, :], ph[p % 2][:, 0:2, :],
                                  ALU.subtract).then_inc(p_lo, 1)
                dve.wait_ge(p_hi, 2 * t + 2)
                dve.tensor_tensor(pl[p % 2][0:CTX_SOFT, 2, :], pf[p % 2][0:CTX_SOFT, 2, :],
                                  ph[p % 2][0:CTX_SOFT, 2, :], ALU.subtract).then_inc(p_lo, 1)

            def attended(own, c, par):
                dve.wait_ge(pv, PAIRS * c + PAIRS)
                out = ps[:, 5:7, 0:H * VW].rearrange("p q (h w) -> p q h w", w=VW)
                own.step(dve.reciprocal(rs[:], out[:, :, :, HD]))
                own.settle()
                for t in range(HALVES):
                    i = dve.tensor_tensor(heads(o32[:, t, :]), out[:, t, :, 0:HD],
                                          rs[:, t, :].unsqueeze(2).to_broadcast([P, H, HD]), ALU.mult)
                i.then_inc(pv_read, 1)
                dve.wait_ge(pv_read, c + 1)
                own.step(dve.tensor_tensor(ob[:], o32[:], tv0[par][:].unsqueeze(1).to_broadcast(
                    [P, HALVES, DIM]), ALU.add))
                own.settle()
                moments(own, part(ob), bn_c, mv_c, ve_c, var_c)

            def center_attended(c):
                dve.wait_ge(rstd_c_done, 3 * c + 1)
                center(part(z), part(ob), mv_c, rstd_c).then_inc(z_done, 1)

            def residual(own, c):
                dve.wait_ge(wp_ps, c + 1)
                dve.wait_ge(bias_added, c + 1)
                for t in range(HALVES):
                    i = dve.tensor_tensor(s.x1[:, HALVES * c + t, :], ps[:, 7, t * DIM:(t + 1) * DIM],
                                          s.x1[:, HALVES * c + t, :], ALU.add)
                i.then_inc(wp_read, 1)
                hold(dve, held_dve, wp_read, c + 1)
                moments(own, rows(s.x1, c), bn_c, mv_c, ve_c, var_c)

            def second_norm(own, c):
                dve.wait_ge(rstd_c_done, 3 * c + 2)
                own.step(center(rows(s.hid, c), rows(s.x1, c), mv_c, rstd_c))
                hold(dve, held_dve, own_c, own.base + own.n)
                moments(own, rows(s.hid, c), bn_c, mv_c, ve_c, var_c)

            def center_second(c):
                dve.wait_ge(rstd_c_done, 3 * c + 3)
                center(part(z), rows(s.hid, c), mv_c, rstd_c).then_inc(y_done, 1)

            def iteration(b, a, c, par):
                odd = 1 - par
                own = Own(dve, own_c, C_STEPS * c) if c is not None else None
                for p in range(PAIRS):
                    if p == 0:
                        if a is not None:
                            norm_x(a)
                        if c is not None:
                            attended(own, c, odd)
                    if p == 2:
                        if a is not None:
                            split_q(a)
                            split_k(a, 0)
                        if c is not None:
                            residual(own, c)
                        if a is not None:
                            split_k(a, 1)
                    if p == 3:
                        if a is not None:
                            split_v(a, odd)
                            gate_v0(a, odd)
                        if c is not None:
                            second_norm(own, c)
                    if p >= 4 and a is not None:
                        for k in range(4):
                            max_unit(a, 4 * (p - 4) + k)
                    if b is not None:
                        lo(b, p)
                    if p == 0:
                        if a is not None:
                            center_x(a)
                        if c is not None:
                            center_attended(c)
                    if p == 3 and c is not None:
                        center_second(c)
                if own is not None:
                    assert own.n == C_STEPS, own.n

            for t in (0, 1):
                dve.memset(qs[t][STACK:ROWS, :, :], 0.0)
                i = dve.memset(ks[t][STACK:ROWS, :, :], 1.0)
            i.then_inc(init_done, 1)
            dve.wait_ge(s.x_in[0], 16)
            dve.wait_ge(init_done, 2)
            dve.wait_ge(s.const_in, s.N_CONST)
            dve.wait_ge(s.tgate_done, 1)
            iteration(None, 0, None, 1)
            dve.wait_ge(s.x_in[1], 16)
            iteration(0, 1, None, 0)
            dve.wait_ge(s.x_in[2], 16)
            with dve.Fori(0, (B - 2) // 2) as i:
                for odd in (0, 1):
                    n = 2 * i + 1 + odd
                    iteration(n, n + 1, n - 1, 1 - odd)
            iteration(B - 1, None, B - 2, 1)
            iteration(None, None, B - 1, 0)


def second_attention(nc, sb, sem, s):
    ps = s.ps
    prod = [sb(f"prod{i}", [P, B, DIM]) for i in range(2)]
    sc = [sb(f"sc{i}", [P, B, B, H]) for i in range(HALVES)]
    red = [sb(f"red{i}", [P, B, H]) for i in range(HALVES)]
    inv = [sb(f"inv{i}", [P, B, H]) for i in range(HALVES)]
    ao = [sb(f"ao{i}", [P, B, DIM]) for i in range(HALVES)]
    aot = [sb(f"aot{i}", [P, 2, P]) for i in range(2)]
    bn = sb("bn_d", [P, B, 6])
    mv = [sb(f"mv_d{i}", [P, B, 2]) for i in range(HALVES)]
    ve = [sb(f"ve_d{i}", [P, B]) for i in range(HALVES)]
    rstd = [sb(f"rstd_d{i}", [P, B]) for i in range(HALVES)]
    centered = [sb(f"centered{i}", [P, DIM]) for i in range(2)]

    masked = sem("masked")
    prod_pool, prod_dve, prod_read = sem("prod_pool"), sem("prod_dve"), sem("prod_read")
    shifted, exp_done, weighted = sem("shifted"), sem("exp_done"), sem("weighted")
    ao_done, ao_ps, aot_done, proj_ps, hid_done = sem("ao_done"), sem("ao_ps"), sem("aot_done"), sem("proj_ps"), sem("hid_done")
    var_d, rstd_done, centered_done, ln2_done = sem("var_d"), sem("rstd_d_done"), sem("centered_done"), sem("ln2_done")
    ln2_ps, ln2t_done, logits_ps = sem("ln2_ps"), sem("ln2t_done"), sem("logits_ps")
    own_d = sem("own_d")
    own_pool = sem("own_pool_d")
    ROUNDS = 2 * B
    POOL_KV = 3

    def score_product(eng, half, k, g, dst):
        n = B - k
        q = s.qkv[:, half::HALVES, g * REP * HD:(g + 1) * REP * HD][:, k:B, :]
        key = s.qkv[:, HALVES * k + half, H * HD + g * HD:H * HD + (g + 1) * HD]
        return eng.tensor_tensor(
            dst[:, 0:n, g * REP * HD:(g + 1) * REP * HD].rearrange("p q (r d) -> p q r d", d=HD),
            q.rearrange("p q (r d) -> p q r d", d=HD),
            key.unsqueeze(1).unsqueeze(1).to_broadcast([P, n, REP, HD]), ALU.mult)

    def value_product(eng, half, q, g, dst):
        n = q + 1
        at = (H + KV_H) * HD + g * HD
        v = s.qkv[:, half::HALVES, at:at + HD][:, 0:n, :]
        w = sc[half][:, q, 0:n, g * REP:(g + 1) * REP]
        return eng.tensor_tensor(
            dst[:, 0:n, g * REP * HD:(g + 1) * REP * HD].rearrange("p k (r d) -> p k r d", d=HD),
            w.unsqueeze(3).to_broadcast([P, n, REP, HD]),
            v.unsqueeze(2).to_broadcast([P, n, REP, HD]), ALU.mult)

    with nc.Block() as block:

        @block.gpsimd
        def _(pool):
            for half in range(HALVES):
                for q in range(B - 1):
                    i = pool.memset(sc[half][:, q, q + 1:B, :], MASKED)
                i.then_inc(masked, 1)
            for half in range(HALVES):
                for r in range(ROUNDS):
                    n = ROUNDS * half + r
                    if n >= 2:
                        pool.wait_ge(prod_read, n - 1)
                    if r == B:
                        pool.wait_ge(weighted, half + 1)
                    for g in range(KV_H - POOL_KV, KV_H):
                        i = (score_product if r < B else value_product)(pool, half, r % B, g, prod[n % 2])
                    i.then_inc(prod_pool, 1)
            for half in range(HALVES):
                pool.wait_ge(var_d, half + 1)
                pool.tensor_tensor(rstd[half][:], ve[half][:], s.minus_half[:, 0:B],
                                   ALU.pow).then_inc(rstd_done, 1)
                for k in range(B):
                    t, n = HALVES * k + half, B * half + k
                    pool.tensor_tensor(s.x1[:, t, :], s.x1[:, t, :], s.hid[:, t, :], ALU.add)
                    pool.wait_ge(centered_done, n + 1)
                    pool.tensor_tensor(centered[n % 2][:], centered[n % 2][:], s.w2n_sb[:],
                                       ALU.mult).then_inc(own_pool, 1)
                    pool.wait_ge(own_pool, n + 1)
                    pool.tensor_tensor(s.ln2[:, t, :], centered[n % 2][:], s.b2n_sb[:],
                                       ALU.add).then_inc(ln2_done, 1)

        @block.vector
        def _(dve):
            own = Own(dve, own_d, 0)

            def round_(half, r):
                n = ROUNDS * half + r
                for g in range(KV_H - POOL_KV):
                    i = (score_product if r < B else value_product)(dve, half, r % B, g, prod[n % 2])
                i.then_inc(prod_dve, 1)
                dve.wait_ge(prod_dve, n + 1)
                dve.wait_ge(prod_pool, n + 1)
                if r < B:
                    q = B - r
                    dve.tensor_reduce(sc[half][:, r:B, r, :],
                                      prod[n % 2][:, 0:q, :].rearrange("p q (h d) -> p q h d", d=HD),
                                      AX.X, ALU.add).then_inc(prod_read, 1)
                else:
                    q = r - B
                    dve.tensor_reduce(ao[half][:, q, :],
                                      prod[n % 2][:, 0:q + 1, :].rearrange("p k x -> p x k"),
                                      AX.X, ALU.add).then_inc(prod_read, 1)

            def softmax(half):
                by_key = sc[half][:].rearrange("p q k h -> p q h k")
                dve.wait_ge(prod_read, ROUNDS * half + B)
                own.step(dve.tensor_reduce(red[half][:], by_key, AX.X, ALU.max))
                own.settle()
                dve.tensor_tensor(sc[half][:], sc[half][:], red[half][:].unsqueeze(2).to_broadcast(
                    [P, B, B, H]), ALU.subtract).then_inc(shifted, 1)
                dve.wait_ge(exp_done, half + 1)
                own.step(dve.tensor_reduce(red[half][:], by_key, AX.X, ALU.add))
                own.settle()
                own.step(dve.reciprocal(inv[half][:], red[half][:]))
                own.settle()
                dve.tensor_tensor(sc[half][:], sc[half][:], inv[half][:].unsqueeze(2).to_broadcast(
                    [P, B, B, H]), ALU.mult).then_inc(weighted, 1)
                dve.wait_ge(weighted, half + 1)

            def hidden(half):
                for k in range(B):
                    t, n = HALVES * k + half, B * half + k
                    dve.wait_ge(proj_ps, n + 1)
                    dve.tensor_tensor(s.hid[:, t, :], ps[:, 2 + n % 2, 0:DIM], s.hid[:, t, :],
                                      ALU.add).then_inc(hid_done, 1)
                    dve.wait_ge(hid_done, n + 1)
                    own.step(dve.bn_stats(bn[:, k, :], s.hid[:, t, :]))
                own.settle()
                for k in range(B):
                    own.step(dve.bn_aggr(mv[half][:, k, :], bn[:, k, :]))
                own.settle()
                dve.tensor_scalar(ve[half][:], mv[half][:, :, 1], EPS, None, ALU.add).then_inc(var_d, 1)
                dve.wait_ge(rstd_done, half + 1)
                for k in range(B):
                    t, n = HALVES * k + half, B * half + k
                    if n >= 2:
                        dve.wait_ge(ln2_done, n - 1)
                    dve.tensor_scalar(centered[n % 2][:], s.hid[:, t, :], mv[half][:, k, 0:1],
                                      rstd[half][:, k:k + 1], ALU.subtract,
                                      ALU.mult).then_inc(centered_done, 1)

            for half in range(HALVES):
                dve.wait_ge(masked, half + 1)
                for r in range(B):
                    round_(half, r)
                softmax(half)
                for r in range(B, ROUNDS):
                    round_(half, r)
            for half in range(HALVES):
                hidden(half)

        @block.scalar
        def _(act):
            for half in range(HALVES):
                act.wait_ge(shifted, half + 1)
                act.activation(sc[half][:], sc[half][:], ACT.Exp, scale=SCALE).then_inc(exp_done, 1)
            for half in range(HALVES):
                for k in range(B):
                    n = B * half + k
                    act.wait_ge(ao_ps, n + 1)
                    act.activation(aot[n % 2][:], ps[:, n % 2, 0:2 * P].rearrange("p (f t) -> p f t", f=2),
                                   ACT.Copy).then_inc(aot_done, 1)
            for n in range(NT):
                act.wait_ge(ln2_ps, n + 1)
                act.activation(aot[n % 2][:], ps[:, n % 2, 0:2 * P].rearrange("p (f t) -> p f t", f=2),
                               ACT.Copy).then_inc(ln2t_done, 1)

        @block.tensor
        def _(pe):
            def transpose_tile(src, n):
                for f in range(2):
                    i = pe.transpose(ps[:, n % 2, f * P:(f + 1) * P], src[:, f * P:(f + 1) * P], s.id32[:])
                return i

            for half in range(HALVES):
                for k in range(B):
                    n = B * half + k
                    pe.wait_ge(prod_read, ROUNDS * half + B + k + 1)
                    if n >= 2:
                        pe.wait_ge(aot_done, n - 1)
                    transpose_tile(ao[half][:, k, :], n).then_inc(ao_ps, 1)
                    pe.wait_ge(aot_done, n + 1)
                    if n >= 2:
                        pe.wait_ge(hid_done, n - 1)
                    for f in range(2):
                        i = pe.matmul(ps[:, 2 + n % 2, 0:DIM], aot[n % 2][:, f, :], s.wproj_sb[:, f, :],
                                      start=f == 0, stop=f == 1)
                    i.then_inc(proj_ps, 1)
            for half in range(HALVES):
                for k in range(B):
                    t, n = HALVES * k + half, B * half + k
                    pe.wait_ge(ln2_done, n + 1)
                    if n >= 2:
                        pe.wait_ge(ln2t_done, n - 1)
                    transpose_tile(s.ln2[:, t, :], n).then_inc(ln2_ps, 1)
                    pe.wait_ge(ln2t_done, n + 1)
                    for f in range(2):
                        i = pe.matmul(ps[:, 4, t * E:(t + 1) * E], aot[n % 2][:, f, :], s.wr_sb[:, f, :],
                                      start=f == 0, stop=f == 1)
                    i.then_inc(logits_ps, 1)


def route(nc, sb, sem, s):
    ps = s.ps
    mx, tot, inv = (sb(n, [P, NT]) for n in ("mx_e", "tot_e", "inv_e"))
    probs = sb("probs", [P, NT, E])
    best = sb("best", [P, NT, 8])
    which = sb("which", [P, NT, 8], U32)
    whichf = sb("whichf", [P, NT, TOP])
    hot = [sb(f"hot{k}", [P, NT, E]) for k in range(TOP)]
    both = sb("both", [P, NT, E])
    earlier = sb("earlier", [P, NT, E])
    place = sb("place", [P, NT, E])
    tmp = [sb(f"tmp_e{k}", [P, NT, E]) for k in range(2)]
    at, base, keep, row = ([sb(f"{n}{k}", [P, NT]) for k in range(TOP)] for n in ("at", "base", "keep", "row"))
    shifted, exp_done, both_done, counted = sem("shifted_e"), sem("exp_done_e"), sem("both_done"), sem("counted")
    own_e = sem("own_e")

    def over_experts(ap):
        return ap[:].unsqueeze(2).to_broadcast([P, NT, E])

    def over_tiles(ap):
        return ap[:].unsqueeze(1).to_broadcast([P, NT, E])

    with nc.Block() as block:

        @block.scalar
        def _(act):
            act.wait_ge(shifted, 1)
            act.activation(probs[:], probs[:], ACT.Exp).then_inc(exp_done, 1)

        @block.tensor
        def _(pe):
            pe.wait_ge(both_done, 1)
            pe.matmul(ps[:, 5, 0:NT * E], s.before_sb[:, 0, :], both[:].rearrange("p t e -> p (t e)"),
                      start=True, stop=True).then_inc(counted, 1)
            pe.matmul(ps[:, 6, 0:NT * E], s.before_sb[:, 1, :], both[:].rearrange("p t e -> p (t e)"),
                      start=True, stop=True).then_inc(counted, 1)

        @block.vector
        def _(dve):
            own = Own(dve, own_e, 0)

            def do(*instructions):
                for i in instructions:
                    own.step(i)
                own.settle()

            def tiles(bank):
                return ps[:, bank, 0:NT * E].rearrange("p (t e) -> p t e", e=E)

            do(dve.tensor_reduce(mx[:], tiles(4), AX.X, ALU.max))
            dve.tensor_tensor(probs[:], tiles(4), over_experts(mx), ALU.subtract).then_inc(shifted, 1)
            dve.wait_ge(exp_done, 1)
            do(dve.tensor_reduce(tot[:], probs[:], AX.X, ALU.add))
            do(dve.reciprocal(inv[:], tot[:]))
            do(dve.tensor_tensor(probs[:], probs[:], over_experts(inv), ALU.mult))
            do(*(dve.max(best[:, t, :], probs[:, t, :]) for t in range(NT)))
            do(*(dve.max_index(which[:, t, :], best[:, t, :], probs[:, t, :]) for t in range(NT)))
            do(dve.tensor_copy(whichf[:], which[:, :, 0:TOP]))
            do(*(dve.tensor_tensor(hot[k][:], over_tiles(s.experts_sb), over_experts(whichf[:, :, k]),
                                   ALU.is_equal) for k in range(TOP)))
            dve.tensor_tensor(both[:], hot[0][:], hot[1][:], ALU.add).then_inc(both_done, 1)
            do(dve.memset(earlier[:, 0, :], 0.0))
            dve.wait_ge(counted, 2)
            for t in range(1, NT):
                do(dve.tensor_tensor(earlier[:, t, :], tiles(6)[:, t - 1, :], earlier[:, t - 1, :], ALU.add))
            do(dve.tensor_tensor(place[:], tiles(5), earlier[:], ALU.add))
            for k in range(TOP):
                do(dve.tensor_tensor(tmp[0][:], hot[k][:], place[:], ALU.mult),
                   dve.tensor_tensor(tmp[1][:], hot[k][:], over_tiles(s.base_sb), ALU.mult))
                do(dve.tensor_reduce(at[k][:], tmp[0][:], AX.X, ALU.add),
                   dve.tensor_reduce(base[k][:], tmp[1][:], AX.X, ALU.add))
                do(dve.tensor_scalar(keep[k][:], at[k][:], float(CAP), None, ALU.is_lt))
                do(dve.tensor_tensor(s.gates[k][:], best[:, :, k], keep[k][:], ALU.mult),
                   dve.tensor_tensor(row[k][:], base[k][:], at[k][:], ALU.add),
                   dve.tensor_scalar(at[k][:], at[k][:], float(CAP - 1), None, ALU.min))
                do(dve.tensor_tensor(row[k][:], row[k][:], s.trash_sb[:, k, :], ALU.subtract),
                   dve.tensor_tensor(at[k][:], at[k][:], base[k][:], ALU.add))
                do(dve.tensor_tensor(row[k][:], row[k][:], keep[k][:], ALU.mult),
                   dve.tensor_copy(s.read_rows[k][:], at[k][:]))
                do(dve.tensor_tensor(row[k][:], row[k][:], s.trash_sb[:, k, :], ALU.add))
                do(dve.tensor_copy(s.write_rows[k][:], row[k][:]))


def run_experts(nc, sb, sem, s):
    ps = s.ps
    w1r = [sb(f"w1r{i}", [P, 2, FFN]) for i in range(2)]
    w2r = [sb(f"w2r{i}", [P, FFN // P, DIM]) for i in range(2)]
    xr = [sb(f"xr{i}", [P, len(EXPERT_TILES), DIM]) for i in range(2)]
    xt = [sb(f"xt{i}", [P, 2, CAP]) for i in range(2)]
    act_t = [sb(f"act_t{i}", [P, FFN // P, CAP]) for i in range(2)]
    y = [sb(f"y{i}", [P, len(EXPERT_TILES), DIM]) for i in range(2)]
    got = [[sb(f"got{k}{i}", [P, DIM]) for i in range(2)] for k in range(TOP)]
    F = FFN // P
    FULL = CAP // P * P
    LAST = len(EXPERT_TILES) - 1

    weights_in = [sem("weights_in0"), sem("weights_in1")]
    rows_in = [sem("rows_in0"), sem("rows_in1")]
    y_out = [sem("y_out0"), sem("y_out1")]
    zeroed, scattered = s.zeroed, sem("scattered")
    xt_ps, xt_done, up_ps, up_done, down_ps, y_done = (
        sem("xt_ps_f"), sem("xt_done_f"), sem("up_ps"), sem("up_done"), sem("down_ps"), sem("y_done_f"))
    gathered = [sem("gathered0"), sem("gathered1")]
    weighed, out_done = sem("weighed"), sem("out_done")
    own_f = sem("own_f")
    ys_done = sem("ys_done")

    with nc.Block() as block:

        @block.sync
        def _(sp):
            def load_weights(e, par):
                sp.dma_start(w1r[par][:], s.w1[e].rearrange("(f p) n -> p f n", p=P)).then_inc(weights_in[par], 16)
                sp.dma_start(w2r[par][:], s.w2[e].rearrange("(f p) n -> p f n", p=P)).then_inc(weights_in[par], 16)

            def load_rows(e, par):
                full = s.slots_dram[0:E * CAP].rearrange("(e r) d -> e r d", e=E)[e]
                sp.dma_start(xr[par][:, 0:LAST, :], full[0:FULL].rearrange("(t p) d -> p t d", p=P)).then_inc(rows_in[par], 16)
                sp.dma_start(xr[par][0:CAP - FULL, LAST, :], full[FULL:CAP]).then_inc(rows_in[par], 16)

            def store(e, par):
                sp.wait_ge(y_done, LAST * e + e + LAST + 1)
                full = s.ffn_dram.rearrange("(e r) d -> e r d", e=E)[e]
                sp.dma_start(full[0:FULL].rearrange("(t p) d -> p t d", p=P), y[par][:, 0:LAST, :]).then_inc(y_out[par], 16)
                sp.dma_start(full[FULL:CAP], y[par][0:CAP - FULL, LAST, :]).then_inc(y_out[par], 16)

            for n in range(2):
                load_weights(n, n)
            sp.wait_ge(scattered, 16 * TOP * NT)
            sp.wait_ge(zeroed, 16 * s.N_ZERO)
            for n in range(2):
                load_rows(n, n)
            with sp.Fori(0, (E - 2) // 2) as i:
                for par in (0, 1):
                    e = 2 * i + par
                    sp.wait_ge(xt_ps, e + 1)
                    load_rows(e + 2, par)
                    store(e, par)
                    load_weights(e + 2, par)
            for e in (E - 2, E - 1):
                store(e, e % 2)
            for par in (0, 1):
                sp.wait_ge(y_out[par], 32 * E // 2)
            sp.sem_inc(ys_done, 1)
            for t in range(NT):
                sp.wait_ge(weighed, t + 1)
                sp.dma_start(s.out_rows[t], s.x1[:, t, :]).then_inc(out_done, 16)
            sp.wait_ge(out_done, 16 * NT)

        @block.gpsimd
        def _(pool):
            pool.wait_ge(zeroed, 16 * s.N_ZERO)
            for t in range(NT):
                for k in range(TOP):
                    pool.indirect_dma_start(
                        s.slots_dram, bass.IndirectOffsetOnAxis(ap=s.write_rows[k][:, t:t + 1], axis=0),
                        s.ln2[:, t, :], None).then_inc(scattered, 16)
            pool.wait_ge(ys_done, 1)
            for t in range(NT):
                if t >= 2:
                    pool.wait_ge(weighed, t - 1)
                for k in range(TOP):
                    pool.indirect_dma_start(
                        got[k][t % 2][:], None, s.ffn_dram,
                        bass.IndirectOffsetOnAxis(ap=s.read_rows[k][:, t:t + 1], axis=0)
                    ).then_inc(gathered[t % 2], 16)

        @block.tensor
        def _(pe):
            def transposes(e, par):
                pe.wait_ge(rows_in[par], 32 * (e // 2 + 1) if isinstance(e, int) else 16 * (e - par) + 32)
                wait(pe, xt_done, 2 * e)
                for f in range(2):
                    for n, (at, m) in enumerate(EXPERT_TILES):
                        i = pe.transpose(ps[:, f, at:at + m], xr[par][0:m, n, f * P:(f + 1) * P],
                                         s.id32[0:m, 0:m])
                i.then_inc(xt_ps, 1)

            def up(e, par):
                pe.wait_ge(weights_in[par], 32 * (e // 2 + 1) if isinstance(e, int) else 16 * (e - par) + 32)
                pe.wait_ge(xt_done, 2 * e + 2)
                for j in range(F):
                    if not (isinstance(e, int) and e == 0 and j < 2):
                        pe.wait_ge(up_done, F * e + j - 1)
                    for f in range(2):
                        i = pe.matmul(ps[:, 2 + j % 2, 0:CAP], w1r[par][:, f, j * P:(j + 1) * P],
                                      xt[par][:, f, :], start=f == 0, stop=f == 1)
                    i.then_inc(up_ps, 1)

            def down(e, par):
                pe.wait_ge(up_done, F * e + F)
                for n, (at, m) in enumerate(EXPERT_TILES):
                    wait(pe, y_done, len(EXPERT_TILES) * (e - 1) + n + 1)
                    for j in range(F):
                        i = pe.matmul(ps[0:m, 4 + n, 0:DIM], act_t[par][:, j, at:at + m], w2r[par][:, j, :],
                                      start=j == 0, stop=j == F - 1)
                    i.then_inc(down_ps, 1)

            transposes(0, 0)

            def expert(e, par, last=False):
                up(e, par)
                if not last:
                    transposes(e + 1, 1 - par)
                down(e, par)

            expert(0, 0)
            expert(1, 1)
            with pe.Fori(1, E // 2 - 1) as i:
                for par in (0, 1):
                    expert(2 * i + par, par)
            expert(E - 2, 0)
            expert(E - 1, 1, last=True)

        @block.scalar
        def _(act):
            def gelu(e, par):
                for j in range(F):
                    act.wait_ge(up_ps, F * e + j + 1)
                    act.activation(act_t[par][:, j, :], ps[:, 2 + j % 2, 0:CAP],
                                   ACT.Gelu_apprx_tanh).then_inc(up_done, 1)

            with act.Fori(0, E // 2) as i:
                for par in (0, 1):
                    gelu(2 * i + par, par)

        @block.vector
        def _(dve):
            def copy_xt(e, par):
                dve.wait_ge(xt_ps, e + 1)
                for f in range(2):
                    dve.tensor_copy(xt[par][:, f, :], ps[:, f, 0:CAP]).then_inc(xt_done, 1)

            def copy_y(e, par):
                wait(dve, y_out[par], 32 * (e // 2) if isinstance(e, int) else 16 * (e - par))
                for n, (at, m) in enumerate(EXPERT_TILES):
                    dve.wait_ge(down_ps, len(EXPERT_TILES) * e + n + 1)
                    dve.tensor_copy(y[par][0:m, n, :], ps[0:m, 4 + n, 0:DIM]).then_inc(y_done, 1)

            def expert(e, par, last=False):
                if not last:
                    copy_xt(e + 1, 1 - par)
                copy_y(e, par)

            copy_xt(0, 0)
            expert(0, 0)
            expert(1, 1)
            with dve.Fori(1, E // 2 - 1) as i:
                for par in (0, 1):
                    expert(2 * i + par, par)
            expert(E - 2, 0)
            expert(E - 1, 1, last=True)
            own = Own(dve, own_f, 0)
            for t in range(NT):
                dve.wait_ge(gathered[t % 2], 16 * TOP * (t // 2 + 1))
                own.step(dve.scalar_tensor_tensor(s.x1[:, t, :], got[0][t % 2][:], s.gates[0][:, t:t + 1],
                                                  s.x1[:, t, :], ALU.mult, ALU.add))
                own.settle()
                dve.scalar_tensor_tensor(s.x1[:, t, :], got[1][t % 2][:], s.gates[1][:, t:t + 1],
                                         s.x1[:, t, :], ALU.mult, ALU.add).then_inc(weighed, 1)


def bass_xattn_moe(nc, x, ctx_t, wq, wk, wv, gate, ln_g, ln_b, wp, bp, ln1_w, ln1_b, ln2_w, ln2_b,
                   wqkv, wproj, wrouter, w1, w2, ident, before, ctx0_row, experts, expert_base,
                   trash_rows, out):
    with ExitStack() as whole:
        s = Shared()

        def allocator(stack):
            def sb(name, shape, dt=F32):
                return stack.enter_context(nc.sbuf_tensor(name, shape, dt))
            return sb

        def sem(name):
            return whole.enter_context(nc.semaphore(name))

        sb = allocator(whole)
        s.ps = whole.enter_context(nc.psum_tensor("ps", [P, 8, 512], F32))
        s.slots_dram = nc.dram_tensor("expert_slots", (TRASH + TOP * NT * P, DIM), F32).ap()
        s.ffn_dram = nc.dram_tensor("expert_results", (E * CAP, DIM), F32).ap()
        s.w1, s.w2 = w1, w2
        s.out_rows = out.rearrange("b (h p) d -> (b h) p d", p=P)

        s.x1 = sb("x1", [P, NT, DIM])
        s.hid = sb("hid", [P, NT, DIM])
        s.id32 = sb("id32", [P, P])
        s.minus_half = sb("minus_half", [P, NT])
        s.wproj_sb = sb("wproj_sb", [P, 2, DIM])
        s.wr_sb = sb("wr_sb", [P, 2, E])
        s.w2n_sb, s.b2n_sb = sb("w2n_sb", [P, DIM]), sb("b2n_sb", [P, DIM])
        s.before_sb = sb("before_sb", [P, 2, P])
        s.experts_sb, s.base_sb = sb("experts_sb", [P, E]), sb("base_sb", [P, E])
        s.trash_sb = sb("trash_sb", [P, TOP, NT])
        s.gates = [sb(f"gates{k}", [P, NT]) for k in range(TOP)]
        s.read_rows = [sb(f"read_rows{k}", [P, NT], U32) for k in range(TOP)]
        s.write_rows = [sb(f"write_rows{k}", [P, NT], U32) for k in range(TOP)]

        s.const_in, s.late_in = sem("const_in"), sem("late_in")
        s.x_in = [sem(f"x_in{i}") for i in range(3)]
        s.id16_done, s.tgate_done = sem("id16_done"), sem("tgate_done")
        x_tiles = x.rearrange("b (h p) d -> p (b h) d", p=P)

        s.qkv = sb("qkv", [P, NT, QKV])
        with ExitStack() as first:
            sb = allocator(first)
            s.zeros = sb("zeros", [P, 4 * DIM])
            s.id16 = sb("id16", [P, P], F16)
            s.wq_sb, s.wk_sb, s.wv_sb, s.wp_sb = (
                sb(n, [P, 2, DIM]) for n in ("wq_sb", "wk_sb", "wv_sb", "wp_sb"))
            s.wqkv_sb = sb("wqkv_sb", [P, 2, QKV])
            s.g_sb, s.b_sb, s.g1_sb, s.b1_sb = (sb(n, [P, 2]) for n in ("g_sb", "b_sb", "g1_sb", "b1_sb"))
            s.bp_sb = sb("bp_sb", [P, DIM])
            s.gate_sb, s.tgate = sb("gate_sb", [P, H]), sb("tgate", [P, H])
            s.ctx0_sb = sb("ctx0_sb", [CTX, P])
            s.ctx_sb = sb("ctx_sb", [P, B, 2, CTX])
            early = [(s.id32, ident), (s.ctx_sb, ctx_t), (s.wq_sb, wq), (s.wk_sb, wk), (s.wv_sb, wv),
                     (s.bp_sb, bp.partition_broadcast(P)), (s.gate_sb, gate.partition_broadcast(P)),
                     (s.ctx0_sb, ctx0_row), (s.wp_sb, wp), (s.wqkv_sb, wqkv), (s.g_sb, ln_g),
                     (s.b_sb, ln_b), (s.g1_sb, ln1_w), (s.b1_sb, ln1_b)]
            late = [(s.wproj_sb, wproj), (s.wr_sb, wrouter), (s.w2n_sb, ln2_w.partition_broadcast(P)),
                    (s.b2n_sb, ln2_b.partition_broadcast(P)), (s.before_sb, before),
                    (s.experts_sb, experts.partition_broadcast(P)),
                    (s.base_sb, expert_base.partition_broadcast(P)), (s.trash_sb, trash_rows)]
            s.N_CONST = 16 * len(early)
            s.late_count = 16 * len(late)
            s.zeroed = sem("zeroed")
            s.N_ZERO = E * CAP // (4 * P)

            def load_constants(sp):
                sp.dma_start(s.x1[:, 0:2, :], x_tiles[:, 0:2, :]).then_inc(s.x_in[0], 16)
                for dst, src in early:
                    sp.dma_start(dst[:], src).then_inc(s.const_in, 16)
                sp.dma_start(s.x1[:, 2:4, :], x_tiles[:, 2:4, :]).then_inc(s.x_in[1], 16)
                sp.dma_start(s.x1[:, 4:NT, :], x_tiles[:, 4:NT, :]).then_inc(s.x_in[2], 16)
                for dst, src in late:
                    sp.dma_start(dst[:], src).then_inc(s.late_in, 16)

            def clear_slots(sp):
                view = s.slots_dram[0:E * CAP].rearrange("(n p r) d -> n p (r d)", p=P, r=4)
                for n in range(s.N_ZERO):
                    sp.dma_start(view[n], s.zeros[:]).then_inc(s.zeroed, 16)
                sp.wait_ge(s.zeroed, 16 * s.N_ZERO)
                sp.wait_ge(s.late_in, s.late_count)
            s.load_constants, s.clear_slots = load_constants, clear_slots
            cross_attention(nc, sb, sem, s)
        s.ln2 = whole.enter_context(nc.sbuf_tensor("ln2", [P, NT, DIM], F32))
        with ExitStack() as second:
            second_attention(nc, allocator(second), sem, s)
        with ExitStack() as routing:
            route(nc, allocator(routing), sem, s)
        with ExitStack() as last:
            run_experts(nc, allocator(last), sem, s)


_INS = ("x", "ctx_t", "wq", "wk", "wv", "gate", "ln_g", "ln_b", "wp", "bp", "ln1_w", "ln1_b", "ln2_w", "ln2_b",
        "wqkv", "wproj", "wrouter", "w1", "w2", "ident", "before", "ctx0_row", "experts", "expert_base",
        "trash_rows")


def kernel(**inputs):
    import concourse.bacc as bacc
    from concourse.bass_utils import run_bass_kernel_spmd

    a = {k: np.asarray(v) for k, v in inputs.items()}

    def chunks(w):
        return w.reshape(2, P, -1).transpose(1, 0, 2)

    def by_head_dim(w):
        return w.reshape(DIM, 2, GROUP, HD).transpose(0, 1, 3, 2).reshape(DIM, DIM)

    def column(v):
        return v.reshape(2, P).T

    ctx = np.concatenate([a["ctx_1024"][:, 1:], a["ctx_1024"][:, :1]], axis=1)
    ctx0_row = np.zeros((CTX, P), np.float32)
    ctx0_row[CTX - 1] = 1.0
    before = np.stack([np.triu(np.ones((P, P), np.float32), 1), np.ones((P, P), np.float32)], axis=1)
    trash = (TRASH + np.arange(TOP * NT * P, dtype=np.float32).reshape(TOP, NT, P)).transpose(2, 0, 1)
    arrays = {
        "x": a["x"],
        "ctx_t": ctx.reshape(B, CTX, 2, P).transpose(3, 0, 2, 1),
        "wq": chunks(by_head_dim(a["L0_xattn_Wq"].T)),
        "wk": chunks(by_head_dim(a["L0_xattn_Wk"].T)),
        "wv": chunks(a["L0_xattn_Wv"].T),
        "gate": a["L0_xattn_gate"].reshape(H),
        "ln_g": column(a["L0_xattn_ln_g"]),
        "ln_b": column(a["L0_xattn_ln_b"]),
        "wp": chunks(a["L0_xattn_Wp"].T),
        "bp": a["L0_xattn_bp"],
        "ln1_w": column(a["L0_ffn_ln1_weight"]),
        "ln1_b": column(a["L0_ffn_ln1_bias"]),
        "ln2_w": a["L0_ffn_ln2_weight"],
        "ln2_b": a["L0_ffn_ln2_bias"],
        "wqkv": chunks(a["L0_ffn_qkv_weight"].T),
        "wproj": chunks(a["L0_ffn_proj_weight"].T),
        "wrouter": chunks(a["L0_ffn_router_weight"].T),
        "w1": a["L0_ffn_moe_w1"].transpose(0, 2, 1),
        "w2": a["L0_ffn_moe_w2"].transpose(0, 2, 1),
        "ident": np.eye(P, dtype=np.float32),
        "before": before,
        "ctx0_row": ctx0_row,
        "experts": np.arange(E, dtype=np.float32),
        "expert_base": np.arange(E, dtype=np.float32) * CAP,
        "trash_rows": trash,
    }
    nc = bacc.Bacc("TRN2", target_bir_lowering=False, num_devices=1)
    feeds, args = {}, []
    for name in _INS:
        array = np.ascontiguousarray(arrays[name])
        feeds[f"in_{name}"] = array
        args.append(nc.dram_tensor(f"in_{name}", array.shape, mybir.dt.from_np(array.dtype),
                                   kind="ExternalInput").ap())
    args.append(nc.dram_tensor("out", (B, N, DIM), F32, kind="ExternalOutput").ap())
    bass_xattn_moe(nc, *args)
    r = run_bass_kernel_spmd(nc, [feeds], core_ids=[0])
    return r.results[0]["out"]
```

```python
from contextlib import ExitStack

import numpy as np

import concourse.bass as bass
import concourse.mybir as mybir

F32 = mybir.dt.float32
F16 = mybir.dt.float16
BF16 = mybir.dt.bfloat16
U32 = mybir.dt.uint32
ALU = mybir.AluOpType
ACT = mybir.ActivationFunctionType
AX = mybir.AxisListType

P = 128
B, N, DIM = 8, 256, 256
HALVES = N // P
CTX = 77
H, HD = 16, 16
KV_H = 4
REP = H // KV_H
SOFT = N + CTX - 1
CTX_SOFT = CTX - 1
KEYS = N + CTX
NT = B * N // P
E, TOP, FFN = 16, 2, 512
CAP = -(-B * N * TOP * 5 // (E * 4))
TRASH = E * CAP
EPS = 1e-5
SCALE = HD ** -0.5
QKV = (H + 2 * KV_H) * HD
PAIRS = H // 2
GROUP = 8
PARTS = 4
STACK = PARTS * HD
ROWS = STACK + 2
VW = HD + 1
UNITS = PAIRS * HALVES
OWN_UNITS = {0: range(10, 12), 1: range(12, 14), 2: range(14, 16)}
NEXT_UNITS = {4: range(0, 2), 5: range(2, 5), 6: range(5, 8), 7: range(8, 10)}
MASKED = -1e30
EXPERT_TILES = [(s, min(P, CAP - s)) for s in range(0, CAP, P)]


class Shared:
    pass


def wait(eng, semaphore, value):
    if not isinstance(value, int) or value > 0:
        eng.wait_ge(semaphore, value)


def hold(eng, held, semaphore, value):
    eng.wait_ge(semaphore, value)
    eng.sem_inc(held, 1)


class Own:

    def __init__(self, eng, semaphore, base):
        self.eng, self.semaphore, self.base, self.n = eng, semaphore, base, 0

    def step(self, instruction):
        instruction.then_inc(self.semaphore, 1)
        self.n += 1

    def settle(self):
        self.eng.wait_ge(self.semaphore, self.base + self.n)


def heads(ap):
    return ap.rearrange("p (h d) -> p h d", d=HD)


def cross_attention(nc, sb, sem, s):
    ps = s.ps
    xn = sb("xn", [P, HALVES, DIM])
    xct = sb("xct", [P, 2, KEYS])
    qh, ql = (sb(n, [P, 2, N], F16) for n in ("qh", "ql"))
    kh, kl = (sb(n, [P, 2, KEYS], F16) for n in ("kh", "kl"))
    qs = [sb(f"qs{i}", [ROWS, H, N], F16) for i in range(2)]
    ks = [sb(f"ks{i}", [ROWS, H, KEYS], F16) for i in range(2)]
    vh = [sb(f"vh{i}", [P, 3, H, VW], F16) for i in range(2)]
    vl = [sb(f"vl{i}", [P, 3, H, VW], F16) for i in range(2)]
    v0f = sb("v0f", [CTX, DIM])
    tv0 = [sb(f"tv0{i}", [P, DIM]) for i in range(2)]
    nmx = sb("nmx", [P, HALVES, H], F16)
    mrow = [sb(f"mrow{i}", [GROUP, N], F16) for i in range(2)]
    pf = [sb(f"pf{i}", [P, 3, 512]) for i in range(2)]
    ph = [sb(f"ph{i}", [P, 3, 512], F16) for i in range(2)]
    pl = [sb(f"pl{i}", [P, 3, 512], F16) for i in range(2)]
    rs = sb("rs", [P, HALVES, H])
    o32 = sb("o32", [P, HALVES, DIM])
    ob = sb("ob", [P, HALVES, DIM], BF16)
    z = sb("z", [P, HALVES, DIM])
    zt = sb("zt", [P, 2, N])
    bn_a, bn_c = sb("bn_a", [P, NT, 6]), sb("bn_c", [P, HALVES, 6])
    mv_a, mv_c = sb("mv_a", [P, NT, 2]), sb("mv_c", [P, HALVES, 2])
    ve_a, ve_c = sb("ve_a", [P, NT]), sb("ve_c", [P, HALVES])
    rstd_a, rstd_c = sb("rstd_a", [P, NT, 1]), sb("rstd_c", [P, HALVES])

    init_done = sem("init_done")
    var_a, rstd_a_done, xn_done, bias_added = sem("var_a"), sem("rstd_a_done"), sem("xn_done"), sem("bias_added")
    xt_ps, xct_done = sem("xt_ps"), sem("xct_done")
    q_ps, k_ps, v_ps, v0_ps = sem("q_ps"), sem("k_ps"), sem("v_ps"), sem("v0_ps")
    q_hi, k_hi, v_hi, v0_done = sem("q_hi"), sem("k_hi"), sem("v_hi"), sem("v0_done")
    q_lo, k_lo, v_lo, tv0_done = sem("q_lo"), sem("k_lo"), sem("v_lo"), sem("tv0_done")
    stacked = sem("stacked")
    max_ps, max_done = sem("max_ps"), sem("max_done")
    mrow_ps, mrow_done = sem("mrow_ps"), sem("mrow_done")
    mrow_in = [sem("mrow_in0"), sem("mrow_in1")]
    scores, p_hi, p_lo, pool_lo, pv = (
        sem("scores"), sem("p_hi"), sem("p_lo"), sem("pool_lo"), sem("pv"))
    pv_read, var_c, rstd_c_done = sem("pv_read"), sem("var_c"), sem("rstd_c_done")
    z_done, zt_ps, zt_done = sem("z_done"), sem("zt_ps"), sem("zt_done")
    wp_ps, wp_read, y_done, yt_ps, yt_done = sem("wp_ps"), sem("wp_read"), sem("y_done"), sem("yt_ps"), sem("yt_done")
    qkv_ps, qkv_done = sem("qkv_ps"), sem("qkv_done")
    own_a, own_c, held_dve = sem("own_a"), sem("own_c"), sem("held_dve")
    STACK_DMAS = 2 * PARTS * 2

    with nc.Block() as block:

        @block.sync
        def _(sp):
            s.stacks = list(zip(qs, ks))
            s.load_constants(sp)

            def stack(dst, src, g, rows):
                for r in rows:
                    sp.dma_start(dst[r * HD:(r + 1) * HD, g * GROUP:(g + 1) * GROUP, :],
                                 src[:, g, :]).then_inc(stacked, 16)

            def put_maxima(b, par, g):
                sp.wait_ge(mrow_done, 2 * b + g + 1)
                sp.dma_start(qs[par][STACK + 1:STACK + 2, g * GROUP:(g + 1) * GROUP, :],
                             mrow[g][:, :]).then_inc(mrow_in[g], 16)

            def iteration(b, a, par):
                odd = 1 - par
                if a is not None:
                    for g in range(2):
                        sp.wait_ge(q_hi, a + 1)
                        stack(qs[odd], qh, g, (0, 1))
                    for g in range(2):
                        sp.wait_ge(q_lo, a + 1)
                        stack(qs[odd], ql, g, (2, 3))
                    sp.wait_ge(k_hi, 2 * a + 1)
                    stack(ks[odd], kh, 0, (0, 2))
                    sp.wait_ge(k_lo, 2 * a + 1)
                    stack(ks[odd], kl, 0, (1, 3))
                    sp.wait_ge(k_hi, 2 * a + 2)
                    stack(ks[odd], kh, 1, (0, 2))
                    sp.wait_ge(k_lo, 2 * a + 2)
                if b is not None:
                    put_maxima(b, par, 1)
                if a is not None:
                    stack(ks[odd], kl, 1, (1, 3))
                    put_maxima(a, odd, 0)

            iteration(None, 0, 1)
            iteration(0, 1, 0)
            with sp.Fori(0, (B - 2) // 2) as i:
                for odd in (0, 1):
                    n = 2 * i + 1 + odd
                    iteration(n, n + 1, 1 - odd)
            iteration(B - 1, None, 1)
            s.clear_slots(sp)

        @block.gpsimd
        def _(pool):
            def init():
                for t in (0, 1):
                    pool.memset(vh[t][:], 1.0)
                    pool.memset(vl[t][:], 0.0)
                pool.memset(s.zeros[:], 0.0)
                pool.memset(s.minus_half[:], -0.5).then_inc(init_done, 1)
                pool.wait_ge(init_done, 1)

            def power(c, k):
                pool.wait_ge(var_c, 3 * c + k + 1)
                pool.tensor_tensor(rstd_c[:], ve_c[:], s.minus_half[:, 0:HALVES], ALU.pow).then_inc(rstd_c_done, 1)

            def power_x(first, last, k):
                pool.wait_ge(var_a, k)
                pool.tensor_tensor(rstd_a[:, first:last, 0], ve_a[:, first:last], s.minus_half[:, first:last],
                                   ALU.pow).then_inc(rstd_a_done, 1)

            def add_bias(b):
                pool.wait_ge(xn_done, b + 1)
                for t in range(HALVES):
                    i = pool.tensor_tensor(s.x1[:, HALVES * b + t, :], s.x1[:, HALVES * b + t, :],
                                           s.bp_sb[:], ALU.add)
                i.then_inc(bias_added, 1)

            def lo(b, p):
                t = PAIRS * b + p
                pool.wait_ge(p_hi, 3 * t + 2)
                pool.tensor_tensor(pl[p % 2][:, 1, :], pf[p % 2][:, 1, :], ph[p % 2][:, 1, :], ALU.subtract)
                pool.wait_ge(p_hi, 3 * t + 3)
                pool.tensor_tensor(pl[p % 2][0:CTX_SOFT, 2, :], pf[p % 2][0:CTX_SOFT, 2, :],
                                   ph[p % 2][0:CTX_SOFT, 2, :], ALU.subtract).then_inc(pool_lo, 1)

            def iteration(b, a, c):
                for p in range(PAIRS):
                    if b is not None:
                        lo(b, p)
                    if c is not None and p in (1, 3, 5):
                        power(c, {1: 0, 3: 1, 5: 2}[p])
                    if p == 1 and a is not None:
                        add_bias(a)

            init()
            power_x(0, HALVES, 1)
            power_x(HALVES, NT, 2)
            pool.wait_ge(s.const_in, s.N_CONST)
            iteration(None, 0, None)
            iteration(0, 1, None)
            with pool.Fori(0, (B - 2) // 2) as i:
                for odd in (0, 1):
                    n = 2 * i + 1 + odd
                    iteration(n, n + 1, n - 1)
            iteration(B - 1, None, B - 2)
            iteration(None, None, B - 1)

        @block.tensor
        def _(pe):
            def transposes(src, bank):
                for f in range(2):
                    for t in range(HALVES):
                        i = pe.transpose(ps[:, bank, f * N + t * P:f * N + (t + 1) * P],
                                         src[:, t, f * P:(f + 1) * P], s.id32[:])
                return i

            def x_t(a, c):
                pe.wait_ge(xn_done, a + 1)
                if c is not None:
                    pe.wait_ge(qkv_done, 2 * c + 1)
                else:
                    wait(pe, tv0_done, a)
                transposes(xn, 7).then_inc(xt_ps, 1)

            def project_q(a):
                pe.wait_ge(xct_done, 2 * a + 2)
                for g in range(2):
                    for f in range(2):
                        i = pe.matmul(ps[:, 7, g * N:(g + 1) * N], s.wq_sb[:, f, g * P:(g + 1) * P],
                                      xct[:, f, 0:N], start=f == 0, stop=f == 1)
                i.then_inc(q_ps, 1)

            def project_k(a, g):
                if g == 0:
                    pe.wait_ge(q_lo, a + 1)
                else:
                    pe.wait_ge(k_lo, 2 * a + 1)
                for f in range(2):
                    i = pe.matmul(ps[:, 7, 0:KEYS], s.wk_sb[:, f, g * P:(g + 1) * P],
                                  xct[:, f, :], start=f == 0, stop=f == 1)
                i.then_inc(k_ps, 1)

            def project_v(a, c):
                if c is not None:
                    pe.wait_ge(wp_read, c + 1)
                else:
                    pe.wait_ge(k_lo, 2 * a + 2)
                for n in range(2):
                    for f in range(2):
                        i = pe.matmul(ps[:, 7, n * DIM:(n + 1) * DIM], xct[:, f, n * P:(n + 1) * P],
                                      s.wv_sb[:, f, :], start=f == 0, stop=f == 1)
                i.then_inc(v_ps, 1)

            def project_ctx_v(a):
                pe.wait_ge(v_lo, 2 * a + 1)
                for f in range(2):
                    i = pe.matmul(ps[0:CTX, 7, 0:DIM], xct[:, f, N:KEYS], s.wv_sb[:, f, :],
                                  start=f == 0, stop=f == 1)
                i.then_inc(v_ps, 1)

            def spread_v0(a):
                pe.wait_ge(v0_done, a + 1)
                pe.wait_ge(v_lo, 2 * a + 2)
                pe.matmul(ps[:, 7, 0:DIM], s.ctx0_sb[:], v0f[:], start=True, stop=True).then_inc(v0_ps, 1)

            def max_unit(a, par, u):
                p, t = u // HALVES, u % HALVES
                if u == 0:
                    pe.wait_ge(stacked, 16 * STACK_DMAS * (a + 1))
                    wait(pe, mrow_done, 2 * a)
                else:
                    pe.wait_ge(max_done, UNITS * a + u)
                if u == UNITS // 2:
                    pe.wait_ge(mrow_done, 2 * a + 1)
                for e in range(2):
                    i = pe.matmul(ps[:, 3 + e, 0:SOFT], qs[par][0:STACK + 1, 2 * p + e, t * P:(t + 1) * P],
                                  ks[par][0:STACK + 1, 2 * p + e, 0:SOFT], start=True, stop=True)
                i.then_inc(max_ps, 1)

            def max_rows(a, g):
                pe.wait_ge(max_done, UNITS * a + (g + 1) * UNITS // 2)
                rows = ps[0:GROUP, 3, 0:P].bitcast(F16)
                for t in range(HALVES):
                    i = pe.transpose(rows[:, t * P:(t + 1) * P], nmx[:, t, g * GROUP:(g + 1) * GROUP],
                                     s.id16[:])
                i.then_inc(mrow_ps, 1)

            def score(b, par, p, e):
                t = PAIRS * b + p
                if e == 0 and p % 4 == 0:
                    pe.wait_ge(mrow_in[p // 4], 16 * (b + 1))
                h = 2 * p + e
                if not (isinstance(b, int) and t == 0):
                    pe.wait_ge(p_hi, 3 * t - 2 + e)
                for c in range(2):
                    i = pe.matmul(ps[:, e, c * N:(c + 1) * N], ks[par][:, h, c * P:(c + 1) * P],
                                  qs[par][:, h, :], start=True, stop=True)
                i.then_inc(scores, 1)

            def score_ctx(b, par, p):
                t = PAIRS * b + p
                if not (isinstance(b, int) and t == 0):
                    pe.wait_ge(p_hi, 3 * t)
                for e in range(2):
                    i = pe.matmul(ps[0:CTX_SOFT, 2, e * N:(e + 1) * N], ks[par][:, 2 * p + e, 2 * P:SOFT],
                                  qs[par][:, 2 * p + e, :], start=True, stop=True)
                i.then_inc(scores, 1)

            def values(b, par, p, e):
                t = PAIRS * b + p
                if e == 0:
                    pe.wait_ge(p_lo, t + 1)
                    pe.wait_ge(pool_lo, t + 1)
                    if p == 0:
                        wait(pe, pv_read, b)
                h = 2 * p + e
                for q in range(HALVES):
                    n = 0
                    for left, right in ((ph, vh), (ph, vl), (pl, vh)):
                        for c in range(3):
                            k = P if c < 2 else CTX_SOFT
                            slab, at = (e, c * N) if c < 2 else (2, e * N)
                            i = pe.matmul(ps[:, 5 + q, h * VW:(h + 1) * VW],
                                          left[p % 2][0:k, slab, at + q * P:at + (q + 1) * P],
                                          right[par][0:k, c, h, :], start=n == 0, stop=n == 8)
                            n += 1
                if e == 1:
                    i.then_inc(pv, 1)

            def z_t(c, a):
                pe.wait_ge(z_done, c + 1)
                if a is not None:
                    pe.wait_ge(k_lo, 2 * a + 2)
                else:
                    pe.wait_ge(qkv_done, 2 * c + 1)
                transposes(z, 7).then_inc(zt_ps, 1)

            def project_out(c):
                pe.wait_ge(zt_done, 2 * c + 2)
                for t in range(HALVES):
                    for f in range(2):
                        i = pe.matmul(ps[:, 7, t * DIM:(t + 1) * DIM], zt[:, f, t * P:(t + 1) * P],
                                      s.wp_sb[:, f, :], start=f == 0, stop=f == 1)
                i.then_inc(wp_ps, 1)

            def y_t(c, a):
                pe.wait_ge(y_done, c + 1)
                if a is not None:
                    pe.wait_ge(tv0_done, a + 1)
                transposes(z, 7).then_inc(yt_ps, 1)

            def project_qkv(c, t):
                if t == 0:
                    pe.wait_ge(yt_done, 2 * c + 2)
                else:
                    pe.wait_ge(qkv_done, 2 * c + 2)
                for f in range(2):
                    i = pe.matmul(ps[:, 7, 0:QKV], zt[:, f, t * P:(t + 1) * P], s.wqkv_sb[:, f, :],
                                  start=f == 0, stop=f == 1)
                i.then_inc(qkv_ps, 1)

            def iteration(b, a, c, par):
                odd = 1 - par
                for p in range(PAIRS):
                    units = []
                    if b is not None and p in OWN_UNITS:
                        units = [(b, par, u) for u in OWN_UNITS[p]]
                    if a is not None and p in NEXT_UNITS:
                        units = [(a, odd, u) for u in NEXT_UNITS[p]]

                    def unit():
                        if units:
                            max_unit(*units.pop(0))

                    def value(e):
                        if p == 0 and c is not None:
                            values(c, odd, PAIRS - 1, e)
                        elif p > 0 and b is not None:
                            values(b, par, p - 1, e)

                    if b is not None:
                        score(b, par, p, 0)
                        score(b, par, p, 1)
                        score_ctx(b, par, p)
                    if p == 3 and b is not None:
                        max_rows(b, 1)
                    if p == 7 and a is not None:
                        max_rows(a, 0)
                    if p == 2 and a is not None:
                        project_k(a, 1)
                    if p != 7:
                        unit()
                    if a is not None:
                        if p == 0:
                            x_t(a, c)
                        if p == 4:
                            project_v(a, c)
                        if p == 5:
                            project_ctx_v(a)
                    if p == 6 and c is not None:
                        y_t(c, a)
                    value(0)
                    if p == 1 and a is not None:
                        if b is None:
                            pe.wait_ge(s.const_in, s.N_CONST)
                        project_k(a, 0)
                    if c is not None:
                        if p == 3:
                            project_out(c)
                        if p == 7:
                            project_qkv(c, 1)
                    unit()
                    value(1)
                    if p == 0 and a is not None:
                        project_q(a)
                    if p == 5 and a is not None:
                        spread_v0(a)
                    if p == 6 and c is not None:
                        project_qkv(c, 0)
                    unit()
                    if p == 2 and c is not None:
                        z_t(c, a)
                    assert not units

            pe.wait_ge(init_done, 1)
            pe.wait_ge(s.first_in, s.N_FIRST)
            pe.wait_ge(s.id16_done, 1)
            iteration(None, 0, None, 1)
            iteration(0, 1, None, 0)
            with pe.Fori(0, (B - 2) // 2) as i:
                for odd in (0, 1):
                    n = 2 * i + 1 + odd
                    iteration(n, n + 1, n - 1, 1 - odd)
            iteration(B - 1, None, B - 2, 1)
            iteration(None, None, B - 1, 0)

        @block.scalar
        def _(act):
            def copy(dst, src):
                return act.activation(dst, src, ACT.Copy)

            def x_t(a):
                copy(xct[:, :, N:KEYS], s.ctx_sb[:, a, :, :]).then_inc(xct_done, 1)
                act.wait_ge(xt_ps, a + 1)
                copy(xct[:, :, 0:N], ps[:, 7, :].rearrange("p (f n) -> p f n", f=2)).then_inc(xct_done, 1)

            def split_q(a):
                wait(act, stacked, 16 * STACK_DMAS * a)
                act.wait_ge(q_ps, a + 1)
                copy(qh[:], ps[:, 7, :].rearrange("p (g n) -> p g n", g=2)).then_inc(q_hi, 1)

            def split_k(a, g):
                act.wait_ge(k_ps, 2 * a + g + 1)
                copy(kh[:, g, :], ps[:, 7, 0:KEYS]).then_inc(k_hi, 1)

            def split_v(a, par):
                act.wait_ge(v_ps, 2 * a + 1)
                copy(vh[par][:, 0:2, :, 0:HD],
                     ps[:, 7, :].rearrange("p (c h d) -> p c h d", c=2, h=H)).then_inc(v_hi, 1)

            def split_ctx_v(a, par):
                act.wait_ge(v_ps, 2 * a + 2)
                copy(v0f[:], ps[0:CTX, 7, 0:DIM]).then_inc(v0_done, 1)
                copy(vh[par][0:CTX, 2, :, 0:HD], heads(ps[0:CTX, 7, 0:DIM])).then_inc(v_hi, 1)

            def max_rows(a, g):
                act.wait_ge(mrow_ps, 2 * a + g + 1)
                wait(act, mrow_in[g], 16 * a)
                copy(mrow[g][:], ps[0:GROUP, 3, 0:P].bitcast(F16)).then_inc(mrow_done, 1)

            def exponentials(b, p, parts):
                t = PAIRS * b + p
                if 0 in parts and not (isinstance(b, int) and t < 2):
                    act.wait_ge(p_lo, t - 1)
                    act.wait_ge(pool_lo, t - 1)
                    act.wait_ge(pv, t - 1)
                for e in parts:
                    k = P if e < 2 else CTX_SOFT
                    act.wait_ge(scores, 3 * t + e + 1)
                    act.activation(pf[p % 2][0:k, e, :], ps[0:k, e, :], ACT.Exp, scale=SCALE)
                    act.activation(ph[p % 2][0:k, e, :], ps[0:k, e, :], ACT.Exp, scale=SCALE).then_inc(p_hi, 1)

            def affine(dst, gain, bias, done):
                for f in range(2):
                    act.activation(dst[:, f, :], ps[:, 7, f * N:(f + 1) * N], ACT.Identity,
                                   bias=bias[:, f:f + 1], scale=gain[:, f:f + 1]).then_inc(done, 1)

            def open_gate():
                act.wait_ge(s.const_in, s.N_CONST)
                act.activation(s.tgate[:], s.gate_sb[:], ACT.Tanh).then_inc(s.tgate_done, 1)
                act.wait_ge(s.tgate_done, 1)
                copy(s.gate_sb[:], s.tgate[:]).then_inc(qkv_done, 1)

            def z_t(c):
                act.wait_ge(zt_ps, c + 1)
                affine(zt, s.g_sb, s.b_sb, zt_done)

            def y_t(c):
                act.wait_ge(yt_ps, c + 1)
                affine(zt, s.g1_sb, s.b1_sb, yt_done)

            def store_qkv(c, t):
                act.wait_ge(qkv_ps, 2 * c + t + 1)
                copy(s.qkv[:, HALVES * c + t, :], ps[:, 7, 0:QKV]).then_inc(qkv_done, 1)

            def iteration(b, a, c, par):
                odd = 1 - par
                for p in range(PAIRS):
                    if p == 1 and b is None and a is not None:
                        open_gate()
                    if p == 1 and a is not None:
                        split_q(a)
                    if c is not None:
                        if p == 3:
                            z_t(c)
                        if p == 7:
                            store_qkv(c, 0)
                    if b is not None:
                        exponentials(b, p, (0,))
                    if p == 3 and b is not None:
                        max_rows(b, 1)
                    if p == 7 and a is not None:
                        max_rows(a, 0)
                    if a is not None:
                        if p == 0:
                            x_t(a)
                        if p == 2:
                            split_k(a, 1)
                        if p == 4:
                            split_v(a, odd)
                        if p == 5:
                            split_ctx_v(a, odd)
                    if p == 6 and c is not None:
                        y_t(c)
                    if b is not None:
                        exponentials(b, p, (1, 2))
                    if p == 1 and a is not None:
                        split_k(a, 0)
                    if p == 7 and c is not None:
                        store_qkv(c, 1)

            act.wait_ge(s.first_in, s.N_FIRST)
            copy(s.id16[:], s.id32[:]).then_inc(s.id16_done, 1)
            act.wait_ge(init_done, 1)
            iteration(None, 0, None, 1)
            iteration(0, 1, None, 0)
            with act.Fori(0, (B - 2) // 2) as i:
                for odd in (0, 1):
                    n = 2 * i + 1 + odd
                    iteration(n, n + 1, n - 1, 1 - odd)
            iteration(B - 1, None, B - 2, 1)
            iteration(None, None, B - 1, 0)

        @block.vector
        def _(dve):
            C_STEPS = 15

            def moments(own, src, bn, mv, ve, ready):
                for t in range(HALVES):
                    own.step(dve.bn_stats(bn[:, t, :], src(t)))
                hold(dve, held_dve, own.semaphore, own.base + own.n)
                for t in range(HALVES):
                    own.step(dve.bn_aggr(mv[:, t, :], bn[:, t, :]))
                own.settle()
                dve.tensor_scalar(ve[:], mv[:, :, 1], EPS, None, ALU.add).then_inc(ready, 1)

            def center(dst, src, mv, rstd):
                for t in range(HALVES):
                    i = dve.tensor_scalar(dst(t), src(t), mv[:, t, 0:1], rstd[:, t:t + 1], ALU.subtract,
                                          ALU.mult)
                return i

            def rows(tensor, b):
                return lambda t: tensor[:, HALVES * b + t, :]

            def part(tensor):
                return lambda t: tensor[:, t, :]

            def norm_x(own, first, last):
                for t in range(first, last):
                    own.step(dve.bn_stats(bn_a[:, t, :], s.x1[:, t, :]))
                own.settle()
                for t in range(first, last):
                    own.step(dve.bn_aggr(mv_a[:, t, :], bn_a[:, t, :]))
                own.settle()
                dve.tensor_scalar(ve_a[:, first:last], mv_a[:, first:last, 1], EPS, None,
                                  ALU.add).then_inc(var_a, 1)

            def center_x(a):
                for t in range(HALVES):
                    n = HALVES * a + t
                    i = dve.tensor_scalar(xn[:, t, :], s.x1[:, n, :], mv_a[:, n, 0:1], rstd_a[:, n, :],
                                          ALU.subtract, ALU.mult)
                i.then_inc(xn_done, 1)

            def split_q(a):
                dve.wait_ge(q_hi, a + 1)
                dve.tensor_tensor(ql[:], ps[:, 7, :].rearrange("p (g n) -> p g n", g=2), qh[:],
                                  ALU.subtract).then_inc(q_lo, 1)

            def split_k(a, g):
                dve.wait_ge(k_hi, 2 * a + g + 1)
                dve.tensor_tensor(kl[:, g, :], ps[:, 7, 0:KEYS], kh[:, g, :],
                                  ALU.subtract).then_inc(k_lo, 1)

            def split_v(a, par):
                dve.wait_ge(v_hi, 2 * a + 1)
                dve.tensor_tensor(vl[par][:, 0:2, :, 0:HD],
                                  ps[:, 7, :].rearrange("p (c h d) -> p c h d", c=2, h=H),
                                  vh[par][:, 0:2, :, 0:HD], ALU.subtract).then_inc(v_lo, 1)

            def split_ctx_v(a, par):
                dve.wait_ge(v_hi, 2 * a + 2)
                dve.tensor_tensor(vl[par][0:CTX, 2, :, 0:HD], heads(ps[0:CTX, 7, 0:DIM]),
                                  vh[par][0:CTX, 2, :, 0:HD], ALU.subtract).then_inc(v_lo, 1)

            def gate_v0(a, par):
                dve.wait_ge(v0_ps, a + 1)
                dve.tensor_tensor(heads(tv0[par][:]), heads(ps[:, 7, 0:DIM]),
                                  s.tgate[:].unsqueeze(2).to_broadcast([P, H, HD]),
                                  ALU.mult).then_inc(tv0_done, 1)

            def max_unit(a, u):
                p, t = u // HALVES, u % HALVES
                dve.wait_ge(max_ps, UNITS * a + u + 1)
                dve.tensor_reduce(nmx[:, t, 2 * p:2 * p + 2], ps[:, 3:5, 0:SOFT], AX.X, ALU.max,
                                  negate=True).then_inc(max_done, 1)

            def lo(b, p):
                t = PAIRS * b + p
                dve.wait_ge(p_hi, 3 * t + 1)
                dve.tensor_tensor(pl[p % 2][:, 0, :], pf[p % 2][:, 0, :], ph[p % 2][:, 0, :],
                                  ALU.subtract).then_inc(p_lo, 1)

            def attended(own, c, par):
                dve.wait_ge(pv, PAIRS * c + PAIRS)
                out = ps[:, 5:7, 0:H * VW].rearrange("p q (h w) -> p q h w", w=VW)
                own.step(dve.reciprocal(rs[:], out[:, :, :, HD]))
                own.settle()
                for t in range(HALVES):
                    i = dve.tensor_tensor(heads(o32[:, t, :]), out[:, t, :, 0:HD],
                                          rs[:, t, :].unsqueeze(2).to_broadcast([P, H, HD]), ALU.mult)
                i.then_inc(pv_read, 1)
                dve.wait_ge(pv_read, c + 1)
                own.step(dve.tensor_tensor(ob[:], o32[:], tv0[par][:].unsqueeze(1).to_broadcast(
                    [P, HALVES, DIM]), ALU.add))
                own.settle()
                moments(own, part(ob), bn_c, mv_c, ve_c, var_c)

            def center_attended(c):
                dve.wait_ge(rstd_c_done, 3 * c + 1)
                center(part(z), part(ob), mv_c, rstd_c).then_inc(z_done, 1)

            def residual(own, c):
                dve.wait_ge(wp_ps, c + 1)
                dve.wait_ge(bias_added, c + 1)
                for t in range(HALVES):
                    i = dve.tensor_tensor(s.x1[:, HALVES * c + t, :], ps[:, 7, t * DIM:(t + 1) * DIM],
                                          s.x1[:, HALVES * c + t, :], ALU.add)
                i.then_inc(wp_read, 1)
                hold(dve, held_dve, wp_read, c + 1)
                moments(own, rows(s.x1, c), bn_c, mv_c, ve_c, var_c)

            def second_norm(own, c):
                dve.wait_ge(rstd_c_done, 3 * c + 2)
                own.step(center(rows(s.hid, c), rows(s.x1, c), mv_c, rstd_c))
                hold(dve, held_dve, own_c, own.base + own.n)
                moments(own, rows(s.hid, c), bn_c, mv_c, ve_c, var_c)

            def center_second(c):
                dve.wait_ge(rstd_c_done, 3 * c + 3)
                center(part(z), rows(s.hid, c), mv_c, rstd_c).then_inc(y_done, 1)

            def iteration(b, a, c, par):
                odd = 1 - par
                own = Own(dve, own_c, C_STEPS * c) if c is not None else None
                for p in range(PAIRS):
                    units = []
                    if b is not None and p in OWN_UNITS:
                        units = [(b, u) for u in OWN_UNITS[p]]
                    if a is not None and p in NEXT_UNITS:
                        units = [(a, u) for u in NEXT_UNITS[p]]

                    def unit():
                        if units:
                            max_unit(*units.pop(0))

                    if a is not None:
                        if p == 0:
                            center_x(a)
                            if b is None:
                                dve.wait_ge(s.x_in[1], 16)
                                norm_x(Own(dve, own_a, 2 * HALVES), HALVES, NT)
                        if p == 2:
                            split_k(a, 0)
                        if p == 6:
                            if b is None:
                                dve.wait_ge(s.tgate_done, 1)
                            gate_v0(a, odd)
                        if p == 1:
                            split_q(a)
                    if p == 0 and c is not None:
                        lo(c, PAIRS - 1)
                    elif p > 0 and b is not None:
                        lo(b, p - 1)
                    unit()
                    if p == 2 and c is not None:
                        center_attended(c)
                    if a is not None:
                        if p == 2:
                            split_k(a, 1)
                        if p == 4:
                            split_v(a, odd)
                        if p == 5:
                            split_ctx_v(a, odd)
                    unit()
                    if c is not None:
                        if p == 0:
                            attended(own, c, odd)
                        if p == 3:
                            residual(own, c)
                        if p == 4:
                            second_norm(own, c)
                        if p == 5:
                            center_second(c)
                    unit()
                    assert not units
                if own is not None:
                    assert own.n == C_STEPS, own.n

            own = Own(dve, own_a, 0)
            dve.wait_ge(s.x_in[0], 16)
            norm_x(own, 0, HALVES)
            dve.wait_ge(rstd_a_done, 1)
            iteration(None, 0, None, 1)
            dve.wait_ge(rstd_a_done, 2)
            iteration(0, 1, None, 0)
            with dve.Fori(0, (B - 2) // 2) as i:
                for odd in (0, 1):
                    n = 2 * i + 1 + odd
                    iteration(n, n + 1, n - 1, 1 - odd)
            iteration(B - 1, None, B - 2, 1)
            iteration(None, None, B - 1, 0)


def second_attention(nc, sb, sem, s):
    ps = s.ps
    RING = 4
    prod = [sb(f"prod{i}", [P, B, DIM]) for i in range(RING)]
    sc = [sb(f"sc{i}", [P, B, B, H]) for i in range(HALVES)]
    red = [sb(f"red{i}", [P, B, H]) for i in range(HALVES)]
    inv = [sb(f"inv{i}", [P, B, H]) for i in range(HALVES)]
    ao = [sb(f"ao{i}", [P, B, DIM]) for i in range(HALVES)]
    aot = [sb(f"aot{i}", [P, 2, P]) for i in range(2)]
    ln2t = [sb(f"ln2t{i}", [P, 2, P]) for i in range(2)]
    bn = [sb(f"bn_d{i}", [P, B, 6]) for i in range(HALVES)]
    mv = [sb(f"mv_d{i}", [P, B, 2]) for i in range(HALVES)]
    ve = [sb(f"ve_d{i}", [P, B]) for i in range(HALVES)]
    rstd = [sb(f"rstd_d{i}", [P, B]) for i in range(HALVES)]
    scaled = [sb(f"scaled{i}", [P, DIM]) for i in range(3)]

    masked = sem("masked")
    prod_pool, prod_dve, prod_read = sem("prod_pool"), sem("prod_dve"), sem("prod_read")
    shifted, exp_done, weighted = sem("shifted"), sem("exp_done"), sem("weighted")
    ao_ps, aot_done, proj_ps, hid_done = sem("ao_ps"), sem("aot_done"), sem("proj_ps"), sem("hid_done")
    var_d, rstd_done, ln2_done = sem("var_d"), sem("rstd_d_done"), sem("ln2_done")
    ln2_ps, ln2t_done, logits_ps = sem("ln2_ps"), sem("ln2t_done"), sem("logits_ps")
    own_d, scaled_done = sem("own_d"), sem("scaled_done")
    ROUNDS = 2 * HALVES * B
    POOL_KV = 3

    def product(eng, n, g):
        values, half, r = n // (HALVES * B), n // B % HALVES, n % B
        dst = prod[n % RING]
        over = slice(g * REP * HD, (g + 1) * REP * HD)
        if values:
            at = (H + KV_H) * HD + g * HD
            left = sc[half][:, r, 0:r + 1, g * REP:(g + 1) * REP].unsqueeze(3).to_broadcast([P, r + 1, REP, HD])
            right = s.qkv[:, half::HALVES, at:at + HD][:, 0:r + 1, :].unsqueeze(2).to_broadcast([P, r + 1, REP, HD])
            m = r + 1
        else:
            m = B - r
            key = s.qkv[:, HALVES * r + half, H * HD + g * HD:H * HD + (g + 1) * HD]
            left = s.qkv[:, half::HALVES, over][:, r:B, :].rearrange("p q (r d) -> p q r d", d=HD)
            right = key.unsqueeze(1).unsqueeze(1).to_broadcast([P, m, REP, HD])
        return eng.tensor_tensor(dst[:, 0:m, over].rearrange("p q (r d) -> p q r d", d=HD), left, right, ALU.mult)

    TILES = [("project", n) for n in range(2 * B)] + [("logits", n) for n in range(2 * B)]

    with nc.Block() as block:

        @block.gpsimd
        def _(pool):
            for half in range(HALVES):
                for q in range(B - 1):
                    i = pool.memset(sc[half][:, q, q + 1:B, :], MASKED)
                i.then_inc(masked, 1)
            for n in range(ROUNDS):
                if n >= RING:
                    pool.wait_ge(prod_read, n - RING + 1)
                if n >= HALVES * B and n % B == 0:
                    pool.wait_ge(weighted, n // B - 1)
                for g in range(KV_H - POOL_KV, KV_H):
                    i = product(pool, n, g)
                i.then_inc(prod_pool, 1)
            for half in range(HALVES):
                pool.wait_ge(var_d, half + 1)
                pool.tensor_tensor(rstd[half][:], ve[half][:], s.minus_half[:, 0:B],
                                   ALU.pow).then_inc(rstd_done, 1)

        @block.vector
        def _(dve):
            own = Own(dve, own_d, 0)

            def products(n):
                if n >= HALVES * B and n % B == 0:
                    dve.wait_ge(weighted, n // B - 1)
                for g in range(KV_H - POOL_KV):
                    i = product(dve, n, g)
                i.then_inc(prod_dve, 1)

            def reduce(n):
                values, half, r = n // (HALVES * B), n // B % HALVES, n % B
                dve.wait_ge(prod_dve, n + 1)
                dve.wait_ge(prod_pool, n + 1)
                if values:
                    dve.tensor_reduce(ao[half][:, r, :], prod[n % RING][:, 0:r + 1, :].rearrange("p k x -> p x k"),
                                      AX.X, ALU.add).then_inc(prod_read, 1)
                else:
                    dve.tensor_reduce(sc[half][:, r:B, r, :],
                                      prod[n % RING][:, 0:B - r, :].rearrange("p q (h d) -> p q h d", d=HD),
                                      AX.X, ALU.add).then_inc(prod_read, 1)

            def by_key(half):
                return sc[half][:].rearrange("p q k h -> p q h k")

            def shift(half):
                dve.wait_ge(masked, half + 1)
                dve.wait_ge(prod_read, B * half + B)
                own.step(dve.tensor_reduce(red[half][:], by_key(half), AX.X, ALU.max))
                own.settle()
                dve.tensor_tensor(sc[half][:], sc[half][:], red[half][:].unsqueeze(2).to_broadcast(
                    [P, B, B, H]), ALU.subtract).then_inc(shifted, 1)

            def weigh(half):
                dve.wait_ge(exp_done, half + 1)
                own.step(dve.tensor_reduce(red[half][:], by_key(half), AX.X, ALU.add))
                own.settle()
                own.step(dve.reciprocal(inv[half][:], red[half][:]))
                own.settle()
                dve.tensor_tensor(sc[half][:], sc[half][:], inv[half][:].unsqueeze(2).to_broadcast(
                    [P, B, B, H]), ALU.mult).then_inc(weighted, 1)

            def hidden(n):
                half, k = n // B, n % B
                t = HALVES * k + half
                dve.wait_ge(proj_ps, n + 1)
                dve.tensor_tensor(s.hid[:, t, :], ps[:, 2 + n % 2, 0:DIM], s.hid[:, t, :],
                                  ALU.add).then_inc(hid_done, 1)

            def stats(n):
                half, k = n // B, n % B
                dve.wait_ge(hid_done, n + 1)
                own.step(dve.bn_stats(bn[half][:, k, :], s.hid[:, HALVES * k + half, :]))

            def variance(half):
                own.settle()
                for k in range(B):
                    own.step(dve.bn_aggr(mv[half][:, k, :], bn[half][:, k, :]))
                own.settle()
                dve.tensor_scalar(ve[half][:], mv[half][:, :, 1], EPS, None, ALU.add).then_inc(var_d, 1)

            def scale(n):
                half, k = n // B, n % B
                if n >= 3:
                    dve.wait_ge(ln2_done, n - 2)
                dve.scalar_tensor_tensor(scaled[n % 3][:], s.hid[:, HALVES * k + half, :], mv[half][:, k, 0:1],
                                         s.w2n_sb[:], ALU.subtract, ALU.mult).then_inc(scaled_done, 1)

            def norm(n):
                half, k = n // B, n % B
                if k == 0:
                    dve.wait_ge(rstd_done, half + 1)
                dve.wait_ge(scaled_done, n + 1)
                dve.scalar_tensor_tensor(s.ln2[:, HALVES * k + half, :], scaled[n % 3][:],
                                         rstd[half][:, k:k + 1], s.b2n_sb[:], ALU.mult,
                                         ALU.add).then_inc(ln2_done, 1)

            products(0)
            for n in range(ROUNDS):
                if n + 1 < ROUNDS:
                    products(n + 1)
                reduce(n)
                if n in (B - 1, 2 * B - 1):
                    shift(n // B)
                if n in (B + 1, 2 * B + 1):
                    weigh(n // B - 1)
                if n >= 3 * B:
                    hidden(n - 3 * B)
                    if n > 3 * B:
                        stats(n - 3 * B - 1)
            stats(B - 1)
            variance(0)
            scale(0)
            for k in range(B):
                if k + 1 < B:
                    scale(k + 1)
                norm(k)
                hidden(B + k)
                if k >= 1:
                    stats(B + k - 1)
            stats(2 * B - 1)
            variance(1)
            scale(B)
            for k in range(B):
                if k + 1 < B:
                    scale(B + k + 1)
                norm(B + k)

        @block.scalar
        def _(act):
            def exponentials(half):
                act.wait_ge(shifted, half + 1)
                act.activation(sc[half][:], sc[half][:], ACT.Exp, scale=SCALE).then_inc(exp_done, 1)

            def evacuate(what, n):
                src, dst, ready, done = {"project": (0, aot, ao_ps, aot_done),
                                         "logits": (6, ln2t, ln2_ps, ln2t_done)}[what]
                act.wait_ge(ready, n + 1)
                act.activation(dst[n % 2][:], ps[:, src + n % 2, 0:2 * P].rearrange("p (f t) -> p f t", f=2),
                               ACT.Copy).then_inc(done, 1)

            exponentials(0)
            exponentials(1)
            for what, n in TILES:
                evacuate(what, n)

        @block.tensor
        def _(pe):
            def transpose_tile(src, bank):
                for f in range(2):
                    i = pe.transpose(ps[:, bank, f * P:(f + 1) * P], src[:, f * P:(f + 1) * P], s.id32[:])
                return i

            def transposed(what, n):
                half, k = n // B, n % B
                if what == "project":
                    pe.wait_ge(prod_read, (HALVES + half) * B + k + 1)
                    if n >= 2:
                        pe.wait_ge(aot_done, n - 1)
                    transpose_tile(ao[half][:, k, :], n % 2).then_inc(ao_ps, 1)
                else:
                    pe.wait_ge(ln2_done, n + 1)
                    if n >= 2:
                        pe.wait_ge(ln2t_done, n - 1)
                    transpose_tile(s.ln2[:, HALVES * k + half, :], 6 + n % 2).then_inc(ln2_ps, 1)

            def multiplied(what, n):
                if what == "project":
                    pe.wait_ge(aot_done, n + 1)
                    if n >= 2:
                        pe.wait_ge(hid_done, n - 1)
                    for f in range(2):
                        i = pe.matmul(ps[:, 2 + n % 2, 0:DIM], aot[n % 2][:, f, :], s.wproj_sb[:, f, :],
                                      start=f == 0, stop=f == 1)
                    i.then_inc(proj_ps, 1)
                else:
                    t = HALVES * (n % B) + n // B
                    pe.wait_ge(ln2t_done, n + 1)
                    for f in range(2):
                        i = pe.matmul(ps[:, 4, t * E:(t + 1) * E], ln2t[n % 2][:, f, :], s.wr_sb[:, f, :],
                                      start=f == 0, stop=f == 1)
                    i.then_inc(logits_ps, 1)

            for i, tile in enumerate(TILES):
                transposed(*tile)
                if i > 0:
                    multiplied(*TILES[i - 1])
            multiplied(*TILES[-1])


def route(nc, sb, sem, s):
    ps = s.ps
    mx, tot, inv = (sb(n, [P, NT]) for n in ("mx_e", "tot_e", "inv_e"))
    probs = sb("probs", [P, NT, E])
    best = sb("best", [P, NT, 8])
    which = sb("which", [P, NT, 8], U32)
    whichf = sb("whichf", [P, NT, TOP])
    hot = [sb(f"hot{k}", [P, NT, E]) for k in range(TOP)]
    both = sb("both", [P, NT, E])
    earlier = sb("earlier", [P, NT, E])
    place = sb("place", [P, NT, E])
    tmp = [sb(f"tmp_e{k}", [P, NT, E]) for k in range(2)]
    at, base, keep, row = ([sb(f"{n}{k}", [P, NT]) for k in range(TOP)] for n in ("at", "base", "keep", "row"))
    shifted, exp_done, both_done, counted = sem("shifted_e"), sem("exp_done_e"), sem("both_done"), sem("counted")
    own_e = sem("own_e")

    def over_experts(ap):
        return ap[:].unsqueeze(2).to_broadcast([P, NT, E])

    def over_tiles(ap):
        return ap[:].unsqueeze(1).to_broadcast([P, NT, E])

    with nc.Block() as block:

        @block.scalar
        def _(act):
            act.wait_ge(shifted, 1)
            act.activation(probs[:], probs[:], ACT.Exp).then_inc(exp_done, 1)

        @block.tensor
        def _(pe):
            pe.wait_ge(both_done, 1)
            pe.matmul(ps[:, 5, 0:NT * E], s.before_sb[:, 0, :], both[:].rearrange("p t e -> p (t e)"),
                      start=True, stop=True).then_inc(counted, 1)
            pe.matmul(ps[:, 6, 0:NT * E], s.before_sb[:, 1, :], both[:].rearrange("p t e -> p (t e)"),
                      start=True, stop=True).then_inc(counted, 1)

        @block.vector
        def _(dve):
            own = Own(dve, own_e, 0)

            def do(*instructions):
                for i in instructions:
                    own.step(i)
                own.settle()

            def tiles(bank):
                return ps[:, bank, 0:NT * E].rearrange("p (t e) -> p t e", e=E)

            do(dve.tensor_reduce(mx[:], tiles(4), AX.X, ALU.max))
            dve.tensor_tensor(probs[:], tiles(4), over_experts(mx), ALU.subtract).then_inc(shifted, 1)
            dve.wait_ge(exp_done, 1)
            do(dve.tensor_reduce(tot[:], probs[:], AX.X, ALU.add))
            do(dve.reciprocal(inv[:], tot[:]))
            do(dve.tensor_tensor(probs[:], probs[:], over_experts(inv), ALU.mult))
            do(*(dve.max(best[:, t, :], probs[:, t, :]) for t in range(NT)))
            do(*(dve.max_index(which[:, t, :], best[:, t, :], probs[:, t, :]) for t in range(NT)))
            do(dve.tensor_copy(whichf[:], which[:, :, 0:TOP]))
            do(*(dve.tensor_tensor(hot[k][:], over_tiles(s.experts_sb), over_experts(whichf[:, :, k]),
                                   ALU.is_equal) for k in range(TOP)))
            dve.tensor_tensor(both[:], hot[0][:], hot[1][:], ALU.add).then_inc(both_done, 1)
            do(dve.memset(earlier[:, 0, :], 0.0))
            dve.wait_ge(counted, 2)
            for t in range(1, NT):
                do(dve.tensor_tensor(earlier[:, t, :], tiles(6)[:, t - 1, :], earlier[:, t - 1, :], ALU.add))
            do(dve.tensor_tensor(place[:], tiles(5), earlier[:], ALU.add))
            for k in range(TOP):
                do(dve.tensor_tensor(tmp[0][:], hot[k][:], place[:], ALU.mult),
                   dve.tensor_tensor(tmp[1][:], hot[k][:], over_tiles(s.base_sb), ALU.mult))
                do(dve.tensor_reduce(at[k][:], tmp[0][:], AX.X, ALU.add),
                   dve.tensor_reduce(base[k][:], tmp[1][:], AX.X, ALU.add))
                do(dve.tensor_scalar(keep[k][:], at[k][:], float(CAP), None, ALU.is_lt))
                do(dve.tensor_tensor(s.gates[k][:], best[:, :, k], keep[k][:], ALU.mult),
                   dve.tensor_tensor(row[k][:], base[k][:], at[k][:], ALU.add),
                   dve.tensor_scalar(at[k][:], at[k][:], float(CAP - 1), None, ALU.min))
                do(dve.tensor_tensor(row[k][:], row[k][:], s.trash_sb[:, k, :], ALU.subtract),
                   dve.tensor_tensor(at[k][:], at[k][:], base[k][:], ALU.add))
                do(dve.tensor_tensor(row[k][:], row[k][:], keep[k][:], ALU.mult),
                   dve.tensor_copy(s.read_rows[k][:], at[k][:]))
                do(dve.tensor_tensor(row[k][:], row[k][:], s.trash_sb[:, k, :], ALU.add))
                do(dve.tensor_copy(s.write_rows[k][:], row[k][:]))


def run_experts(nc, sb, sem, s):
    ps = s.ps
    w1r = [sb(f"w1r{i}", [P, 2, FFN]) for i in range(2)]
    w2r = [sb(f"w2r{i}", [P, FFN // P, DIM]) for i in range(2)]
    xr = [sb(f"xr{i}", [P, len(EXPERT_TILES), DIM]) for i in range(2)]
    xt = [sb(f"xt{i}", [P, 2, CAP]) for i in range(2)]
    act_t = [sb(f"act_t{i}", [P, FFN // P, CAP]) for i in range(2)]
    y = [sb(f"y{i}", [P, len(EXPERT_TILES), DIM]) for i in range(2)]
    GOT = 6
    got = [[sb(f"got{k}{i}", [P, DIM]) for i in range(GOT)] for k in range(TOP)]
    F = FFN // P
    FULL = CAP // P * P
    LAST = len(EXPERT_TILES) - 1

    weights_in = [sem("weights_in0"), sem("weights_in1")]
    rows_in = [sem("rows_in0"), sem("rows_in1")]
    y_out = [sem("y_out0"), sem("y_out1")]
    zeroed, scattered = s.zeroed, sem("scattered")
    xt_ps, xt_done, up_ps, up_done, down_ps, y_done = (
        sem("xt_ps_f"), sem("xt_done_f"), sem("up_ps"), sem("up_done"), sem("down_ps"), sem("y_done_f"))
    gathered = [sem(f"gathered{i}") for i in range(GOT)]
    summed = sem("summed")
    weighed, out_done = sem("weighed"), sem("out_done")
    own_f = sem("own_f")
    ys_done = sem("ys_done")

    with nc.Block() as block:

        @block.sync
        def _(sp):
            def load_weights(e, par):
                sp.dma_start(w1r[par][:], s.w1[e].rearrange("(f p) n -> p f n", p=P)).then_inc(weights_in[par], 16)
                sp.dma_start(w2r[par][:], s.w2[e].rearrange("(f p) n -> p f n", p=P)).then_inc(weights_in[par], 16)

            def load_rows(e, par):
                full = s.slots_dram[0:E * CAP].rearrange("(e r) d -> e r d", e=E)[e]
                sp.dma_start(xr[par][:, 0:LAST, :], full[0:FULL].rearrange("(t p) d -> p t d", p=P)).then_inc(rows_in[par], 16)
                sp.dma_start(xr[par][0:CAP - FULL, LAST, :], full[FULL:CAP]).then_inc(rows_in[par], 16)

            def store(e, par):
                sp.wait_ge(y_done, LAST * e + e + LAST + 1)
                full = s.ffn_dram.rearrange("(e r) d -> e r d", e=E)[e]
                sp.dma_start(full[0:FULL].rearrange("(t p) d -> p t d", p=P), y[par][:, 0:LAST, :]).then_inc(y_out[par], 16)
                sp.dma_start(full[FULL:CAP], y[par][0:CAP - FULL, LAST, :]).then_inc(y_out[par], 16)

            for n in range(2):
                load_weights(n, n)
            sp.wait_ge(scattered, 16 * TOP * NT)
            sp.wait_ge(zeroed, 16 * s.N_ZERO)
            for n in range(2):
                load_rows(n, n)
            with sp.Fori(0, (E - 2) // 2) as i:
                for par in (0, 1):
                    e = 2 * i + par
                    sp.wait_ge(xt_ps, e + 1)
                    load_rows(e + 2, par)
                    store(e, par)
                    load_weights(e + 2, par)
            for e in (E - 2, E - 1):
                store(e, e % 2)
            for par in (0, 1):
                sp.wait_ge(y_out[par], 32 * E // 2)
            sp.sem_inc(ys_done, 1)
            for t in range(NT):
                sp.wait_ge(weighed, t + 1)
                sp.dma_start(s.out_rows[t], s.x1[:, t, :]).then_inc(out_done, 16)
            sp.wait_ge(out_done, 16 * NT)

        @block.gpsimd
        def _(pool):
            pool.wait_ge(zeroed, 16 * s.N_ZERO)
            for t in range(NT):
                for k in range(TOP):
                    pool.indirect_dma_start(
                        s.slots_dram, bass.IndirectOffsetOnAxis(ap=s.write_rows[k][:, t:t + 1], axis=0),
                        s.ln2[:, t, :], None).then_inc(scattered, 16)
            for t in range(NT):
                pool.tensor_tensor(s.x1[:, t, :], s.x1[:, t, :], s.hid[:, t, :], ALU.add).then_inc(summed, 1)
            pool.wait_ge(ys_done, 1)
            for t in range(NT):
                if t >= GOT:
                    pool.wait_ge(weighed, t - GOT + 1)
                for k in range(TOP):
                    pool.indirect_dma_start(
                        got[k][t % GOT][:], None, s.ffn_dram,
                        bass.IndirectOffsetOnAxis(ap=s.read_rows[k][:, t:t + 1], axis=0)
                    ).then_inc(gathered[t % GOT], 16)

        @block.tensor
        def _(pe):
            def transposes(e, par):
                pe.wait_ge(rows_in[par], 32 * (e // 2 + 1) if isinstance(e, int) else 16 * (e - par) + 32)
                wait(pe, xt_done, 2 * e)
                for f in range(2):
                    for n, (at, m) in enumerate(EXPERT_TILES):
                        i = pe.transpose(ps[:, f, at:at + m], xr[par][0:m, n, f * P:(f + 1) * P],
                                         s.id32[0:m, 0:m])
                i.then_inc(xt_ps, 1)

            def up(e, par):
                pe.wait_ge(weights_in[par], 32 * (e // 2 + 1) if isinstance(e, int) else 16 * (e - par) + 32)
                pe.wait_ge(xt_done, 2 * e + 2)
                for j in range(F):
                    if not (isinstance(e, int) and e == 0 and j < 2):
                        pe.wait_ge(up_done, F * e + j - 1)
                    for f in range(2):
                        i = pe.matmul(ps[:, 2 + j % 2, 0:CAP], w1r[par][:, f, j * P:(j + 1) * P],
                                      xt[par][:, f, :], start=f == 0, stop=f == 1)
                    i.then_inc(up_ps, 1)

            def down(e, par):
                pe.wait_ge(up_done, F * e + F)
                for n, (at, m) in enumerate(EXPERT_TILES):
                    wait(pe, y_done, len(EXPERT_TILES) * (e - 1) + n + 1)
                    for j in range(F):
                        i = pe.matmul(ps[0:m, 4 + n, 0:DIM], act_t[par][:, j, at:at + m], w2r[par][:, j, :],
                                      start=j == 0, stop=j == F - 1)
                    i.then_inc(down_ps, 1)

            transposes(0, 0)

            def expert(e, par, last=False):
                up(e, par)
                if not last:
                    transposes(e + 1, 1 - par)
                down(e, par)

            expert(0, 0)
            expert(1, 1)
            with pe.Fori(1, E // 2 - 1) as i:
                for par in (0, 1):
                    expert(2 * i + par, par)
            expert(E - 2, 0)
            expert(E - 1, 1, last=True)

        @block.scalar
        def _(act):
            def gelu(e, par):
                for j in range(F):
                    act.wait_ge(up_ps, F * e + j + 1)
                    act.activation(act_t[par][:, j, :], ps[:, 2 + j % 2, 0:CAP],
                                   ACT.Gelu_apprx_tanh).then_inc(up_done, 1)

            with act.Fori(0, E // 2) as i:
                for par in (0, 1):
                    gelu(2 * i + par, par)

        @block.vector
        def _(dve):
            def copy_xt(e, par):
                dve.wait_ge(xt_ps, e + 1)
                for f in range(2):
                    dve.tensor_copy(xt[par][:, f, :], ps[:, f, 0:CAP]).then_inc(xt_done, 1)

            def copy_y(e, par):
                wait(dve, y_out[par], 32 * (e // 2) if isinstance(e, int) else 16 * (e - par))
                for n, (at, m) in enumerate(EXPERT_TILES):
                    dve.wait_ge(down_ps, len(EXPERT_TILES) * e + n + 1)
                    dve.tensor_copy(y[par][0:m, n, :], ps[0:m, 4 + n, 0:DIM]).then_inc(y_done, 1)

            def expert(e, par, last=False):
                if not last:
                    copy_xt(e + 1, 1 - par)
                copy_y(e, par)

            copy_xt(0, 0)
            expert(0, 0)
            expert(1, 1)
            with dve.Fori(1, E // 2 - 1) as i:
                for par in (0, 1):
                    expert(2 * i + par, par)
            expert(E - 2, 0)
            expert(E - 1, 1, last=True)
            own = Own(dve, own_f, 0)
            dve.wait_ge(summed, NT)
            for t in range(NT):
                dve.wait_ge(gathered[t % GOT], 16 * TOP * (t // GOT + 1))
                own.step(dve.scalar_tensor_tensor(s.x1[:, t, :], got[0][t % GOT][:], s.gates[0][:, t:t + 1],
                                                  s.x1[:, t, :], ALU.mult, ALU.add))
                own.settle()
                dve.scalar_tensor_tensor(s.x1[:, t, :], got[1][t % GOT][:], s.gates[1][:, t:t + 1],
                                         s.x1[:, t, :], ALU.mult, ALU.add).then_inc(weighed, 1)


def bass_xattn_moe(nc, x, ctx_t, wq, wk, wv, gate, ln_g, ln_b, wp, bp, ln1_w, ln1_b, ln2_w, ln2_b,
                   wqkv, wproj, wrouter, w1, w2, ident, before, ctx0_row, experts, expert_base,
                   trash_rows, stack_rows, out):
    with ExitStack() as whole:
        s = Shared()

        def allocator(stack):
            def sb(name, shape, dt=F32):
                return stack.enter_context(nc.sbuf_tensor(name, shape, dt))
            return sb

        def sem(name):
            return whole.enter_context(nc.semaphore(name))

        sb = allocator(whole)
        s.ps = whole.enter_context(nc.psum_tensor("ps", [P, 8, 512], F32))
        s.slots_dram = nc.dram_tensor("expert_slots", (TRASH + TOP * NT * P, DIM), F32).ap()
        s.ffn_dram = nc.dram_tensor("expert_results", (E * CAP, DIM), F32).ap()
        s.w1, s.w2 = w1, w2
        s.out_rows = out.rearrange("b (h p) d -> (b h) p d", p=P)

        s.x1 = sb("x1", [P, NT, DIM])
        s.hid = sb("hid", [P, NT, DIM])
        s.id32 = sb("id32", [P, P])
        s.minus_half = sb("minus_half", [P, NT])
        s.wproj_sb = sb("wproj_sb", [P, 2, DIM])
        s.wr_sb = sb("wr_sb", [P, 2, E])
        s.w2n_sb, s.b2n_sb = sb("w2n_sb", [P, DIM]), sb("b2n_sb", [P, DIM])
        s.before_sb = sb("before_sb", [P, 2, P])
        s.experts_sb, s.base_sb = sb("experts_sb", [P, E]), sb("base_sb", [P, E])
        s.trash_sb = sb("trash_sb", [P, TOP, NT])
        s.gates = [sb(f"gates{k}", [P, NT]) for k in range(TOP)]
        s.read_rows = [sb(f"read_rows{k}", [P, NT], U32) for k in range(TOP)]
        s.write_rows = [sb(f"write_rows{k}", [P, NT], U32) for k in range(TOP)]

        s.const_in, s.late_in = sem("const_in"), sem("late_in")
        s.x_in = [sem(f"x_in{i}") for i in range(2)]
        s.first_in = sem("first_in")
        s.id16_done, s.tgate_done = sem("id16_done"), sem("tgate_done")
        x_tiles = x.rearrange("b (h p) d -> p (b h) d", p=P)

        s.qkv = sb("qkv", [P, NT, QKV])
        with ExitStack() as first:
            sb = allocator(first)
            s.zeros = sb("zeros", [P, 4 * DIM])
            s.id16 = sb("id16", [P, P], F16)
            s.wq_sb, s.wk_sb, s.wv_sb, s.wp_sb = (
                sb(n, [P, 2, DIM]) for n in ("wq_sb", "wk_sb", "wv_sb", "wp_sb"))
            s.wqkv_sb = sb("wqkv_sb", [P, 2, QKV])
            s.g_sb, s.b_sb, s.g1_sb, s.b1_sb = (sb(n, [P, 2]) for n in ("g_sb", "b_sb", "g1_sb", "b1_sb"))
            s.bp_sb = sb("bp_sb", [P, DIM])
            s.gate_sb, s.tgate = sb("gate_sb", [P, H]), sb("tgate", [P, H])
            s.ctx0_sb = sb("ctx0_sb", [CTX, P])
            s.ctx_sb = sb("ctx_sb", [P, B, 2, CTX])
            first_ones = [(s.id32, ident), (s.wq_sb, wq), (s.ctx_sb, ctx_t)]
            early = [(s.wk_sb, wk), (s.wv_sb, wv),
                     (s.bp_sb, bp.partition_broadcast(P)), (s.gate_sb, gate.partition_broadcast(P)),
                     (s.ctx0_sb, ctx0_row), (s.wp_sb, wp), (s.wqkv_sb, wqkv), (s.g_sb, ln_g),
                     (s.b_sb, ln_b), (s.g1_sb, ln1_w), (s.b1_sb, ln1_b)]
            late = [(s.wproj_sb, wproj), (s.wr_sb, wrouter), (s.w2n_sb, ln2_w.partition_broadcast(P)),
                    (s.b2n_sb, ln2_b.partition_broadcast(P)), (s.before_sb, before),
                    (s.experts_sb, experts.partition_broadcast(P)),
                    (s.base_sb, expert_base.partition_broadcast(P)), (s.trash_sb, trash_rows)]
            s.N_FIRST, s.N_CONST = 16 * len(first_ones), 16 * (len(early) + 4)
            s.late_count = 16 * len(late)
            s.zeroed = sem("zeroed")
            s.N_ZERO = E * CAP // (4 * P)

            def load_constants(sp):
                sp.dma_start(s.x1[:, 0:2, :], x_tiles[:, 0:2, :]).then_inc(s.x_in[0], 16)
                for dst, src in first_ones:
                    sp.dma_start(dst[:], src).then_inc(s.first_in, 16)
                sp.dma_start(s.x1[:, 2:NT, :], x_tiles[:, 2:NT, :]).then_inc(s.x_in[1], 16)
                for dst, src in early:
                    sp.dma_start(dst[:], src).then_inc(s.const_in, 16)
                for qs, ks in s.stacks:
                    sp.dma_start(qs[STACK:STACK + 1], stack_rows[0:1, :, 0:N]).then_inc(s.const_in, 16)
                    sp.dma_start(ks[STACK:ROWS], stack_rows[1:3]).then_inc(s.const_in, 16)
                for dst, src in late:
                    sp.dma_start(dst[:], src).then_inc(s.late_in, 16)

            def clear_slots(sp):
                view = s.slots_dram[0:E * CAP].rearrange("(n p r) d -> n p (r d)", p=P, r=4)
                for n in range(s.N_ZERO):
                    sp.dma_start(view[n], s.zeros[:]).then_inc(s.zeroed, 16)
                sp.wait_ge(s.zeroed, 16 * s.N_ZERO)
                sp.wait_ge(s.late_in, s.late_count)
            s.load_constants, s.clear_slots = load_constants, clear_slots
            cross_attention(nc, sb, sem, s)
        s.ln2 = whole.enter_context(nc.sbuf_tensor("ln2", [P, NT, DIM], F32))
        with ExitStack() as second:
            second_attention(nc, allocator(second), sem, s)
        with ExitStack() as routing:
            route(nc, allocator(routing), sem, s)
        with ExitStack() as last:
            run_experts(nc, allocator(last), sem, s)


_INS = ("x", "ctx_t", "wq", "wk", "wv", "gate", "ln_g", "ln_b", "wp", "bp", "ln1_w", "ln1_b", "ln2_w", "ln2_b",
        "wqkv", "wproj", "wrouter", "w1", "w2", "ident", "before", "ctx0_row", "experts", "expert_base",
        "trash_rows", "stack_rows")


def kernel(**inputs):
    import concourse.bacc as bacc
    from concourse.bass_utils import run_bass_kernel_spmd

    a = {k: np.asarray(v) for k, v in inputs.items()}

    def chunks(w):
        return w.reshape(2, P, -1).transpose(1, 0, 2)

    def by_head_dim(w):
        return w.reshape(DIM, 2, GROUP, HD).transpose(0, 1, 3, 2).reshape(DIM, DIM)

    def column(v):
        return v.reshape(2, P).T

    ctx = np.concatenate([a["ctx_1024"][:, 1:], a["ctx_1024"][:, :1]], axis=1)
    ctx0_row = np.zeros((CTX, P), np.float32)
    ctx0_row[CTX - 1] = 1.0
    before = np.stack([np.triu(np.ones((P, P), np.float32), 1), np.ones((P, P), np.float32)], axis=1)
    trash = (TRASH + np.arange(TOP * NT * P, dtype=np.float32).reshape(TOP, NT, P)).transpose(2, 0, 1)
    arrays = {
        "x": a["x"],
        "ctx_t": ctx.reshape(B, CTX, 2, P).transpose(3, 0, 2, 1),
        "wq": chunks(by_head_dim(a["L0_xattn_Wq"].T)),
        "wk": chunks(by_head_dim(a["L0_xattn_Wk"].T)),
        "wv": chunks(a["L0_xattn_Wv"].T),
        "gate": a["L0_xattn_gate"].reshape(H),
        "ln_g": column(a["L0_xattn_ln_g"]),
        "ln_b": column(a["L0_xattn_ln_b"]),
        "wp": chunks(a["L0_xattn_Wp"].T),
        "bp": a["L0_xattn_bp"],
        "ln1_w": column(a["L0_ffn_ln1_weight"]),
        "ln1_b": column(a["L0_ffn_ln1_bias"]),
        "ln2_w": a["L0_ffn_ln2_weight"],
        "ln2_b": a["L0_ffn_ln2_bias"],
        "wqkv": chunks(a["L0_ffn_qkv_weight"].T),
        "wproj": chunks(a["L0_ffn_proj_weight"].T),
        "wrouter": chunks(a["L0_ffn_router_weight"].T),
        "w1": a["L0_ffn_moe_w1"].transpose(0, 2, 1),
        "w2": a["L0_ffn_moe_w2"].transpose(0, 2, 1),
        "ident": np.eye(P, dtype=np.float32),
        "before": before,
        "ctx0_row": ctx0_row,
        "experts": np.arange(E, dtype=np.float32),
        "expert_base": np.arange(E, dtype=np.float32) * CAP,
        "trash_rows": trash,
        "stack_rows": np.repeat(np.array([0, 1, 1], np.float16), H * KEYS).reshape(3, H, KEYS),
    }
    nc = bacc.Bacc("TRN2", target_bir_lowering=False, num_devices=1)
    feeds, args = {}, []
    for name in _INS:
        array = np.ascontiguousarray(arrays[name])
        feeds[f"in_{name}"] = array
        args.append(nc.dram_tensor(f"in_{name}", array.shape, mybir.dt.from_np(array.dtype),
                                   kind="ExternalInput").ap())
    args.append(nc.dram_tensor("out", (B, N, DIM), F32, kind="ExternalOutput").ap())
    bass_xattn_moe(nc, *args)
    r = run_bass_kernel_spmd(nc, [feeds], core_ids=[0])
    return r.results[0]["out"]
```

```python
from contextlib import ExitStack

import numpy as np

import concourse.bass as bass
import concourse.mybir as mybir

F32 = mybir.dt.float32
F16 = mybir.dt.float16
BF16 = mybir.dt.bfloat16
U32 = mybir.dt.uint32
ALU = mybir.AluOpType
ACT = mybir.ActivationFunctionType
AX = mybir.AxisListType

P = 128
B, N, DIM = 8, 256, 256
HALVES = N // P
CTX = 77
H, HD = 16, 16
KV_H = 4
REP = H // KV_H
SOFT = N + CTX - 1
CTX_SOFT = CTX - 1
KEYS = N + CTX
NT = B * N // P
E, TOP, FFN = 16, 2, 512
CAP = -(-B * N * TOP * 5 // (E * 4))
TRASH = E * CAP
EPS = 1e-5
SCALE = HD ** -0.5
QKV = (H + 2 * KV_H) * HD
PAIRS = H // 2
GROUP = 8
PARTS = 4
STACK = PARTS * HD
ROWS = STACK + 2
VW = HD + 1
UNITS = PAIRS * HALVES
OWN_UNITS = {0: range(10, 12), 1: range(12, 14), 2: range(14, 16)}
NEXT_UNITS = {4: range(0, 2), 5: range(2, 5), 6: range(5, 8), 7: range(8, 10)}
MASKED = -1e30
EXPERT_TILES = [(s, min(P, CAP - s)) for s in range(0, CAP, P)]


class Shared:
    pass


def wait(eng, semaphore, value):
    if not isinstance(value, int) or value > 0:
        eng.wait_ge(semaphore, value)


def hold(eng, held, semaphore, value):
    eng.wait_ge(semaphore, value)
    eng.sem_inc(held, 1)


class Own:

    def __init__(self, eng, semaphore, base):
        self.eng, self.semaphore, self.base, self.n = eng, semaphore, base, 0

    def step(self, instruction):
        instruction.then_inc(self.semaphore, 1)
        self.n += 1

    def settle(self):
        self.eng.wait_ge(self.semaphore, self.base + self.n)


def rounds_beside(b, p):
    if b is not None:
        return (p,)
    return {1: (8, 9, 10), 5: (11, 12, 13)}.get(p, ())


def heads(ap):
    return ap.rearrange("p (h d) -> p h d", d=HD)


def cross_attention(nc, sb, sem, s):
    ps = s.ps
    xn = sb("xn", [P, HALVES, DIM])
    xct = sb("xct", [P, 2, KEYS])
    qh, ql = (sb(n, [P, 2, N], F16) for n in ("qh", "ql"))
    kh, kl = (sb(n, [P, 2, KEYS], F16) for n in ("kh", "kl"))
    qs = [sb(f"qs{i}", [ROWS, H, N], F16) for i in range(2)]
    ks = [sb(f"ks{i}", [ROWS, H, KEYS], F16) for i in range(2)]
    vh = [sb(f"vh{i}", [P, 3, H, VW], F16) for i in range(2)]
    vl = [sb(f"vl{i}", [P, 3, H, VW], F16) for i in range(2)]
    v0f = sb("v0f", [CTX, DIM])
    tv0 = [sb(f"tv0{i}", [P, DIM]) for i in range(2)]
    nmx = sb("nmx", [P, HALVES, H], F16)
    mrow = [sb(f"mrow{i}", [GROUP, N], F16) for i in range(2)]
    pf = [sb(f"pf{i}", [P, 3, 512]) for i in range(2)]
    ph = [sb(f"ph{i}", [P, 3, 512], F16) for i in range(2)]
    pl = [sb(f"pl{i}", [P, 3, 512], F16) for i in range(2)]
    rs = sb("rs", [P, HALVES, H])
    o32 = sb("o32", [P, HALVES, DIM])
    ob = sb("ob", [P, HALVES, DIM], BF16)
    z = o32
    zt = sb("zt", [P, 2, N])
    bn_a, bn_c = sb("bn_a", [P, NT, 6]), sb("bn_c", [P, HALVES, 6])
    mv_a, mv_c = sb("mv_a", [P, NT, 2]), sb("mv_c", [P, HALVES, 2])
    ve_a, ve_c = sb("ve_a", [P, NT]), sb("ve_c", [P, HALVES])
    rstd_a, rstd_c = sb("rstd_a", [P, NT, 1]), sb("rstd_c", [P, HALVES])

    init_done = sem("init_done")
    var_a, rstd_a_done, xn_done, bias_added = sem("var_a"), sem("rstd_a_done"), sem("xn_done"), sem("bias_added")
    xt_ps, xct_done = sem("xt_ps"), sem("xct_done")
    q_ps, k_ps, v_ps, v0_ps = sem("q_ps"), sem("k_ps"), sem("v_ps"), sem("v0_ps")
    q_hi, k_hi, v_hi, v0_done = sem("q_hi"), sem("k_hi"), sem("v_hi"), sem("v0_done")
    q_lo, k_lo, v_lo, tv0_done = sem("q_lo"), sem("k_lo"), sem("v_lo"), sem("tv0_done")
    stacked = sem("stacked")
    max_ps, max_done = sem("max_ps"), sem("max_done")
    mrow_ps, mrow_done = sem("mrow_ps"), sem("mrow_done")
    mrow_in = [sem("mrow_in0"), sem("mrow_in1")]
    scores, p_hi, p_lo, pool_lo, pv = (
        sem("scores"), sem("p_hi"), sem("p_lo"), sem("pool_lo"), sem("pv"))
    pv_read, var_c, rstd_c_done = sem("pv_read"), sem("var_c"), sem("rstd_c_done")
    z_done, zt_ps, zt_done = sem("z_done"), sem("zt_ps"), sem("zt_done")
    wp_ps, wp_read, y_done, yt_ps, yt_done = sem("wp_ps"), sem("wp_read"), sem("y_done"), sem("yt_ps"), sem("yt_done")
    qkv_ps, qkv_done = sem("qkv_ps"), s.qkv_done
    own_a, own_c, held_dve = sem("own_a"), sem("own_c"), sem("held_dve")
    STACK_DMAS = 2 * PARTS * 2

    with nc.Block() as block:

        @block.sync
        def _(sp):
            s.stacks = list(zip(qs, ks))
            s.load_constants(sp)

            def stack(dst, src, g, rows):
                for r in rows:
                    sp.dma_start(dst[r * HD:(r + 1) * HD, g * GROUP:(g + 1) * GROUP, :],
                                 src[:, g, :]).then_inc(stacked, 16)

            def put_maxima(b, par, g):
                sp.wait_ge(mrow_done, 2 * b + g + 1)
                sp.dma_start(qs[par][STACK + 1:STACK + 2, g * GROUP:(g + 1) * GROUP, :],
                             mrow[g][:, :]).then_inc(mrow_in[g], 16)

            def iteration(b, a, par):
                odd = 1 - par
                if a is not None:
                    for g in range(2):
                        sp.wait_ge(q_hi, a + 1)
                        stack(qs[odd], qh, g, (0, 1))
                    for g in range(2):
                        sp.wait_ge(q_lo, a + 1)
                        stack(qs[odd], ql, g, (2, 3))
                    sp.wait_ge(k_hi, 2 * a + 1)
                    stack(ks[odd], kh, 0, (0, 2))
                    sp.wait_ge(k_lo, 2 * a + 1)
                    stack(ks[odd], kl, 0, (1, 3))
                    sp.wait_ge(k_hi, 2 * a + 2)
                    stack(ks[odd], kh, 1, (0, 2))
                    sp.wait_ge(k_lo, 2 * a + 2)
                if b is not None:
                    put_maxima(b, par, 1)
                if a is not None:
                    stack(ks[odd], kl, 1, (1, 3))
                    put_maxima(a, odd, 0)

            iteration(None, 0, 1)
            iteration(0, 1, 0)
            sp.wait_ge(init_done, 1)
            s.clear_slots(sp)
            with sp.Fori(0, (B - 2) // 2) as i:
                for odd in (0, 1):
                    n = 2 * i + 1 + odd
                    iteration(n, n + 1, 1 - odd)
            iteration(B - 1, None, 1)
            sp.wait_ge(s.late_in, s.late_count)

        @block.gpsimd
        def _(pool):
            def init():
                for t in (0, 1):
                    pool.memset(vh[t][:], 1.0)
                    pool.memset(vl[t][:], 0.0)
                pool.memset(s.zeros, 0.0)
                pool.memset(s.minus_half[:], -0.5).then_inc(init_done, 1)
                pool.wait_ge(init_done, 1)
                for half in range(HALVES):
                    for q in range(B - 1):
                        i = pool.memset(s.sc[half][:, q, q + 1:B, :], MASKED)
                    i.then_inc(s.masked, 1)

            def power(c, k):
                pool.wait_ge(var_c, 3 * c + k + 1)
                pool.tensor_tensor(rstd_c[:], ve_c[:], s.minus_half[:, 0:HALVES], ALU.pow).then_inc(rstd_c_done, 1)

            def power_x(first, last, k):
                pool.wait_ge(var_a, k)
                pool.tensor_tensor(rstd_a[:, first:last, 0], ve_a[:, first:last], s.minus_half[:, first:last],
                                   ALU.pow).then_inc(rstd_a_done, 1)

            def add_bias(b):
                pool.wait_ge(xn_done, b + 1)
                for t in range(HALVES):
                    i = pool.tensor_tensor(s.x1[:, HALVES * b + t, :], s.x1[:, HALVES * b + t, :],
                                           s.bp_sb[:], ALU.add)
                i.then_inc(bias_added, 1)

            def lo(b, p):
                t = PAIRS * b + p
                pool.wait_ge(p_hi, 3 * t + 2)
                pool.tensor_tensor(pl[p % 2][:, 1, :], pf[p % 2][:, 1, :], ph[p % 2][:, 1, :], ALU.subtract)
                pool.wait_ge(p_hi, 3 * t + 3)
                pool.tensor_tensor(pl[p % 2][0:CTX_SOFT, 2, :], pf[p % 2][0:CTX_SOFT, 2, :],
                                   ph[p % 2][0:CTX_SOFT, 2, :], ALU.subtract).then_inc(pool_lo, 1)

            def iteration(b, a, c):
                for p in range(PAIRS):
                    if b is not None:
                        lo(b, p)
                    if c is not None and p in (1, 3, 5):
                        power(c, {1: 0, 3: 1, 5: 2}[p])
                    if p == 1 and a is not None:
                        add_bias(a)
                    if a is None and b is not None and p == 0:
                        pool.wait_ge(s.zeroed, 16 * s.N_ZERO)
                    for n in (rounds_beside(b, p) if a is None else ()):
                        s.pool_products(pool, n)

            init()
            power_x(0, HALVES, 1)
            power_x(HALVES, NT, 2)
            pool.wait_ge(s.const_in, s.N_CONST)
            iteration(None, 0, None)
            iteration(0, 1, None)
            with pool.Fori(0, (B - 2) // 2) as i:
                for odd in (0, 1):
                    n = 2 * i + 1 + odd
                    iteration(n, n + 1, n - 1)
            iteration(B - 1, None, B - 2)
            iteration(None, None, B - 1)

        @block.tensor
        def _(pe):
            def transposes(src, bank):
                for f in range(2):
                    for t in range(HALVES):
                        i = pe.transpose(ps[:, bank, f * N + t * P:f * N + (t + 1) * P],
                                         src[:, t, f * P:(f + 1) * P], s.id32[:])
                return i

            def x_t(a, c):
                pe.wait_ge(xn_done, a + 1)
                if c is not None:
                    pe.wait_ge(qkv_done, 2 * c + 1)
                else:
                    wait(pe, tv0_done, a)
                transposes(xn, 7).then_inc(xt_ps, 1)

            def project_q(a):
                pe.wait_ge(xct_done, 2 * a + 2)
                for g in range(2):
                    for f in range(2):
                        i = pe.matmul(ps[:, 7, g * N:(g + 1) * N], s.wq_sb[:, f, g * P:(g + 1) * P],
                                      xct[:, f, 0:N], start=f == 0, stop=f == 1)
                i.then_inc(q_ps, 1)

            def project_k(a, g):
                if g == 0:
                    pe.wait_ge(q_lo, a + 1)
                else:
                    pe.wait_ge(k_lo, 2 * a + 1)
                for f in range(2):
                    i = pe.matmul(ps[:, 7, 0:KEYS], s.wk_sb[:, f, g * P:(g + 1) * P],
                                  xct[:, f, :], start=f == 0, stop=f == 1)
                i.then_inc(k_ps, 1)

            def project_v(a, c):
                if c is not None:
                    pe.wait_ge(wp_read, c + 1)
                else:
                    pe.wait_ge(k_lo, 2 * a + 2)
                for n in range(2):
                    for f in range(2):
                        i = pe.matmul(ps[:, 7, n * DIM:(n + 1) * DIM], xct[:, f, n * P:(n + 1) * P],
                                      s.wv_sb[:, f, :], start=f == 0, stop=f == 1)
                i.then_inc(v_ps, 1)

            def project_ctx_v(a):
                pe.wait_ge(v_lo, 2 * a + 1)
                for f in range(2):
                    i = pe.matmul(ps[0:CTX, 7, 0:DIM], xct[:, f, N:KEYS], s.wv_sb[:, f, :],
                                  start=f == 0, stop=f == 1)
                i.then_inc(v_ps, 1)

            def spread_v0(a):
                pe.wait_ge(v0_done, a + 1)
                pe.wait_ge(v_lo, 2 * a + 2)
                pe.matmul(ps[:, 7, 0:DIM], s.ctx0_sb[:], v0f[:], start=True, stop=True).then_inc(v0_ps, 1)

            def max_unit(a, par, u):
                p, t = u // HALVES, u % HALVES
                if u == 0:
                    pe.wait_ge(stacked, 16 * STACK_DMAS * (a + 1))
                    wait(pe, mrow_done, 2 * a)
                else:
                    pe.wait_ge(max_done, UNITS * a + u)
                if u == UNITS // 2:
                    pe.wait_ge(mrow_done, 2 * a + 1)
                for e in range(2):
                    i = pe.matmul(ps[:, 3 + e, 0:SOFT], qs[par][0:STACK + 1, 2 * p + e, t * P:(t + 1) * P],
                                  ks[par][0:STACK + 1, 2 * p + e, 0:SOFT], start=True, stop=True)
                i.then_inc(max_ps, 1)

            def max_rows(a, g):
                pe.wait_ge(max_done, UNITS * a + (g + 1) * UNITS // 2)
                rows = ps[0:GROUP, 3, 0:P].bitcast(F16)
                for t in range(HALVES):
                    i = pe.transpose(rows[:, t * P:(t + 1) * P], nmx[:, t, g * GROUP:(g + 1) * GROUP],
                                     s.id16[:])
                i.then_inc(mrow_ps, 1)

            def score(b, par, p, e):
                t = PAIRS * b + p
                if e == 0 and p % 4 == 0:
                    pe.wait_ge(mrow_in[p // 4], 16 * (b + 1))
                h = 2 * p + e
                if not (isinstance(b, int) and t == 0):
                    pe.wait_ge(p_hi, 3 * t - 2 + e)
                for c in range(2):
                    i = pe.matmul(ps[:, e, c * N:(c + 1) * N], ks[par][:, h, c * P:(c + 1) * P],
                                  qs[par][:, h, :], start=True, stop=True)
                i.then_inc(scores, 1)

            def score_ctx(b, par, p):
                t = PAIRS * b + p
                if not (isinstance(b, int) and t == 0):
                    pe.wait_ge(p_hi, 3 * t)
                for e in range(2):
                    i = pe.matmul(ps[0:CTX_SOFT, 2, e * N:(e + 1) * N], ks[par][:, 2 * p + e, 2 * P:SOFT],
                                  qs[par][:, 2 * p + e, :], start=True, stop=True)
                i.then_inc(scores, 1)

            def values(b, par, p, e):
                t = PAIRS * b + p
                if e == 0:
                    pe.wait_ge(p_lo, t + 1)
                    pe.wait_ge(pool_lo, t + 1)
                    if p == 0:
                        wait(pe, pv_read, b)
                h = 2 * p + e
                for q in range(HALVES):
                    n = 0
                    for left, right in ((ph, vh), (ph, vl), (pl, vh)):
                        for c in range(3):
                            k = P if c < 2 else CTX_SOFT
                            slab, at = (e, c * N) if c < 2 else (2, e * N)
                            i = pe.matmul(ps[:, 5 + q, h * VW:(h + 1) * VW],
                                          left[p % 2][0:k, slab, at + q * P:at + (q + 1) * P],
                                          right[par][0:k, c, h, :], start=n == 0, stop=n == 8)
                            n += 1
                if e == 1:
                    i.then_inc(pv, 1)

            def z_t(c, a):
                pe.wait_ge(z_done, c + 1)
                if a is not None:
                    pe.wait_ge(k_lo, 2 * a + 2)
                else:
                    pe.wait_ge(qkv_done, 2 * c + 1)
                transposes(z, 7).then_inc(zt_ps, 1)

            def project_out(c):
                pe.wait_ge(zt_done, 2 * c + 2)
                for t in range(HALVES):
                    for f in range(2):
                        i = pe.matmul(ps[:, 7, t * DIM:(t + 1) * DIM], zt[:, f, t * P:(t + 1) * P],
                                      s.wp_sb[:, f, :], start=f == 0, stop=f == 1)
                i.then_inc(wp_ps, 1)

            def y_t(c, a):
                pe.wait_ge(y_done, c + 1)
                if a is not None:
                    pe.wait_ge(tv0_done, a + 1)
                transposes(z, 7).then_inc(yt_ps, 1)

            def project_qkv(c, t):
                if t == 0:
                    pe.wait_ge(yt_done, 2 * c + 2)
                else:
                    pe.wait_ge(qkv_done, 2 * c + 2)
                for f in range(2):
                    i = pe.matmul(ps[:, 7, 0:QKV], zt[:, f, t * P:(t + 1) * P], s.wqkv_sb[:, f, :],
                                  start=f == 0, stop=f == 1)
                i.then_inc(qkv_ps, 1)

            def iteration(b, a, c, par):
                odd = 1 - par
                for p in range(PAIRS):
                    units = []
                    if b is not None and p in OWN_UNITS:
                        units = [(b, par, u) for u in OWN_UNITS[p]]
                    if a is not None and p in NEXT_UNITS:
                        units = [(a, odd, u) for u in NEXT_UNITS[p]]

                    def unit():
                        if units:
                            max_unit(*units.pop(0))

                    def value(e):
                        if p == 0 and c is not None:
                            values(c, odd, PAIRS - 1, e)
                        elif p > 0 and b is not None:
                            values(b, par, p - 1, e)

                    if b is not None:
                        score(b, par, p, 0)
                        score(b, par, p, 1)
                        score_ctx(b, par, p)
                    if p == 3 and b is not None:
                        max_rows(b, 1)
                    if p == 7 and a is not None:
                        max_rows(a, 0)
                    if p == 2 and a is not None:
                        project_k(a, 1)
                    if p != 7:
                        unit()
                    if a is not None:
                        if p == 0:
                            x_t(a, c)
                        if p == 4:
                            project_v(a, c)
                        if p == 5:
                            project_ctx_v(a)
                    if p == 6 and c is not None:
                        y_t(c, a)
                    value(0)
                    if p == 1 and a is not None:
                        if b is None:
                            pe.wait_ge(s.const_in, s.N_CONST)
                        project_k(a, 0)
                    if c is not None:
                        if p == 3:
                            project_out(c)
                        if p == 7:
                            project_qkv(c, 1)
                    unit()
                    value(1)
                    if p == 0 and a is not None:
                        project_q(a)
                    if p == 5 and a is not None:
                        spread_v0(a)
                    if p == 6 and c is not None:
                        project_qkv(c, 0)
                    unit()
                    if p == 2 and c is not None:
                        z_t(c, a)
                    assert not units

            pe.wait_ge(init_done, 1)
            pe.wait_ge(s.first_in, s.N_FIRST)
            pe.wait_ge(s.id16_done, 1)
            iteration(None, 0, None, 1)
            iteration(0, 1, None, 0)
            with pe.Fori(0, (B - 2) // 2) as i:
                for odd in (0, 1):
                    n = 2 * i + 1 + odd
                    iteration(n, n + 1, n - 1, 1 - odd)
            iteration(B - 1, None, B - 2, 1)
            iteration(None, None, B - 1, 0)

        @block.scalar
        def _(act):
            def copy(dst, src):
                return act.activation(dst, src, ACT.Copy)

            def x_t(a):
                copy(xct[:, :, N:KEYS], s.ctx_sb[:, a, :, :]).then_inc(xct_done, 1)
                act.wait_ge(xt_ps, a + 1)
                copy(xct[:, :, 0:N], ps[:, 7, :].rearrange("p (f n) -> p f n", f=2)).then_inc(xct_done, 1)

            def split_q(a):
                wait(act, stacked, 16 * STACK_DMAS * a)
                act.wait_ge(q_ps, a + 1)
                copy(qh[:], ps[:, 7, :].rearrange("p (g n) -> p g n", g=2)).then_inc(q_hi, 1)

            def split_k(a, g):
                act.wait_ge(k_ps, 2 * a + g + 1)
                copy(kh[:, g, :], ps[:, 7, 0:KEYS]).then_inc(k_hi, 1)

            def split_v(a, par):
                act.wait_ge(v_ps, 2 * a + 1)
                copy(vh[par][:, 0:2, :, 0:HD],
                     ps[:, 7, :].rearrange("p (c h d) -> p c h d", c=2, h=H)).then_inc(v_hi, 1)

            def split_ctx_v(a, par):
                act.wait_ge(v_ps, 2 * a + 2)
                copy(v0f[:], ps[0:CTX, 7, 0:DIM]).then_inc(v0_done, 1)
                copy(vh[par][0:CTX, 2, :, 0:HD], heads(ps[0:CTX, 7, 0:DIM])).then_inc(v_hi, 1)

            def max_rows(a, g):
                act.wait_ge(mrow_ps, 2 * a + g + 1)
                wait(act, mrow_in[g], 16 * a)
                copy(mrow[g][:], ps[0:GROUP, 3, 0:P].bitcast(F16)).then_inc(mrow_done, 1)

            def exponentials(b, p, parts):
                t = PAIRS * b + p
                if 0 in parts and not (isinstance(b, int) and t < 2):
                    act.wait_ge(p_lo, t - 1)
                    act.wait_ge(pool_lo, t - 1)
                    act.wait_ge(pv, t - 1)
                for e in parts:
                    k = P if e < 2 else CTX_SOFT
                    act.wait_ge(scores, 3 * t + e + 1)
                    act.activation(pf[p % 2][0:k, e, :], ps[0:k, e, :], ACT.Exp, scale=SCALE)
                    act.activation(ph[p % 2][0:k, e, :], ps[0:k, e, :], ACT.Exp, scale=SCALE).then_inc(p_hi, 1)

            def affine(dst, gain, bias, done):
                for f in range(2):
                    act.activation(dst[:, f, :], ps[:, 7, f * N:(f + 1) * N], ACT.Identity,
                                   bias=bias[:, f:f + 1], scale=gain[:, f:f + 1]).then_inc(done, 1)

            def open_gate():
                act.wait_ge(s.const_in, s.N_CONST)
                act.activation(s.tgate[:], s.gate_sb[:], ACT.Tanh).then_inc(s.tgate_done, 1)
                act.wait_ge(s.tgate_done, 1)
                copy(s.gate_sb[:], s.tgate[:]).then_inc(qkv_done, 1)

            def z_t(c):
                act.wait_ge(zt_ps, c + 1)
                affine(zt, s.g_sb, s.b_sb, zt_done)

            def y_t(c):
                act.wait_ge(yt_ps, c + 1)
                affine(zt, s.g1_sb, s.b1_sb, yt_done)

            def store_qkv(c, t):
                act.wait_ge(qkv_ps, 2 * c + t + 1)
                copy(s.qkv[:, HALVES * c + t, :], ps[:, 7, 0:QKV]).then_inc(qkv_done, 1)

            def iteration(b, a, c, par):
                odd = 1 - par
                for p in range(PAIRS):
                    if p == 1 and b is None and a is not None:
                        open_gate()
                    if p == 1 and a is not None:
                        split_q(a)
                    if c is not None:
                        if p == 3:
                            z_t(c)
                        if p == 7:
                            store_qkv(c, 0)
                    if b is not None:
                        exponentials(b, p, (0,))
                    if p == 3 and b is not None:
                        max_rows(b, 1)
                    if p == 7 and a is not None:
                        max_rows(a, 0)
                    if a is not None:
                        if p == 0:
                            x_t(a)
                        if p == 2:
                            split_k(a, 1)
                        if p == 4:
                            split_v(a, odd)
                        if p == 5:
                            split_ctx_v(a, odd)
                    if p == 6 and c is not None:
                        y_t(c)
                    if b is not None:
                        exponentials(b, p, (1, 2))
                    if p == 1 and a is not None:
                        split_k(a, 0)
                    if p == 7 and c is not None:
                        store_qkv(c, 1)

            act.wait_ge(s.first_in, s.N_FIRST)
            copy(s.id16[:], s.id32[:]).then_inc(s.id16_done, 1)
            act.wait_ge(init_done, 1)
            iteration(None, 0, None, 1)
            iteration(0, 1, None, 0)
            with act.Fori(0, (B - 2) // 2) as i:
                for odd in (0, 1):
                    n = 2 * i + 1 + odd
                    iteration(n, n + 1, n - 1, 1 - odd)
            iteration(B - 1, None, B - 2, 1)
            iteration(None, None, B - 1, 0)

        @block.vector
        def _(dve):
            C_STEPS = 15

            def moments(own, src, bn, mv, ve, ready):
                for t in range(HALVES):
                    own.step(dve.bn_stats(bn[:, t, :], src(t)))
                hold(dve, held_dve, own.semaphore, own.base + own.n)
                for t in range(HALVES):
                    own.step(dve.bn_aggr(mv[:, t, :], bn[:, t, :]))
                own.settle()
                dve.tensor_scalar(ve[:], mv[:, :, 1], EPS, None, ALU.add).then_inc(ready, 1)

            def center(dst, src, mv, rstd):
                for t in range(HALVES):
                    i = dve.tensor_scalar(dst(t), src(t), mv[:, t, 0:1], rstd[:, t:t + 1], ALU.subtract,
                                          ALU.mult)
                return i

            def rows(tensor, b):
                return lambda t: tensor[:, HALVES * b + t, :]

            def part(tensor):
                return lambda t: tensor[:, t, :]

            def norm_x(own, first, last):
                for t in range(first, last):
                    own.step(dve.bn_stats(bn_a[:, t, :], s.x1[:, t, :]))
                own.settle()
                for t in range(first, last):
                    own.step(dve.bn_aggr(mv_a[:, t, :], bn_a[:, t, :]))
                own.settle()
                dve.tensor_scalar(ve_a[:, first:last], mv_a[:, first:last, 1], EPS, None,
                                  ALU.add).then_inc(var_a, 1)

            def center_x(a):
                for t in range(HALVES):
                    n = HALVES * a + t
                    i = dve.tensor_scalar(xn[:, t, :], s.x1[:, n, :], mv_a[:, n, 0:1], rstd_a[:, n, :],
                                          ALU.subtract, ALU.mult)
                i.then_inc(xn_done, 1)

            def split_q(a):
                dve.wait_ge(q_hi, a + 1)
                dve.tensor_tensor(ql[:], ps[:, 7, :].rearrange("p (g n) -> p g n", g=2), qh[:],
                                  ALU.subtract).then_inc(q_lo, 1)

            def split_k(a, g):
                dve.wait_ge(k_hi, 2 * a + g + 1)
                dve.tensor_tensor(kl[:, g, :], ps[:, 7, 0:KEYS], kh[:, g, :],
                                  ALU.subtract).then_inc(k_lo, 1)

            def split_v(a, par):
                dve.wait_ge(v_hi, 2 * a + 1)
                dve.tensor_tensor(vl[par][:, 0:2, :, 0:HD],
                                  ps[:, 7, :].rearrange("p (c h d) -> p c h d", c=2, h=H),
                                  vh[par][:, 0:2, :, 0:HD], ALU.subtract).then_inc(v_lo, 1)

            def split_ctx_v(a, par):
                dve.wait_ge(v_hi, 2 * a + 2)
                dve.tensor_tensor(vl[par][0:CTX, 2, :, 0:HD], heads(ps[0:CTX, 7, 0:DIM]),
                                  vh[par][0:CTX, 2, :, 0:HD], ALU.subtract).then_inc(v_lo, 1)

            def gate_v0(a, par):
                dve.wait_ge(v0_ps, a + 1)
                dve.tensor_tensor(heads(tv0[par][:]), heads(ps[:, 7, 0:DIM]),
                                  s.tgate[:].unsqueeze(2).to_broadcast([P, H, HD]),
                                  ALU.mult).then_inc(tv0_done, 1)

            def max_unit(a, u):
                p, t = u // HALVES, u % HALVES
                dve.wait_ge(max_ps, UNITS * a + u + 1)
                dve.tensor_reduce(nmx[:, t, 2 * p:2 * p + 2], ps[:, 3:5, 0:SOFT], AX.X, ALU.max,
                                  negate=True).then_inc(max_done, 1)

            def lo(b, p):
                t = PAIRS * b + p
                dve.wait_ge(p_hi, 3 * t + 1)
                dve.tensor_tensor(pl[p % 2][:, 0, :], pf[p % 2][:, 0, :], ph[p % 2][:, 0, :],
                                  ALU.subtract).then_inc(p_lo, 1)

            def attended(own, c, par):
                dve.wait_ge(pv, PAIRS * c + PAIRS)
                out = ps[:, 5:7, 0:H * VW].rearrange("p q (h w) -> p q h w", w=VW)
                own.step(dve.reciprocal(rs[:], out[:, :, :, HD]))
                own.settle()
                for t in range(HALVES):
                    i = dve.tensor_tensor(heads(o32[:, t, :]), out[:, t, :, 0:HD],
                                          rs[:, t, :].unsqueeze(2).to_broadcast([P, H, HD]), ALU.mult)
                i.then_inc(pv_read, 1)
                dve.wait_ge(pv_read, c + 1)
                own.step(dve.tensor_tensor(ob[:], o32[:], tv0[par][:].unsqueeze(1).to_broadcast(
                    [P, HALVES, DIM]), ALU.add))
                own.settle()
                moments(own, part(ob), bn_c, mv_c, ve_c, var_c)

            def center_attended(c):
                dve.wait_ge(rstd_c_done, 3 * c + 1)
                center(part(z), part(ob), mv_c, rstd_c).then_inc(z_done, 1)

            def residual(own, c):
                dve.wait_ge(wp_ps, c + 1)
                dve.wait_ge(bias_added, c + 1)
                for t in range(HALVES):
                    i = dve.tensor_tensor(s.x1[:, HALVES * c + t, :], ps[:, 7, t * DIM:(t + 1) * DIM],
                                          s.x1[:, HALVES * c + t, :], ALU.add)
                i.then_inc(wp_read, 1)
                hold(dve, held_dve, wp_read, c + 1)
                moments(own, rows(s.x1, c), bn_c, mv_c, ve_c, var_c)

            def second_norm(own, c):
                dve.wait_ge(rstd_c_done, 3 * c + 2)
                own.step(center(rows(s.hid, c), rows(s.x1, c), mv_c, rstd_c))
                hold(dve, held_dve, own_c, own.base + own.n)
                moments(own, rows(s.hid, c), bn_c, mv_c, ve_c, var_c)

            def center_second(c):
                dve.wait_ge(rstd_c_done, 3 * c + 3)
                center(part(z), rows(s.hid, c), mv_c, rstd_c).then_inc(y_done, 1)

            def iteration(b, a, c, par):
                odd = 1 - par
                own = Own(dve, own_c, C_STEPS * c) if c is not None else None
                for p in range(PAIRS):
                    units = []
                    if b is not None and p in OWN_UNITS:
                        units = [(b, u) for u in OWN_UNITS[p]]
                    if a is not None and p in NEXT_UNITS:
                        units = [(a, u) for u in NEXT_UNITS[p]]

                    def unit():
                        if units:
                            max_unit(*units.pop(0))

                    if a is not None:
                        if p == 0:
                            center_x(a)
                            if b is None:
                                dve.wait_ge(s.x_in[1], 16)
                                norm_x(Own(dve, own_a, 2 * HALVES), HALVES, NT)
                        if p == 2:
                            split_k(a, 0)
                        if p == 6:
                            if b is None:
                                dve.wait_ge(s.tgate_done, 1)
                            gate_v0(a, odd)
                        if p == 1:
                            split_q(a)
                    if p == 0 and c is not None:
                        lo(c, PAIRS - 1)
                    elif p > 0 and b is not None:
                        lo(b, p - 1)
                    unit()
                    if p == 2 and c is not None:
                        center_attended(c)
                    if a is not None:
                        if p == 2:
                            split_k(a, 1)
                        if p == 4:
                            split_v(a, odd)
                        if p == 5:
                            split_ctx_v(a, odd)
                    unit()
                    if c is not None:
                        if p == 0:
                            attended(own, c, odd)
                        if p == 3:
                            residual(own, c)
                        if p == 4:
                            second_norm(own, c)
                        if p == 5:
                            center_second(c)
                    unit()
                    if a is None:
                        if b is not None and p > 0:
                            s.dve_sums(dve, p - 1)
                        if b is None:
                            for n in {0: (7,), 2: (8, 9), 4: (10,), 6: (11, 12, 13)}.get(p, ()):
                                s.dve_sums(dve, n)
                        if b is not None and p == 0:
                            dve.wait_ge(s.zeroed, 16 * s.N_ZERO)
                        for n in rounds_beside(b, p):
                            s.dve_products(dve, n)
                    assert not units
                if own is not None:
                    assert own.n == C_STEPS, own.n

            own = Own(dve, own_a, 0)
            dve.wait_ge(s.x_in[0], 16)
            norm_x(own, 0, HALVES)
            dve.wait_ge(rstd_a_done, 1)
            iteration(None, 0, None, 1)
            dve.wait_ge(rstd_a_done, 2)
            iteration(0, 1, None, 0)
            with dve.Fori(0, (B - 2) // 2) as i:
                for odd in (0, 1):
                    n = 2 * i + 1 + odd
                    iteration(n, n + 1, n - 1, 1 - odd)
            iteration(B - 1, None, B - 2, 1)
            iteration(None, None, B - 1, 0)


def attention_rounds(sb, sem, s):
    RING = 4
    prod = [s.scratch[:, i * B:(i + 1) * B, :] for i in range(RING)]
    s.sc = sc = [sb(f"sc{i}", [P, B, B, H]) for i in range(HALVES)]
    s.masked, s.prod_read, s.weighted = masked, prod_read, weighted = sem("masked"), sem("prod_read"), sem("weighted")
    prod_pool, prod_dve = sem("prod_pool"), sem("prod_dve")
    POOL_KV = 3
    s.SCORE_ROUNDS, s.ROUNDS = HALVES * B, 2 * HALVES * B

    def place(n):
        if n < s.SCORE_ROUNDS:
            return False, n % HALVES, n // HALVES
        return True, n // B % HALVES, n % B

    def product(eng, n, g):
        values, half, q = place(n)
        m = q + 1
        over = slice(g * REP * HD, (g + 1) * REP * HD)
        at = (H + (KV_H if values else 0)) * HD + g * HD
        if values:
            left = s.sc[half][:, q, 0:m, g * REP:(g + 1) * REP].unsqueeze(3)
        else:
            left = s.qkv[:, HALVES * q + half, over].rearrange("p (r d) -> p r d", d=HD).unsqueeze(1)
        right = s.qkv[:, half::HALVES, at:at + HD][:, 0:m, :].unsqueeze(2)
        return eng.tensor_tensor(
            prod[n % RING][:, 0:m, over].rearrange("p k (r d) -> p k r d", d=HD),
            left.to_broadcast([P, m, REP, HD]), right.to_broadcast([P, m, REP, HD]), ALU.mult)

    def sources(eng, n):
        values, half, q = place(n)
        if not values:
            eng.wait_ge(s.qkv_done, 1 + HALVES * (q + 1))
        elif q == 0:
            eng.wait_ge(weighted, half + 1)

    def pool_products(pool, n):
        if n >= RING:
            pool.wait_ge(prod_read, n - RING + 1)
        sources(pool, n)
        for g in range(KV_H - POOL_KV, KV_H):
            i = product(pool, n, g)
        i.then_inc(prod_pool, 1)

    def dve_products(dve, n):
        sources(dve, n)
        for g in range(KV_H - POOL_KV):
            i = product(dve, n, g)
        i.then_inc(prod_dve, 1)

    def dve_sums(dve, n):
        values, half, q = place(n)
        dve.wait_ge(prod_dve, n + 1)
        dve.wait_ge(prod_pool, n + 1)
        m = q + 1
        if values:
            i = dve.tensor_reduce(s.ao[half][:, q, :], prod[n % RING][:, 0:m, :].rearrange("p k x -> p x k"),
                                  AX.X, ALU.add)
        else:
            i = dve.tensor_reduce(sc[half][:, q, 0:m, :],
                                  prod[n % RING][:, 0:m, :].rearrange("p k (h d) -> p k h d", d=HD),
                                  AX.X, ALU.add)
        i.then_inc(prod_read, 1)

    s.pool_products, s.dve_products, s.dve_sums = pool_products, dve_products, dve_sums


def second_attention(nc, sb, sem, s):
    ps = s.ps
    sc, masked, prod_read, weighted = s.sc, s.masked, s.prod_read, s.weighted
    s.ao = ao = [sb(f"ao{i}", [P, B, DIM]) for i in range(HALVES)]
    red = [sb(f"red{i}", [P, B, H]) for i in range(HALVES)]
    inv = [sb(f"inv{i}", [P, B, H]) for i in range(HALVES)]
    aot = [sb(f"aot{i}", [P, 2, P]) for i in range(2)]
    ln2t = [sb(f"ln2t{i}", [P, 2, P]) for i in range(2)]
    bn = [sb(f"bn_d{i}", [P, B, 6]) for i in range(HALVES)]
    mv = [sb(f"mv_d{i}", [P, B, 2]) for i in range(HALVES)]
    ve = [sb(f"ve_d{i}", [P, B]) for i in range(HALVES)]
    rstd = [sb(f"rstd_d{i}", [P, B]) for i in range(HALVES)]
    scaled = [sb(f"scaled{i}", [P, DIM]) for i in range(3)]

    shifted, exp_done = sem("shifted"), sem("exp_done")
    ao_ps, aot_done, proj_ps, hid_done = sem("ao_ps"), sem("aot_done"), sem("proj_ps"), sem("hid_done")
    var_d, rstd_done, ln2_done = sem("var_d"), sem("rstd_d_done"), sem("ln2_done")
    ln2_ps, ln2t_done, logits_ps = sem("ln2_ps"), sem("ln2t_done"), sem("logits_ps")
    own_d, scaled_done = sem("own_d"), sem("scaled_done")
    TILES = [("project", n) for n in range(2 * B)] + [("logits", n) for n in range(2 * B)]

    with nc.Block() as block:

        @block.gpsimd
        def _(pool):
            for n in range(s.SCORE_ROUNDS - HALVES, s.ROUNDS):
                s.pool_products(pool, n)
            for half in range(HALVES):
                pool.wait_ge(var_d, half + 1)
                pool.tensor_tensor(rstd[half][:], ve[half][:], s.minus_half[:, 0:B],
                                   ALU.pow).then_inc(rstd_done, 1)

        @block.vector
        def _(dve):
            own = Own(dve, own_d, 0)

            def by_key(half):
                return sc[half][:].rearrange("p q k h -> p q h k")

            def shift(half):
                dve.wait_ge(masked, half + 1)
                dve.wait_ge(prod_read, s.SCORE_ROUNDS - 1 + half)
                own.step(dve.tensor_reduce(red[half][:], by_key(half), AX.X, ALU.max))
                own.settle()
                dve.tensor_tensor(sc[half][:], sc[half][:], red[half][:].unsqueeze(2).to_broadcast(
                    [P, B, B, H]), ALU.subtract).then_inc(shifted, 1)

            def weigh(half):
                dve.wait_ge(exp_done, half + 1)
                own.step(dve.tensor_reduce(red[half][:], by_key(half), AX.X, ALU.add))
                own.settle()
                own.step(dve.reciprocal(inv[half][:], red[half][:]))
                own.settle()
                dve.tensor_tensor(sc[half][:], sc[half][:], inv[half][:].unsqueeze(2).to_broadcast(
                    [P, B, B, H]), ALU.mult).then_inc(weighted, 1)

            def hidden(n):
                half, k = n // B, n % B
                t = HALVES * k + half
                dve.wait_ge(proj_ps, n + 1)
                dve.tensor_tensor(s.hid[:, t, :], ps[:, 2 + n % 2, 0:DIM], s.hid[:, t, :],
                                  ALU.add).then_inc(hid_done, 1)

            def stats(n):
                half, k = n // B, n % B
                dve.wait_ge(hid_done, n + 1)
                own.step(dve.bn_stats(bn[half][:, k, :], s.hid[:, HALVES * k + half, :]))

            def variance(half):
                own.settle()
                for k in range(B):
                    own.step(dve.bn_aggr(mv[half][:, k, :], bn[half][:, k, :]))
                own.settle()
                dve.tensor_scalar(ve[half][:], mv[half][:, :, 1], EPS, None, ALU.add).then_inc(var_d, 1)

            def scale(n):
                half, k = n // B, n % B
                if n >= 3:
                    dve.wait_ge(ln2_done, n - 2)
                dve.scalar_tensor_tensor(scaled[n % 3][:], s.hid[:, HALVES * k + half, :], mv[half][:, k, 0:1],
                                         s.w2n_sb[:], ALU.subtract, ALU.mult).then_inc(scaled_done, 1)

            def norm(n):
                half, k = n // B, n % B
                if k == 0:
                    dve.wait_ge(rstd_done, half + 1)
                dve.wait_ge(scaled_done, n + 1)
                dve.scalar_tensor_tensor(s.ln2[:, HALVES * k + half, :], scaled[n % 3][:],
                                         rstd[half][:, k:k + 1], s.b2n_sb[:], ALU.mult,
                                         ALU.add).then_inc(ln2_done, 1)

            for n in range(s.SCORE_ROUNDS - HALVES, s.SCORE_ROUNDS):
                s.dve_products(dve, n)
            s.dve_sums(dve, s.SCORE_ROUNDS - 2)
            shift(0)
            s.dve_sums(dve, s.SCORE_ROUNDS - 1)
            weigh(0)
            s.dve_products(dve, s.SCORE_ROUNDS)
            shift(1)
            for n in range(s.SCORE_ROUNDS, s.ROUNDS):
                if n + 1 < s.ROUNDS:
                    s.dve_products(dve, n + 1)
                s.dve_sums(dve, n)
                if n == s.SCORE_ROUNDS + 2:
                    weigh(1)
                if n >= 3 * B:
                    hidden(n - 3 * B)
                    if n > 3 * B:
                        stats(n - 3 * B - 1)
            stats(B - 1)
            variance(0)
            scale(0)
            for k in range(B):
                if k + 1 < B:
                    scale(k + 1)
                norm(k)
                hidden(B + k)
                if k >= 1:
                    stats(B + k - 1)
            stats(2 * B - 1)
            variance(1)
            scale(B)
            for k in range(B):
                if k + 1 < B:
                    scale(B + k + 1)
                norm(B + k)

        @block.scalar
        def _(act):
            def exponentials(half):
                act.wait_ge(shifted, half + 1)
                act.activation(sc[half][:], sc[half][:], ACT.Exp, scale=SCALE).then_inc(exp_done, 1)

            def evacuate(what, n):
                src, dst, ready, done = {"project": (0, aot, ao_ps, aot_done),
                                         "logits": (6, ln2t, ln2_ps, ln2t_done)}[what]
                act.wait_ge(ready, n + 1)
                act.activation(dst[n % 2][:], ps[:, src + n % 2, 0:2 * P].rearrange("p (f t) -> p f t", f=2),
                               ACT.Copy).then_inc(done, 1)

            exponentials(0)
            exponentials(1)
            for what, n in TILES:
                evacuate(what, n)

        @block.tensor
        def _(pe):
            def transpose_tile(src, bank):
                for f in range(2):
                    i = pe.transpose(ps[:, bank, f * P:(f + 1) * P], src[:, f * P:(f + 1) * P], s.id32[:])
                return i

            def transposed(what, n):
                half, k = n // B, n % B
                if what == "project":
                    pe.wait_ge(prod_read, (HALVES + half) * B + k + 1)
                    if n >= 2:
                        pe.wait_ge(aot_done, n - 1)
                    transpose_tile(ao[half][:, k, :], n % 2).then_inc(ao_ps, 1)
                else:
                    pe.wait_ge(ln2_done, n + 1)
                    if n >= 2:
                        pe.wait_ge(ln2t_done, n - 1)
                    transpose_tile(s.ln2[:, HALVES * k + half, :], 6 + n % 2).then_inc(ln2_ps, 1)

            def multiplied(what, n):
                if what == "project":
                    pe.wait_ge(aot_done, n + 1)
                    if n >= 2:
                        pe.wait_ge(hid_done, n - 1)
                    for f in range(2):
                        i = pe.matmul(ps[:, 2 + n % 2, 0:DIM], aot[n % 2][:, f, :], s.wproj_sb[:, f, :],
                                      start=f == 0, stop=f == 1)
                    i.then_inc(proj_ps, 1)
                else:
                    t = HALVES * (n % B) + n // B
                    pe.wait_ge(ln2t_done, n + 1)
                    for f in range(2):
                        i = pe.matmul(ps[:, 4, t * E:(t + 1) * E], ln2t[n % 2][:, f, :], s.wr_sb[:, f, :],
                                      start=f == 0, stop=f == 1)
                    i.then_inc(logits_ps, 1)

            for i, tile in enumerate(TILES):
                transposed(*tile)
                if i > 0:
                    multiplied(*TILES[i - 1])
            multiplied(*TILES[-1])


def route(nc, sb, sem, s):
    ps = s.ps
    mx, tot, inv = (sb(n, [P, NT]) for n in ("mx_e", "tot_e", "inv_e"))
    probs = sb("probs", [P, NT, E])
    best = sb("best", [P, NT, 8])
    which = sb("which", [P, NT, 8], U32)
    whichf = sb("whichf", [P, NT, TOP])
    hot = [sb(f"hot{k}", [P, NT, E]) for k in range(TOP)]
    both = sb("both", [P, NT, E])
    earlier = [sb(f"earlier{i}", [P, NT, E]) for i in range(2)]
    place = sb("place", [P, NT, E])
    tmp = [sb(f"tmp_e{k}", [P, NT, E]) for k in range(2)]
    at, base, keep, row = ([sb(f"{n}{k}", [P, NT]) for k in range(TOP)] for n in ("at", "base", "keep", "row"))
    shifted, exp_done, both_done, counted = sem("shifted_e"), sem("exp_done_e"), sem("both_done"), sem("counted")
    own_e, ln2_hi = sem("own_e"), sem("ln2_hi")
    s.rows_ready, s.ln2_lo = sem("rows_ready"), sem("ln2_lo")

    def over_experts(ap):
        return ap[:].unsqueeze(2).to_broadcast([P, NT, E])

    def over_tiles(ap):
        return ap[:].unsqueeze(1).to_broadcast([P, NT, E])


    def route_act(act):
        act.wait_ge(shifted, 1)
        act.activation(probs[:], probs[:], ACT.Exp).then_inc(exp_done, 1)
        for half in range(2):
            tiles = slice(half * NT // 2, (half + 1) * NT // 2)
            act.activation(s.ln2_parts[:, tiles, 0, :], s.ln2[:, tiles, :], ACT.Copy).then_inc(ln2_hi, 1)

    def route_pool(pool):
        for half in range(2):
            tiles = slice(half * NT // 2, (half + 1) * NT // 2)
            pool.wait_ge(ln2_hi, half + 1)
            pool.tensor_tensor(s.ln2_parts[:, tiles, 1, :], s.ln2[:, tiles, :], s.ln2_parts[:, tiles, 0, :],
                               ALU.subtract).then_inc(s.ln2_lo, 1)

    def route_pe(pe):
        pe.wait_ge(both_done, 1)
        pe.matmul(ps[:, 5, 0:NT * E], s.before_sb[:, 0, :], both[:].rearrange("p t e -> p (t e)"),
                  start=True, stop=True).then_inc(counted, 1)
        pe.matmul(ps[:, 6, 0:NT * E], s.before_sb[:, 1, :], both[:].rearrange("p t e -> p (t e)"),
                  start=True, stop=True).then_inc(counted, 1)

    def route_dve(dve):
        own = Own(dve, own_e, 0)

        def do(*instructions):
            for i in instructions:
                own.step(i)
            own.settle()

        def tiles(bank):
            return ps[:, bank, 0:NT * E].rearrange("p (t e) -> p t e", e=E)

        do(dve.tensor_reduce(mx[:], tiles(4), AX.X, ALU.max))
        dve.tensor_tensor(probs[:], tiles(4), over_experts(mx), ALU.subtract).then_inc(shifted, 1)
        dve.wait_ge(exp_done, 1)
        do(dve.tensor_reduce(tot[:], probs[:], AX.X, ALU.add))
        do(dve.reciprocal(inv[:], tot[:]))
        do(dve.tensor_tensor(probs[:], probs[:], over_experts(inv), ALU.mult))
        do(*(dve.max(best[:, t, :], probs[:, t, :]) for t in range(NT)))
        do(*(dve.max_index(which[:, t, :], best[:, t, :], probs[:, t, :]) for t in range(NT)))
        do(dve.tensor_copy(whichf[:], which[:, :, 0:TOP]))
        do(*(dve.tensor_tensor(hot[k][:], over_tiles(s.experts_sb), over_experts(whichf[:, :, k]),
                               ALU.is_equal) for k in range(TOP)))
        dve.tensor_tensor(both[:], hot[0][:], hot[1][:], ALU.add).then_inc(both_done, 1)
        do(dve.memset(earlier[0][:, 0, :], 0.0))
        dve.wait_ge(counted, 2)
        do(dve.tensor_copy(earlier[0][:, 1:NT, :], tiles(6)[:, 0:NT - 1, :]))
        step, n = 1, 0
        while step < NT:
            src, dst = earlier[n % 2], earlier[(n + 1) % 2]
            do(dve.tensor_copy(dst[:, 0:step, :], src[:, 0:step, :]),
               dve.tensor_tensor(dst[:, step:NT, :], src[:, step:NT, :], src[:, 0:NT - step, :], ALU.add))
            step, n = 2 * step, n + 1
        do(dve.tensor_tensor(place[:], tiles(5), earlier[n % 2][:], ALU.add))
        for k in range(TOP):
            do(dve.tensor_tensor(tmp[0][:], hot[k][:], place[:], ALU.mult),
               dve.tensor_tensor(tmp[1][:], hot[k][:], over_tiles(s.base_sb), ALU.mult))
            do(dve.tensor_reduce(at[k][:], tmp[0][:], AX.X, ALU.add),
               dve.tensor_reduce(base[k][:], tmp[1][:], AX.X, ALU.add))
            do(dve.tensor_scalar(keep[k][:], at[k][:], float(CAP), None, ALU.is_lt))
            do(dve.tensor_tensor(s.gates[k][:], best[:, :, k], keep[k][:], ALU.mult),
               dve.tensor_tensor(row[k][:], base[k][:], at[k][:], ALU.add),
               dve.tensor_scalar(at[k][:], at[k][:], float(CAP - 1), None, ALU.min))
            do(dve.tensor_tensor(row[k][:], row[k][:], s.trash_sb[:, k, :], ALU.subtract),
               dve.tensor_tensor(at[k][:], at[k][:], base[k][:], ALU.add))
            do(dve.tensor_tensor(row[k][:], row[k][:], keep[k][:], ALU.mult),
               dve.tensor_copy(s.read_rows[k][:], at[k][:]))
            do(dve.tensor_tensor(row[k][:], row[k][:], s.trash_sb[:, k, :], ALU.add))
            dve.tensor_copy(s.write_rows[k][:], row[k][:]).then_inc(s.rows_ready, 1)

    return route_pe, route_act, route_dve, route_pool


def run_experts(nc, sb, sem, s, route_pe, route_act, route_dve, route_pool):
    ps = s.ps
    F = FFN // P
    FULL = CAP // P * P
    M = len(EXPERT_TILES)
    GOT = 6
    WSCALE = 64.0
    w1r = [sb(f"w1r{i}", [P, 2, FFN]) for i in range(2)]
    w2r = [sb(f"w2r{i}", [P, F, DIM]) for i in range(2)]
    w1p = [[sb(f"w1_{n}{i}", [P, 2, FFN], F16) for n in ("hi", "lo")] for i in range(2)]
    w2p = [[sb(f"w2_{n}{i}", [P, F, DIM], F16) for n in ("hi", "lo")] for i in range(2)]
    xr = [sb(f"xr{i}", [P, M, 2, DIM], F16) for i in range(2)]
    xt = [[sb(f"xt_{n}{i}", [P, 2, CAP], F16) for n in ("hi", "lo")] for i in range(2)]
    act_f = [sb(f"act_f{i}", [P, F, CAP]) for i in range(2)]
    act_p = [[sb(f"act_{n}{i}", [P, F, CAP], F16) for n in ("hi", "lo")] for i in range(2)]
    y = [sb(f"y{i}", [P, M, DIM]) for i in range(2)]
    got = [[sb(f"got{k}{i}", [P, DIM]) for i in range(GOT)] for k in range(TOP)]
    PRODUCTS = ((0, 0), (0, 1), (1, 0))

    weights_in = [sem("weights_in0"), sem("weights_in1")]
    rows_in = [sem("rows_in0"), sem("rows_in1")]
    y_out = [sem("y_out0"), sem("y_out1")]
    zeroed, scattered = s.zeroed, sem("scattered")
    w_hi, w_lo = sem("w_hi"), sem("w_lo")
    xt_ps, xt_hi, xt_lo = sem("xt_ps_f"), sem("xt_hi_f"), sem("xt_lo_f")
    up_ps, act_hi, act_lo = sem("up_ps"), sem("act_hi"), sem("act_lo")
    down_ps, y_done = sem("down_ps"), sem("y_done_f")
    gathered = [sem(f"gathered{i}") for i in range(GOT)]
    summed, ys_done, weighed, out_done = sem("summed"), sem("ys_done"), sem("weighed"), sem("out_done")
    own_f = sem("own_f")

    def arrived(e, par):
        return 32 * (e // 2 + 1) if isinstance(e, int) else 16 * (e - par) + 32

    with nc.Block() as block:

        @block.sync
        def _(sp):
            def load_weights(e, par):
                sp.dma_start(w1r[par][:], s.w1[e].rearrange("(f p) n -> p f n", p=P)).then_inc(weights_in[par], 16)
                sp.dma_start(w2r[par][:], s.w2[e].rearrange("(f p) n -> p f n", p=P)).then_inc(weights_in[par], 16)

            def load_rows(e, par):
                full = s.slots_dram[0:E * CAP].rearrange("(e r) d -> e r d", e=E)[e]
                whole = xr[par][:].rearrange("p t i d -> p t (i d)")
                sp.dma_start(whole[:, 0:M - 1, :], full[0:FULL].rearrange("(t p) d -> p t d", p=P)).then_inc(rows_in[par], 16)
                sp.dma_start(whole[0:CAP - FULL, M - 1, :], full[FULL:CAP]).then_inc(rows_in[par], 16)

            def store(e, par):
                sp.wait_ge(y_done, M * e + M)
                full = s.ffn_dram.rearrange("(e r) d -> e r d", e=E)[e]
                sp.dma_start(full[0:FULL].rearrange("(t p) d -> p t d", p=P), y[par][:, 0:M - 1, :]).then_inc(y_out[par], 16)
                sp.dma_start(full[FULL:CAP], y[par][0:CAP - FULL, M - 1, :]).then_inc(y_out[par], 16)

            for n in range(2):
                load_weights(n, n)
            sp.wait_ge(scattered, 16 * TOP * NT)
            sp.wait_ge(zeroed, 16 * s.N_ZERO)
            for n in range(2):
                load_rows(n, n)
            with sp.Fori(0, (E - 2) // 2) as i:
                for par in (0, 1):
                    e = 2 * i + par
                    sp.wait_ge(w_lo, 2 * e + 2)
                    load_weights(e + 2, par)
                    sp.wait_ge(xt_ps, e + 1)
                    load_rows(e + 2, par)
                    store(e, par)
            for e in (E - 2, E - 1):
                store(e, e % 2)
            for par in (0, 1):
                sp.wait_ge(y_out[par], 32 * E // 2)
            sp.sem_inc(ys_done, 1)
            for t in range(NT):
                sp.wait_ge(weighed, t + 1)
                sp.dma_start(s.out_rows[t], s.x1[:, t, :]).then_inc(out_done, 16)
            sp.wait_ge(out_done, 16 * NT)

        @block.gpsimd
        def _(pool):
            route_pool(pool)
            pool.wait_ge(s.ln2_lo, 2)
            pool.wait_ge(zeroed, 16 * s.N_ZERO)
            for k in range(TOP):
                pool.wait_ge(s.rows_ready, k + 1)
                for t in range(NT):
                    pool.indirect_dma_start(
                        s.slots_dram, bass.IndirectOffsetOnAxis(ap=s.write_rows[k][:, t:t + 1], axis=0),
                        s.ln2_parts[:, t, :, :].rearrange("p i d -> p (i d)"), None).then_inc(scattered, 16)
            for t in range(NT):
                pool.tensor_tensor(s.x1[:, t, :], s.x1[:, t, :], s.hid[:, t, :], ALU.add).then_inc(summed, 1)
            pool.wait_ge(ys_done, 1)
            for t in range(NT):
                if t >= GOT:
                    pool.wait_ge(weighed, t - GOT + 1)
                for k in range(TOP):
                    pool.indirect_dma_start(
                        got[k][t % GOT][:], None, s.ffn_dram,
                        bass.IndirectOffsetOnAxis(ap=s.read_rows[k][:, t:t + 1], axis=0)
                    ).then_inc(gathered[t % GOT], 16)

        @block.tensor
        def _(pe):
            route_pe(pe)

            def transposes(e, par):
                pe.wait_ge(rows_in[par], arrived(e, par))
                wait(pe, xt_hi, e)
                wait(pe, xt_lo, e)
                for part in range(2):
                    out = ps[:, part, 0:CAP].bitcast(F16).rearrange("p (f n) -> p f n", f=2)
                    for f in range(2):
                        for n, (at, m) in enumerate(EXPERT_TILES):
                            i = pe.transpose(out[:, f, at:at + m], xr[par][0:m, n, part, f * P:(f + 1) * P],
                                             s.id16[0:m, 0:m])
                i.then_inc(xt_ps, 1)

            def up(e, par):
                pe.wait_ge(w_lo, 2 * e + 1)
                pe.wait_ge(xt_lo, e + 1)
                pe.wait_ge(xt_hi, e + 1)
                for j in range(F):
                    if not (isinstance(e, int) and e == 0 and j < 2):
                        pe.wait_ge(act_hi, F * e + j - 1)
                    for f in range(2):
                        for n, (a, b) in enumerate(PRODUCTS):
                            i = pe.matmul(ps[:, 2 + j % 2, 0:CAP], w1p[par][a][:, f, j * P:(j + 1) * P],
                                          xt[par][b][:, f, :], start=f == 0 and n == 0, stop=f == 1 and n == 2)
                    i.then_inc(up_ps, 1)

            def down(e, par):
                pe.wait_ge(w_lo, 2 * e + 2)
                for t, (at, m) in enumerate(EXPERT_TILES):
                    wait(pe, y_done, M * (e - 1) + t + 1)
                    for n, (a, b) in enumerate(PRODUCTS):
                        for j in range(F):
                            if t == 0 and n == 0:
                                pe.wait_ge(act_hi, F * e + j + 1)
                            if t == 0 and a == 1:
                                pe.wait_ge(act_lo, F * e + j + 1)
                            i = pe.matmul(ps[0:m, 4 + t, 0:DIM], act_p[par][a][:, j, at:at + m],
                                          w2p[par][b][:, j, :], start=j == 0 and n == 0, stop=j == F - 1 and n == 2)
                    i.then_inc(down_ps, 1)

            transposes(0, 0)

            def expert(e, par, last=False):
                up(e, par)
                if not last:
                    transposes(e + 1, 1 - par)
                down(e, par)

            expert(0, 0)
            expert(1, 1)
            with pe.Fori(1, E // 2 - 1) as i:
                for par in (0, 1):
                    expert(2 * i + par, par)
            expert(E - 2, 0)
            expert(E - 1, 1, last=True)

        @block.scalar
        def _(act):
            route_act(act)

            def split_weights(e, par):
                act.wait_ge(weights_in[par], arrived(e, par))
                act.activation(w1p[par][0][:], w1r[par][:], ACT.Copy, scale=WSCALE).then_inc(w_hi, 1)
                act.activation(w2p[par][0][:], w2r[par][:], ACT.Copy, scale=WSCALE).then_inc(w_hi, 1)

            def copy_xt(e, par):
                act.wait_ge(xt_ps, e + 1)
                act.activation(xt[par][0][:].rearrange("p f n -> p (f n)"), ps[:, 0, 0:CAP].bitcast(F16),
                               ACT.Copy).then_inc(xt_hi, 1)

            def gelu(e, par):
                for j in range(F):
                    act.wait_ge(up_ps, F * e + j + 1)
                    act.activation(act_f[par][:, j, :], ps[:, 2 + j % 2, 0:CAP], ACT.Gelu_apprx_tanh,
                                   scale=1 / WSCALE)
                    act.activation(act_p[par][0][:, j, :], ps[:, 2 + j % 2, 0:CAP], ACT.Gelu_apprx_tanh,
                                   scale=1 / WSCALE).then_inc(act_hi, 1)

            def expert(e, par, last=False):
                gelu(e, par)
                if not last:
                    copy_xt(e + 1, 1 - par)
                    split_weights(e + 1, 1 - par)

            split_weights(0, 0)
            copy_xt(0, 0)
            with act.Fori(0, E // 2 - 1) as i:
                for par in (0, 1):
                    expert(2 * i + par, par)
            expert(E - 2, 0)
            expert(E - 1, 1, last=True)

        @block.vector
        def _(dve):
            route_dve(dve)

            def split_weights(e, par):
                dve.wait_ge(w_hi, 2 * e + 1)
                dve.scalar_tensor_tensor(w1p[par][1][:], w1r[par][:], WSCALE, w1p[par][0][:], ALU.mult,
                                         ALU.subtract).then_inc(w_lo, 1)
                dve.wait_ge(w_hi, 2 * e + 2)
                dve.scalar_tensor_tensor(w2p[par][1][:], w2r[par][:], WSCALE, w2p[par][0][:], ALU.mult,
                                         ALU.subtract).then_inc(w_lo, 1)

            def copy_xt(e, par):
                dve.wait_ge(xt_ps, e + 1)
                dve.tensor_copy(xt[par][1][:].rearrange("p f n -> p (f n)"),
                                ps[:, 1, 0:CAP].bitcast(F16)).then_inc(xt_lo, 1)

            def split_act(e, par):
                for j in range(F):
                    dve.wait_ge(act_hi, F * e + j + 1)
                    dve.tensor_tensor(act_p[par][1][:, j, :], act_f[par][:, j, :], act_p[par][0][:, j, :],
                                      ALU.subtract).then_inc(act_lo, 1)

            def copy_y(e, par):
                wait(dve, y_out[par], 32 * (e // 2) if isinstance(e, int) else 16 * (e - par))
                for t, (at, m) in enumerate(EXPERT_TILES):
                    dve.wait_ge(down_ps, M * e + t + 1)
                    dve.tensor_scalar(y[par][0:m, t, :], ps[0:m, 4 + t, 0:DIM], 1 / WSCALE, None,
                                      ALU.mult).then_inc(y_done, 1)

            def expert(e, par, last=False):
                split_act(e, par)
                if not last:
                    copy_xt(e + 1, 1 - par)
                    split_weights(e + 1, 1 - par)
                copy_y(e, par)

            split_weights(0, 0)
            copy_xt(0, 0)
            expert(0, 0)
            expert(1, 1)
            with dve.Fori(1, E // 2 - 1) as i:
                for par in (0, 1):
                    expert(2 * i + par, par)
            expert(E - 2, 0)
            expert(E - 1, 1, last=True)
            own = Own(dve, own_f, 0)
            dve.wait_ge(summed, NT)
            for t in range(NT):
                dve.wait_ge(gathered[t % GOT], 16 * TOP * (t // GOT + 1))
                own.step(dve.scalar_tensor_tensor(s.x1[:, t, :], got[0][t % GOT][:], s.gates[0][:, t:t + 1],
                                                  s.x1[:, t, :], ALU.mult, ALU.add))
                own.settle()
                dve.scalar_tensor_tensor(s.x1[:, t, :], got[1][t % GOT][:], s.gates[1][:, t:t + 1],
                                         s.x1[:, t, :], ALU.mult, ALU.add).then_inc(weighed, 1)


def bass_xattn_moe(nc, x, ctx_t, wq, wk, wv, gate, ln_g, ln_b, wp, bp, ln1_w, ln1_b, ln2_w, ln2_b,
                   wqkv, wproj, wrouter, w1, w2, ident, before, ctx0_row, experts, expert_base,
                   trash_rows, stack_rows, out):
    with ExitStack() as whole:
        s = Shared()

        def allocator(stack):
            def sb(name, shape, dt=F32):
                return stack.enter_context(nc.sbuf_tensor(name, shape, dt))
            return sb

        def sem(name):
            return whole.enter_context(nc.semaphore(name))

        sb = allocator(whole)
        s.ps = whole.enter_context(nc.psum_tensor("ps", [P, 8, 512], F32))
        s.slots_dram = nc.dram_tensor("expert_slots", (TRASH + TOP * NT * P, 2 * DIM), F16).ap()
        s.ffn_dram = nc.dram_tensor("expert_results", (E * CAP, DIM), F32).ap()
        s.w1, s.w2 = w1, w2
        s.out_rows = out.rearrange("b (h p) d -> (b h) p d", p=P)

        s.x1 = sb("x1", [P, NT, DIM])
        s.hid = sb("hid", [P, NT, DIM])
        s.id32, s.id16 = sb("id32", [P, P]), sb("id16", [P, P], F16)
        s.minus_half = sb("minus_half", [P, NT])
        s.wproj_sb = sb("wproj_sb", [P, 2, DIM])
        s.wr_sb = sb("wr_sb", [P, 2, E])
        s.w2n_sb, s.b2n_sb = sb("w2n_sb", [P, DIM]), sb("b2n_sb", [P, DIM])
        s.before_sb = sb("before_sb", [P, 2, P])
        s.experts_sb, s.base_sb = sb("experts_sb", [P, E]), sb("base_sb", [P, E])
        s.trash_sb = sb("trash_sb", [P, TOP, NT])
        s.gates = [sb(f"gates{k}", [P, NT]) for k in range(TOP)]
        s.read_rows = [sb(f"read_rows{k}", [P, NT], U32) for k in range(TOP)]
        s.write_rows = [sb(f"write_rows{k}", [P, NT], U32) for k in range(TOP)]

        s.const_in, s.late_in = sem("const_in"), sem("late_in")
        s.x_in = [sem(f"x_in{i}") for i in range(2)]
        s.first_in = sem("first_in")
        s.id16_done, s.tgate_done = sem("id16_done"), sem("tgate_done")
        x_tiles = x.rearrange("b (h p) d -> p (b h) d", p=P)

        s.qkv = sb("qkv", [P, NT, QKV])
        s.qkv_done = sem("qkv_done")
        s.scratch = sb("scratch", [P, 2 * NT, DIM])
        s.ln2 = s.scratch[:, 0:NT, :]
        s.ln2_parts = s.scratch[:, NT:2 * NT, :].bitcast(F16).rearrange("p t (i d) -> p t i d", i=2)
        middle = ExitStack()
        attention_rounds(allocator(middle), sem, s)
        with ExitStack() as first:
            sb = allocator(first)
            s.zeros = s.scratch[:, 0:4, :].rearrange("p n d -> p (n d)").bitcast(F16)
            s.wq_sb, s.wk_sb, s.wv_sb, s.wp_sb = (
                sb(n, [P, 2, DIM]) for n in ("wq_sb", "wk_sb", "wv_sb", "wp_sb"))
            s.wqkv_sb = sb("wqkv_sb", [P, 2, QKV])
            s.g_sb, s.b_sb, s.g1_sb, s.b1_sb = (sb(n, [P, 2]) for n in ("g_sb", "b_sb", "g1_sb", "b1_sb"))
            s.bp_sb = sb("bp_sb", [P, DIM])
            s.gate_sb, s.tgate = sb("gate_sb", [P, H]), sb("tgate", [P, H])
            s.ctx0_sb = sb("ctx0_sb", [CTX, P])
            s.ctx_sb = sb("ctx_sb", [P, B, 2, CTX])
            first_ones = [(s.id32, ident), (s.wq_sb, wq), (s.ctx_sb, ctx_t)]
            early = [(s.wk_sb, wk), (s.wv_sb, wv),
                     (s.bp_sb, bp.partition_broadcast(P)), (s.gate_sb, gate.partition_broadcast(P)),
                     (s.ctx0_sb, ctx0_row), (s.wp_sb, wp), (s.wqkv_sb, wqkv), (s.g_sb, ln_g),
                     (s.b_sb, ln_b), (s.g1_sb, ln1_w), (s.b1_sb, ln1_b)]
            late = [(s.wproj_sb, wproj), (s.wr_sb, wrouter), (s.w2n_sb, ln2_w.partition_broadcast(P)),
                    (s.b2n_sb, ln2_b.partition_broadcast(P)), (s.before_sb, before),
                    (s.experts_sb, experts.partition_broadcast(P)),
                    (s.base_sb, expert_base.partition_broadcast(P)), (s.trash_sb, trash_rows)]
            s.N_FIRST, s.N_CONST = 16 * len(first_ones), 16 * (len(early) + 4)
            s.late_count = 16 * len(late)
            s.zeroed = sem("zeroed")
            s.N_ZERO = E * CAP // (4 * P)

            def load_constants(sp):
                sp.dma_start(s.x1[:, 0:2, :], x_tiles[:, 0:2, :]).then_inc(s.x_in[0], 16)
                for dst, src in first_ones:
                    sp.dma_start(dst[:], src).then_inc(s.first_in, 16)
                sp.dma_start(s.x1[:, 2:NT, :], x_tiles[:, 2:NT, :]).then_inc(s.x_in[1], 16)
                for dst, src in early:
                    sp.dma_start(dst[:], src).then_inc(s.const_in, 16)
                for qs, ks in s.stacks:
                    sp.dma_start(qs[STACK:STACK + 1], stack_rows[0:1, :, 0:N]).then_inc(s.const_in, 16)
                    sp.dma_start(ks[STACK:ROWS], stack_rows[1:3]).then_inc(s.const_in, 16)
                for dst, src in late:
                    sp.dma_start(dst[:], src).then_inc(s.late_in, 16)

            def clear_slots(sp):
                view = s.slots_dram[0:E * CAP].rearrange("(n p r) d -> n p (r d)", p=P, r=4)
                for n in range(s.N_ZERO):
                    sp.dma_start(view[n], s.zeros).then_inc(s.zeroed, 16)
            s.load_constants, s.clear_slots = load_constants, clear_slots
            cross_attention(nc, sb, sem, s)
        with ExitStack() as second:
            second_attention(nc, allocator(second), sem, s)
        middle.close()
        with ExitStack() as last:
            run_experts(nc, allocator(last), sem, s, *route(nc, allocator(last), sem, s))


_INS = ("x", "ctx_t", "wq", "wk", "wv", "gate", "ln_g", "ln_b", "wp", "bp", "ln1_w", "ln1_b", "ln2_w", "ln2_b",
        "wqkv", "wproj", "wrouter", "w1", "w2", "ident", "before", "ctx0_row", "experts", "expert_base",
        "trash_rows", "stack_rows")


def kernel(**inputs):
    import concourse.bacc as bacc
    from concourse.bass_utils import run_bass_kernel_spmd

    a = {k: np.asarray(v) for k, v in inputs.items()}

    def chunks(w):
        return w.reshape(2, P, -1).transpose(1, 0, 2)

    def by_head_dim(w):
        return w.reshape(DIM, 2, GROUP, HD).transpose(0, 1, 3, 2).reshape(DIM, DIM)

    def column(v):
        return v.reshape(2, P).T

    ctx = np.concatenate([a["ctx_1024"][:, 1:], a["ctx_1024"][:, :1]], axis=1)
    ctx0_row = np.zeros((CTX, P), np.float32)
    ctx0_row[CTX - 1] = 1.0
    before = np.stack([np.triu(np.ones((P, P), np.float32), 1), np.ones((P, P), np.float32)], axis=1)
    trash = (TRASH + np.arange(TOP * NT * P, dtype=np.float32).reshape(TOP, NT, P)).transpose(2, 0, 1)
    arrays = {
        "x": a["x"],
        "ctx_t": ctx.reshape(B, CTX, 2, P).transpose(3, 0, 2, 1),
        "wq": chunks(by_head_dim(a["L0_xattn_Wq"].T)),
        "wk": chunks(by_head_dim(a["L0_xattn_Wk"].T)),
        "wv": chunks(a["L0_xattn_Wv"].T),
        "gate": a["L0_xattn_gate"].reshape(H),
        "ln_g": column(a["L0_xattn_ln_g"]),
        "ln_b": column(a["L0_xattn_ln_b"]),
        "wp": chunks(a["L0_xattn_Wp"].T),
        "bp": a["L0_xattn_bp"],
        "ln1_w": column(a["L0_ffn_ln1_weight"]),
        "ln1_b": column(a["L0_ffn_ln1_bias"]),
        "ln2_w": a["L0_ffn_ln2_weight"],
        "ln2_b": a["L0_ffn_ln2_bias"],
        "wqkv": chunks(a["L0_ffn_qkv_weight"].T),
        "wproj": chunks(a["L0_ffn_proj_weight"].T),
        "wrouter": chunks(a["L0_ffn_router_weight"].T),
        "w1": a["L0_ffn_moe_w1"].transpose(0, 2, 1),
        "w2": a["L0_ffn_moe_w2"].transpose(0, 2, 1),
        "ident": np.eye(P, dtype=np.float32),
        "before": before,
        "ctx0_row": ctx0_row,
        "experts": np.arange(E, dtype=np.float32),
        "expert_base": np.arange(E, dtype=np.float32) * CAP,
        "trash_rows": trash,
        "stack_rows": np.repeat(np.array([0, 1, 1], np.float16), H * KEYS).reshape(3, H, KEYS),
    }
    nc = bacc.Bacc("TRN2", target_bir_lowering=False, num_devices=1)
    feeds, args = {}, []
    for name in _INS:
        array = np.ascontiguousarray(arrays[name])
        feeds[f"in_{name}"] = array
        args.append(nc.dram_tensor(f"in_{name}", array.shape, mybir.dt.from_np(array.dtype),
                                   kind="ExternalInput").ap())
    args.append(nc.dram_tensor("out", (B, N, DIM), F32, kind="ExternalOutput").ap())
    bass_xattn_moe(nc, *args)
    r = run_bass_kernel_spmd(nc, [feeds], core_ids=[0])
    return r.results[0]["out"]
```
